# Optimizing a Trainium2 kernel written in Bass

```python
import numpy as np
import jax
import jax.numpy as jnp

def _softmax(x, axis=-1):
    return jax.nn.softmax(x, axis=axis)

def _gelu(x):
    return jax.nn.gelu(x, approximate=True)

def _silu(x):
    return jax.nn.silu(x)

def _sigmoid(x):
    return jax.nn.sigmoid(x)

def _layernorm(x, axis=-1, eps=1e-05):
    m = jnp.mean(x, axis=axis, keepdims=True)
    v = jnp.var(x, axis=axis, keepdims=True)
    return (x - m) / jnp.sqrt(v + eps)

def _scatter_add(tgt, idx, src, axis=0):
    return tgt.at[idx].add(src)

def _segment_sum(src, seg, n):
    return jax.ops.segment_sum(src, seg, n)
kernel_name = 'mk_hybrid_d1_jaxref_r8_291142'

def setup_inputs(seed: int=0):
    np.random.seed(seed)
    _w = jnp.asarray

    def _L0_attn_a_setup():
        import jax, jax.numpy as jnp
        import numpy as np
        N_EMBD = 128
        N_HEADS = 16
        HEAD_DIM = N_EMBD // N_HEADS
        NUM_BUCKETS = 32
        MAX_DISTANCE = 64

        def _relative_position_bucket(relative_position):
            rp = jnp.maximum(-relative_position, 0)
            max_exact = NUM_BUCKETS // 2
            is_small = rp < max_exact
            rp_f = jnp.maximum(rp, 1).astype(jnp.float32)
            large = max_exact + (jnp.log(rp_f / max_exact) / np.log(MAX_DISTANCE / max_exact) * (NUM_BUCKETS - max_exact)).astype(jnp.int32)
            large = jnp.minimum(large, NUM_BUCKETS - 1)
            return jnp.where(is_small, rp, large)
        key = jax.random.key(seed)
        ks = jax.random.split(key, 10)
        B, S = (2, 256)
        std = 1.0 / np.sqrt(N_EMBD)
        inp = {'hidden_states': jax.random.normal(ks[0], (B, S, N_EMBD), dtype=jnp.float32), 'Wq': jax.random.normal(ks[1], (N_EMBD, N_EMBD), dtype=jnp.float32) * std, 'bq': jnp.zeros((N_EMBD,), jnp.float32), 'Wk': jax.random.normal(ks[2], (N_EMBD, N_EMBD), dtype=jnp.float32) * std, 'bk': jnp.zeros((N_EMBD,), jnp.float32), 'Wv': jax.random.normal(ks[3], (N_EMBD, N_EMBD), dtype=jnp.float32) * std, 'bv': jnp.zeros((N_EMBD,), jnp.float32), 'Wo': jax.random.normal(ks[4], (N_EMBD, N_EMBD), dtype=jnp.float32) * std, 'bo': jnp.zeros((N_EMBD,), jnp.float32), 'rel_bias': jax.random.normal(ks[5], (NUM_BUCKETS, N_HEADS), dtype=jnp.float32) * 0.1}
        return inp
    _L0_attn_a_in = _L0_attn_a_setup()

    def _L0_attn_b_setup():
        import jax, jax.numpy as jnp
        import numpy as np
        B, S, E, H = (4, 256, 128, 16)
        HD = E // H
        key = jax.random.key(seed)
        ks = jax.random.split(key, 5)
        scale = 1.0 / np.sqrt(E)
        x = jax.random.normal(ks[0], (B, S, E), dtype=jnp.float32)
        Wqkv = jax.random.uniform(ks[1], (E, 3 * E), dtype=jnp.float32, minval=-scale, maxval=scale)
        bqkv = jax.random.uniform(ks[2], (3 * E,), dtype=jnp.float32, minval=-scale, maxval=scale)
        Wout = jax.random.uniform(ks[3], (E, E), dtype=jnp.float32, minval=-scale, maxval=scale)
        bout = jax.random.uniform(ks[4], (E,), dtype=jnp.float32, minval=-scale, maxval=scale)
        return {'x': x, 'Wqkv': Wqkv, 'bqkv': bqkv, 'Wout': Wout, 'bout': bout}
    _L0_attn_b_in = _L0_attn_b_setup()

    def _L0_ffn_setup():
        import jax, jax.numpy as jnp
        import numpy as np
        TEMPERATURE = 1.0
        TOPK = 2
        key = jax.random.key(seed)
        ks = jax.random.split(key, 6)
        S, B, H, F, E = (256, 4, 128, 512, 8)
        x = jax.random.normal(ks[0], (S, B, H), dtype=jnp.float32)
        gate_w = jax.random.normal(ks[1], (E, H), dtype=jnp.float32) * (1.0 / np.sqrt(H))
        w1 = jax.random.normal(ks[2], (E, H, F), dtype=jnp.float32) * (1.0 / np.sqrt(H))
        b1 = jnp.zeros((E, F), dtype=jnp.float32)
        w2 = jax.random.normal(ks[3], (E, F, H), dtype=jnp.float32) * (1.0 / np.sqrt(F))
        b2 = jnp.zeros((E, H), dtype=jnp.float32)
        return {'x': x, 'gate_w': gate_w, 'w1': w1, 'b1': b1, 'w2': w2, 'b2': b2}
    _L0_ffn_in = _L0_ffn_setup()
    _d = {'L0_attn_a_hidden_states': _L0_attn_a_in['hidden_states'], 'L0_attn_a_Wq': _L0_attn_a_in['Wq'], 'L0_attn_a_bq': _L0_attn_a_in['bq'], 'L0_attn_a_Wk': _L0_attn_a_in['Wk'], 'L0_attn_a_bk': _L0_attn_a_in['bk'], 'L0_attn_a_Wv': _L0_attn_a_in['Wv'], 'L0_attn_a_bv': _L0_attn_a_in['bv'], 'L0_attn_a_Wo': _L0_attn_a_in['Wo'], 'L0_attn_a_bo': _L0_attn_a_in['bo'], 'L0_attn_a_rel_bias': _L0_attn_a_in['rel_bias'], 'L0_attn_b_Wqkv': _L0_attn_b_in['Wqkv'], 'L0_attn_b_bqkv': _L0_attn_b_in['bqkv'], 'L0_attn_b_Wout': _L0_attn_b_in['Wout'], 'L0_attn_b_bout': _L0_attn_b_in['bout'], 'L0_ffn_gate_w': _L0_ffn_in['gate_w'], 'L0_ffn_w1': _L0_ffn_in['w1'], 'L0_ffn_b1': _L0_ffn_in['b1'], 'L0_ffn_w2': _L0_ffn_in['w2'], 'L0_ffn_b2': _L0_ffn_in['b2']}
    _x0 = _d['L0_attn_a_hidden_states']
    _d['L0_attn_a_hidden_states'] = jax.random.normal(jax.random.fold_in(jax.random.key(seed), 1), (16, 512, 128), dtype=_x0.dtype)
    del _x0
    return _d

def reference(L0_attn_a_hidden_states, L0_attn_a_Wq, L0_attn_a_bq, L0_attn_a_Wk, L0_attn_a_bk, L0_attn_a_Wv, L0_attn_a_bv, L0_attn_a_Wo, L0_attn_a_bo, L0_attn_a_rel_bias, L0_attn_b_Wqkv, L0_attn_b_bqkv, L0_attn_b_Wout, L0_attn_b_bout, L0_ffn_gate_w, L0_ffn_w1, L0_ffn_b1, L0_ffn_w2, L0_ffn_b2):

    def _L0_attn_a_ref(hidden_states, Wq, bq, Wk, bk, Wv, bv, Wo, bo, rel_bias):
        import jax, jax.numpy as jnp
        import numpy as np
        N_EMBD = 128
        N_HEADS = 16
        HEAD_DIM = N_EMBD // N_HEADS
        NUM_BUCKETS = 32
        MAX_DISTANCE = 64

        def _relative_position_bucket(relative_position):
            rp = jnp.maximum(-relative_position, 0)
            max_exact = NUM_BUCKETS // 2
            is_small = rp < max_exact
            rp_f = jnp.maximum(rp, 1).astype(jnp.float32)
            large = max_exact + (jnp.log(rp_f / max_exact) / np.log(MAX_DISTANCE / max_exact) * (NUM_BUCKETS - max_exact)).astype(jnp.int32)
            large = jnp.minimum(large, NUM_BUCKETS - 1)
            return jnp.where(is_small, rp, large)
        B, S, _ = hidden_states.shape

        def shape(x):
            return x.reshape(B, S, N_HEADS, HEAD_DIM).transpose(0, 2, 1, 3)
        scale = 1.0 / np.sqrt(HEAD_DIM)
        q = shape(hidden_states @ Wq + bq)
        k = shape(hidden_states @ Wk + bk)
        v = shape(hidden_states @ Wv + bv)
        scores = jnp.einsum('bhqd,bhkd->bhqk', q * scale, k)
        ctx = jnp.arange(S)[:, None]
        mem = jnp.arange(S)[None, :]
        bucket = _relative_position_bucket(mem - ctx)
        position_bias = rel_bias[bucket].transpose(2, 0, 1)[None]
        scores = scores + position_bias * 8.0
        attn = jax.nn.softmax(scores.astype(jnp.float32), axis=-1).astype(scores.dtype)
        ctx_out = jnp.einsum('bhqk,bhkd->bhqd', attn, v)
        ctx_out = ctx_out.transpose(0, 2, 1, 3).reshape(B, S, N_EMBD)
        return ctx_out @ Wo + bo

    def _L0_attn_b_ref(x, Wqkv, bqkv, Wout, bout):
        import jax, jax.numpy as jnp
        import numpy as np
        B, S, E, H = (4, 256, 128, 16)
        HD = E // H
        b, s, e = x.shape
        qkv = x @ Wqkv + bqkv
        qkv = qkv.reshape(b, s, H, 3 * HD)
        q, k, v = (qkv[..., :HD], qkv[..., HD:2 * HD], qkv[..., 2 * HD:])
        scores = jnp.einsum('bqhd,bkhd->bhqk', q, k) / jnp.sqrt(jnp.float32(HD))
        attn = jax.nn.softmax(scores, axis=-1)
        out = jnp.einsum('bhqk,bkhd->bqhd', attn, v).reshape(b, s, e)
        return out @ Wout + bout

    def _L0_ffn_ref(x, gate_w, w1, b1, w2, b2):
        import jax, jax.numpy as jnp
        import numpy as np
        TEMPERATURE = 1.0
        TOPK = 2
        s, b, h = x.shape
        x_flat = x.reshape(s * b, h)
        logits = x_flat @ gate_w.T
        probs = jax.nn.softmax(logits / TEMPERATURE, axis=-1)
        topk_probs, topk_idx = jax.lax.top_k(probs, TOPK)
        hidden = jax.nn.relu(jnp.einsum('th,ehf->tef', x_flat, w1) + b1[None])
        all_out = jnp.einsum('tef,efh->teh', hidden, w2) + b2[None]
        gathered = jnp.take_along_axis(all_out, topk_idx[:, :, None], axis=1)
        y_flat = jnp.sum(gathered * topk_probs[:, :, None], axis=1)
        return y_flat.reshape(s, b, h)
    x = L0_attn_a_hidden_states
    x = x + _L0_attn_a_ref(_layernorm(x, axis=-1), L0_attn_a_Wq, L0_attn_a_bq, L0_attn_a_Wk, L0_attn_a_bk, L0_attn_a_Wv, L0_attn_a_bv, L0_attn_a_Wo, L0_attn_a_bo, L0_attn_a_rel_bias)
    x = x + _L0_ffn_ref(_layernorm(x, axis=-1), L0_ffn_gate_w, L0_ffn_w1, L0_ffn_b1, L0_ffn_w2, L0_ffn_b2)
    x = x + _L0_attn_b_ref(_layernorm(x, axis=-1), L0_attn_b_Wqkv, L0_attn_b_bqkv, L0_attn_b_Wout, L0_attn_b_bout)
    x = x + _L0_ffn_ref(_layernorm(x, axis=-1), L0_ffn_gate_w, L0_ffn_w1, L0_ffn_b1, L0_ffn_w2, L0_ffn_b2)
    return x

_drawn_inputs = setup_inputs


def setup_inputs(seed=0):
    import zlib

    import numpy as np

    out = dict(_drawn_inputs(seed))
    spreads = {'L0_attn_a_bq': (0.0, 0.1),
     'L0_attn_a_bk': (0.0, 0.1),
     'L0_attn_a_bv': (0.0, 0.1),
     'L0_attn_a_bo': (0.0, 0.1),
     'L0_ffn_b1': (0.0, 0.1),
     'L0_ffn_b2': (0.0, 0.1)}
    factors = {}
    for name, (base, spread) in spreads.items():
        noise = np.random.default_rng([zlib.crc32(name.encode()), seed]).standard_normal(out[name].shape)
        drawn = base * np.exp(spread * noise) if base else spread * noise
        out[name] = jnp.asarray(drawn.astype(out[name].dtype))
    for name, factor in factors.items():
        out[name] = (out[name] * factor).astype(out[name].dtype)
    return out
```

```python
import concourse.bass as bass
from concourse import mybir
from contextlib import ExitStack
import numpy as np

F32 = mybir.dt.float32
BF16 = mybir.dt.bfloat16
ALU = mybir.AluOpType
ACT = mybir.ActivationFunctionType
AX = mybir.AxisListType

BATCH, SEQ, EMBD = 16, 512, 128
P = 128
TILES = SEQ // P
HEADS, HEAD_DIM = 16, 8
GROUPS, GROUP = 4, 4
EXPERTS, FFN_DIM = 8, 512
FFN_CHUNKS = FFN_DIM // P
BUCKETS, MAX_DISTANCE = 32, 64
LN_EPS = 1e-5
PARTS = 3
PROD_ROWS = PARTS * PARTS * HEAD_DIM
CONST_ROW = PROD_ROWS
MAX_ROW = 96
A_ROWS = MAX_ROW
B_ROWS = MAX_ROW + PARTS
BAND = P + MAX_DISTANCE
LOADS = 4
V_COLS = HEAD_DIM + 1


class Step:

    def __init__(self, first, stride=0, reg=None):
        self.first, self.stride, self.reg = first, stride, reg

    def at(self, count):
        base = count(self.first)
        if self.reg is None:
            return base
        rate = count(self.first + self.stride) - base
        return base + rate * self.reg


def wait(eng, sem, value):
    if isinstance(value, int) and value <= 0:
        return
    eng.wait_ge(sem, value)


class Sems:

    def __init__(self, nc):
        self.nc, self.held = nc, []

    def new(self, name):
        self.held.append(self.nc.alloc_semaphore(name))
        return self.held[-1]

    def clear(self):
        self.nc.clear_and_free_semaphores(self.held)
        self.nc.all_engine_barrier()
        self.held = []


def wait_apart(eng, sem, value, passed):
    eng.wait_ge(sem, value)
    eng.sem_inc(passed, 1)


def bias_buckets(limit):
    d = np.arange(limit)
    exact = BUCKETS // 2
    far = np.maximum(d, 1).astype(np.float32)
    large = exact + (np.log(far / np.float32(exact)) / np.float32(np.log(MAX_DISTANCE / exact))
                     * np.float32(BUCKETS - exact)).astype(np.int32)
    return np.where(d < exact, d, np.minimum(large, BUCKETS - 1))


def tokens(x, first):
    if isinstance(first, int):
        return x[:, first:first + TILES]
    return x[:, bass.ds(first, TILES)]


def words(stack):
    return stack.rearrange("p h q -> p (h q)").bitcast(F32)


def load_phase(nc, sems, x_dram, x_sb, mv_all, ident):
    with ExitStack() as ctx:
        stats = ctx.enter_context(nc.sbuf_tensor("ld_stats", [P, TILES, 6], F32))
        mv = ctx.enter_context(nc.sbuf_tensor("ld_mv", [P, TILES, 2], F32))
        x_loaded = [sems.new(f"ld_x_loaded{i}") for i in range(LOADS)]
        stats_done = sems.new("ld_stats_done")
        mv_done = sems.new("ld_mv_done")
        mv_kept = sems.new("ld_mv_kept")
        passed = sems.new("ld_passed")
        zeroed = sems.new("ld_zeroed")
        ident_done = sems.new("ld_ident_done")
        x_tiles = x_dram.rearrange("b (t p) e -> p (b t) e", p=P)
        with nc.Block() as block:
            @block.sync
            def _(sp):
                n = BATCH * TILES // LOADS
                for i in range(LOADS):
                    sp.dma_start(x_sb[:, i * n:(i + 1) * n, :], x_tiles[:, i * n:(i + 1) * n, :]
                                 ).then_inc(x_loaded[i], 16)

            @block.gpsimd
            def _(pool):
                nc.gpsimd.memset(ident[:], 0.0).then_inc(zeroed, 1)
                pool.wait_ge(zeroed, 1)
                nc.gpsimd.affine_select(out=ident[:], in_=ident[:], compare_op=ALU.not_equal, fill=1.0, base=0,
                                        pattern=[[-1, P]], channel_multiplier=1).then_inc(ident_done, 1)
                pool.wait_ge(ident_done, 1)

            @block.vector
            def _(dve):
                for i in range(LOADS):
                    dve.wait_ge(x_loaded[i], 16)
                    with dve.Fori(i * BATCH // LOADS, (i + 1) * BATCH // LOADS) as b:
                        x_b = tokens(x_sb, b * TILES)
                        for t in range(TILES):
                            nc.vector.bn_stats(stats[:, t, :], x_b[:, t, :]).then_inc(stats_done, 1)
                        wait_apart(dve, stats_done, (b + 1) * TILES, passed)
                        for t in range(TILES):
                            nc.vector.bn_aggr(mv[:, t, :], stats[:, t, :]).then_inc(mv_done, 1)
                        wait_apart(dve, mv_done, (b + 1) * TILES, passed)
                        nc.vector.tensor_copy(tokens(mv_all, b * TILES), mv[:]).then_inc(mv_kept, 1)
                        dve.wait_ge(mv_kept, b + 1)


class Norm:

    def __init__(self, nc, sems, ctx, tag, mv_all, rstd):
        self.nc, self.mv_all, self.rstd = nc, mv_all, rstd
        self.var = ctx.enter_context(nc.sbuf_tensor(tag + "_var", [P, BATCH * TILES], F32))
        self.root = ctx.enter_context(nc.sbuf_tensor(tag + "_root", [P, BATCH * TILES], F32))
        self.var_ready = sems.new(tag + "_var_ready")
        self.root_ready = sems.new(tag + "_root_ready")
        self.chain = sems.new(tag + "_rstd_chain")

    def on_scalar(self, act):
        act.wait_ge(self.var_ready, 1)
        self.nc.scalar.activation(self.root[:], self.var[:], ACT.Sqrt).then_inc(self.root_ready, 1)

    def on_vector(self, dve):
        nc, var, root, rstd = self.nc, self.var, self.root, self.rstd
        nc.vector.tensor_scalar(var[:], self.mv_all[:, :, 1], LN_EPS, None, ALU.add).then_inc(self.var_ready, 1)
        dve.wait_ge(self.root_ready, 1)
        nc.vector.reciprocal(rstd[:], root[:]).then_inc(self.chain, 1)
        dve.wait_ge(self.chain, 1)
        nc.vector.tensor_tensor(root[:], rstd[:], rstd[:], ALU.mult).then_inc(self.chain, 1)
        dve.wait_ge(self.chain, 2)
        nc.vector.tensor_tensor(root[:], root[:], var[:], ALU.mult).then_inc(self.chain, 1)
        dve.wait_ge(self.chain, 3)
        nc.vector.tensor_scalar(root[:], root[:], -0.5, 1.5, ALU.mult, ALU.add).then_inc(self.chain, 1)
        dve.wait_ge(self.chain, 4)
        nc.vector.tensor_tensor(rstd[:], rstd[:], root[:], ALU.mult).then_inc(self.chain, 1)
        dve.wait_ge(self.chain, 5)


STAGE_LAG = {"front": 2, "A": 1, "B": 0, "tail": -1}
SLOTS = HEADS
SPARE_USES = [
    (1, "max_hi", "B"), (2, "heads2", "tail"), (3, "xT", "front"), (4, "q", "front"), (5, "heads3", "tail"),
    (6, "k", "front"), (7, "outT", "tail"), (8, "v", "front"), (9, "max_lo", "A"), (10, "y", "tail"),
    (11, "heads0", "B"), (14, "heads1", "B"),
]


def active(stage, s):
    return 0 <= s + STAGE_LAG[stage] < BATCH


def spare_before(s):
    return sum(active(u[2], n) for n in range(-2, s) for u in SPARE_USES)


def spare_index(what):
    def count(s):
        n = spare_before(s)
        for _, name, stage in SPARE_USES:
            n += active(stage, s)
            if name == what:
                return n
    return count


def attention_phase(nc, sems, tag, x_sb, mv_all, rstd, ident, w_dram, rel_bias):
    scale = float(1.0 / np.sqrt(HEAD_DIM))
    biased = rel_bias is not None
    with ExitStack() as ctx:
        def sb(name, shape, dt=F32):
            return ctx.enter_context(nc.sbuf_tensor(tag + name, shape, dt))

        def sem(name):
            return sems.new(tag + name)

        norm = Norm(nc, sems, ctx, tag, mv_all, rstd)
        w_sb = sb("w", [P, 4, EMBD])
        qk_bias = sb("qk_bias", [P, 2])
        bv_rows = sb("bv_rows", [P, EMBD])
        bo_rows = sb("bo_rows", [P, EMBD])
        x_norm = sb("x_norm", [P, TILES, EMBD])
        x_normT = sb("x_normT", [P, SEQ])
        proj = sb("proj", [P, SEQ])
        rest = sb("rest", [P, SEQ])
        parts = [sb("q_parts", [P, PARTS, SEQ], BF16), sb("k_parts", [P, PARTS, SEQ], BF16)]
        v_stage = sb("v_stage", [P, TILES, HEADS, V_COLS])
        v_aug = [sb(f"v_aug{i}", [P, TILES, HEADS, V_COLS]) for i in range(2)]
        q_stack = [sb(f"q_stack{i}", [P, HEADS, SEQ], BF16) for i in range(2)]
        k_stack = [sb(f"k_stack{i}", [P, HEADS, SEQ], BF16) for i in range(2)]
        row_max = sb("row_max", [P, HEADS * TILES])
        max_rest = sb("max_rest", [HEADS * TILES // 2, P])
        max_parts = sb("max_parts", [HEADS * TILES // 2, PARTS, P], BF16)
        probs = sb("probs", [P, 2 * GROUP, TILES, SEQ])
        heads_raw = [sb(f"heads_raw{i}", [P, SEQ]) for i in range(2)]
        recip = sb("recip", [P, TILES, GROUP, 1])
        heads_out = sb("heads_out", [P, TILES, EMBD])
        heads_outT = sb("heads_outT", [P, SEQ])
        stats = sb("stats", [P, TILES, 6])
        mv = sb("mv", [P, TILES, 2])
        band = sb("band", [P, HEADS, BAND]) if biased else None
        a_ps = ctx.enter_context(nc.psum_tensor(tag + "a_ps", [P, TILES, SEQ], F32))
        b_ps = ctx.enter_context(nc.psum_tensor(tag + "b_ps", [P, 2, SEQ], F32))
        o_ps = ctx.enter_context(nc.psum_tensor(tag + "o_ps", [P, SEQ], F32))
        spare = ctx.enter_context(nc.psum_tensor(tag + "spare", [P, SEQ], F32))
        parts_dram = [nc.dram_tensor(f"{tag}parts_{n}", (EMBD, PARTS, SEQ), BF16, kind="Internal").ap() for n in "qk"]

        weights_loaded = sem("weights_loaded")
        filled = sem("filled")
        if biased:
            setup_bias(nc, sems, tag, probs, heads_outT, heads_raw, q_stack, k_stack, band, rel_bias, spare)
        with nc.Block() as block:
            @block.sync
            def _(sp):
                for i, n in enumerate(("wq", "wk", "wv", "wo")):
                    dst = w_sb[:, i, :]
                    if len(w_dram[n].shape) == 3:
                        dst = dst.rearrange("p (h d) -> p h d", d=HEAD_DIM)
                    sp.dma_start(dst, w_dram[n]).then_inc(weights_loaded, 16)
                for i, n in enumerate(("bq", "bk")):
                    sp.dma_start(qk_bias[:, i:i + 1], w_dram[n]).then_inc(weights_loaded, 16)
                bv_dst = bv_rows[:]
                if len(w_dram["bv"].shape) == 3:
                    bv_dst = bv_dst.rearrange("p (h d) -> p h d", d=HEAD_DIM)
                sp.dma_start(bv_dst, w_dram["bv"]).then_inc(weights_loaded, 16)
                sp.dma_start(bo_rows[:], w_dram["bo"]).then_inc(weights_loaded, 16)
                sp.wait_ge(weights_loaded, 16 * 8)

            @block.gpsimd
            def _(pool):
                if not biased:
                    for i in range(2):
                        nc.gpsimd.memset(words(k_stack[i][64:MAX_ROW]), 0.0).then_inc(filled, 1)
                        pool.wait_ge(filled, i + 1)

            @block.scalar
            def _(act):
                norm.on_scalar(act)

            @block.vector
            def _(dve):
                norm.on_vector(dve)
                if not biased:
                    for i in range(2):
                        nc.vector.memset(words(q_stack[i][64:MAX_ROW]), 0.0)
                nc.vector.memset(o_ps[:], 0.0)
                nc.vector.memset(v_stage[:, :, :, HEAD_DIM:V_COLS], 1.0)
                for i in range(2):
                    nc.vector.memset(k_stack[i][MAX_ROW:B_ROWS], 1.0)
                dve.wait_ge(weights_loaded, 16 * 8)
                nc.vector.tensor_scalar(qk_bias[:, 0:1], qk_bias[:, 0:1], scale, None, ALU.mult)

        x_normed = sem("x_normed")
        spare_full = sem("spare_full")
        spare_free = sem("spare_free")
        high_ready = sem("high_ready")
        rest_ready = sem("rest_ready")
        mid_ready = sem("mid_ready")
        parts_ready = sem("parts_ready")
        parts_stored = sem("parts_stored")
        stack_loaded = [sem(f"stack_loaded{i}") for i in range(2)]
        v_ready = sem("v_ready")
        a_full = sem("a_full")
        max_taken = sem("max_taken")
        max_chain = sem("max_chain")
        max_stored = [sem(f"max_stored{i}") for i in range(2)]
        b_full = sem("b_full")
        exp_done = sem("exp_done")
        band_done = sem("band_done")
        pv_done = sem("pv_done")
        heads_kept = sem("heads_kept")
        recip_ready = sem("recip_ready")
        x_added = sem("x_added")
        stats_ready = sem("stats_ready")
        mv_ready = sem("mv_ready")
        mv_kept = sem("mv_kept")
        passed = sem("passed")

        band_rate = 1 if biased else 0
        slot_of = {what: slot for slot, what, _ in SPARE_USES}
        per_half = PARTS + PARTS * PARTS
        half = HEADS // 2
        PAIRS = HEADS * TILES // 2

        def steps(eng, step, unrolled=2):
            for s in (-2, -1, 0):
                step(Step(s), s % 2, lambda stage, s=s: active(stage, s))
            with eng.Fori(0, (BATCH - 4) // unrolled) as reg:
                for i in range(unrolled):
                    step(Step(1 + i, unrolled, reg), (1 + i) % 2, lambda stage: True)
            for s in range(BATCH - 3, BATCH + 1):
                step(Step(s), s % 2, lambda stage, s=s: active(stage, s))

        with nc.Block() as block:
            @block.sync
            def _(sp):
                def load_stacks(which, h):
                    for i in range(PARTS):
                        row = i * PARTS * HEAD_DIM
                        rows = slice(row, row + PARTS * HEAD_DIM)
                        heads = slice(h * half, (h + 1) * half)
                        k_rows = parts_dram[1].rearrange("(h d) j n -> (d j) h n", d=HEAD_DIM)
                        q_rows = parts_dram[0].rearrange("(h d) j n -> d j h n", d=HEAD_DIM)
                        sp.dma_start(k_stack[which][rows, heads, :], k_rows[:, heads, :]).then_inc(stack_loaded[h], 16)
                        for j in range(PARTS):
                            dst = q_stack[which][row + j:row + j + PARTS * (HEAD_DIM - 1) + 1:PARTS, heads, :]
                            sp.dma_start(dst, q_rows[:, i, heads, :]).then_inc(stack_loaded[h], 16)

                def store_max(which, h, count):
                    sp.wait_ge(max_chain, count)
                    for i in range(PARTS):
                        sp.dma_start(q_stack[which][MAX_ROW + i:MAX_ROW + i + 1, h * half:(h + 1) * half, :],
                                     max_parts[:, i, :]).then_inc(max_stored[h], 16)

                def step(st, par, on):
                    if on("A"):
                        wait(sp, b_full, st.at(lambda s: HEADS * TILES * s))
                        load_stacks(1 - par, 1)
                    if on("B"):
                        store_max(par, 1, st.at(lambda s: 6 * s + 6))
                    if on("A"):
                        wait_apart(sp, stack_loaded[1], st.at(lambda s: 16 * per_half * (s + 2)), passed)
                    if on("front"):
                        for i in range(2):
                            sp.wait_ge(parts_ready, st.at(lambda s: 2 * (s + 2) + i + 1))
                            sp.dma_start(parts_dram[i], parts[i][:]).then_inc(parts_stored, 16)
                        wait_apart(sp, parts_stored, st.at(lambda s: 32 * (s + 3)), passed)
                        wait(sp, b_full, st.at(lambda s: HEADS * TILES * s + half * TILES))
                        load_stacks(par, 0)
                    if on("A"):
                        store_max(1 - par, 0, st.at(lambda s: 6 * (s + 1) + 3))
                    if on("front"):
                        wait_apart(sp, stack_loaded[0], st.at(lambda s: 16 * per_half * (s + 3)), passed)

                steps(sp, step)
                for h in range(2):
                    sp.wait_ge(stack_loaded[h], 16 * per_half * BATCH)
                    sp.wait_ge(max_stored[h], 16 * PARTS * BATCH)

            @block.tensor
            def _(pe):
                def use_spare(st, what):
                    wait(pe, spare_free, st.at(lambda s: spare_index(what)(s) - 1))

                def transposes(out, src, rows):
                    for t in range(TILES):
                        last = nc.tensor.transpose(out[0:rows, t * P:(t + 1) * P], src(t), ident[:])
                    return last

                def spare_use(st, what, par):
                    if what in ("max_lo", "max_hi"):
                        if what == "max_lo":
                            pe.wait_ge(max_taken, st.at(lambda s: PAIRS * (s + 1) + PAIRS // 2))
                            src = row_max[:, 0:half * TILES]
                        else:
                            pe.wait_ge(max_taken, st.at(lambda s: PAIRS * (s + 1)))
                            src = row_max[:, half * TILES:HEADS * TILES]
                        use_spare(st, what)
                        last = nc.tensor.transpose(spare[0:half * TILES, 0:P], src, ident[:])
                    elif what == "xT":
                        pe.wait_ge(x_normed, st.at(lambda s: s + 3))
                        use_spare(st, what)
                        last = transposes(spare, lambda t: x_norm[:, t, :], P)
                    elif what in ("q", "k", "v"):
                        use_spare(st, what)
                        if what == "v":
                            for t in range(TILES):
                                last = nc.tensor.matmul(spare[:, t * P:(t + 1) * P], x_normT[:, t * P:(t + 1) * P],
                                                        w_sb[:, 2, :], start=True, stop=True)
                        else:
                            last = nc.tensor.matmul(spare[:], w_sb[:, "qk".index(what), :], x_normT[:],
                                                    start=True, stop=True)
                    elif what[:-1] == "heads":
                        g = int(what[-1])
                        batch_of = (lambda s: s - 1) if g >= 2 else (lambda s: s)
                        pe.wait_ge(heads_kept, st.at(lambda s: GROUPS * batch_of(s) + g + 1))
                        use_spare(st, what)
                        last = transposes(spare, lambda t: heads_raw[g % 2][:, t * P:(t + 1) * P], P)
                    elif what == "outT":
                        use_spare(st, what)
                        last = transposes(spare, lambda t: heads_out[:, t, :], P)
                    elif what == "y":
                        use_spare(st, what)
                        for t in range(TILES):
                            last = nc.tensor.matmul(spare[:, t * P:(t + 1) * P], heads_outT[:, t * P:(t + 1) * P],
                                                    w_sb[:, 3, :], start=True, stop=True)
                    last.then_inc(spare_full, 1)

                def value_products(st, par, on, slot):
                    g, c = slot // GROUP - 1, slot % GROUP
                    if not (on("B") if g >= 0 else on("tail")):
                        return
                    g, lag, which = (g, 0, par) if g >= 0 else (GROUPS - 1, 1, 1 - par)
                    if c == 0:
                        if biased:
                            pe.wait_ge(band_done, st.at(lambda s: HEADS * (s - lag) + GROUP * (g + 1)))
                        else:
                            pe.wait_ge(exp_done, st.at(lambda s: TILES * (HEADS * (s - lag) + GROUP * (g + 1))))
                        pe.wait_ge(v_ready, st.at(lambda s: s - lag + 1))
                        wait(pe, heads_kept, st.at(lambda s: GROUPS * (s - lag) + g))
                    for j in range(GROUP):
                        h = GROUP * g + j
                        last = nc.tensor.matmul(o_ps[32 * j:32 * j + V_COLS, :], v_aug[which][:, c, h, :],
                                                probs[:, h % (2 * GROUP), c, :],
                                                start=(c == 0), stop=(c == TILES - 1))
                    last.then_inc(pv_done, 1)

                def step(st, par, on):
                    for slot in range(SLOTS):
                        if on("A") and slot % half == 0:
                            pe.wait_ge(stack_loaded[slot // half], st.at(lambda s: 16 * per_half * (s + 2)))
                        if on("B") and slot % half == 0:
                            pe.wait_ge(max_stored[slot // half], st.at(lambda s: 16 * PARTS * (s + 1)))
                        for c in range(TILES):
                            if on("A"):
                                if c % 2 == 0:
                                    wait(pe, max_taken, st.at(lambda s: PAIRS * (s + 1) + 2 * slot + c // 2 - 1))
                                last = nc.tensor.matmul(a_ps[:, c, :],
                                                        q_stack[1 - par][0:A_ROWS, slot, c * P:(c + 1) * P],
                                                        k_stack[1 - par][0:A_ROWS, slot, :], start=True, stop=True)
                                if c % 2 == 1:
                                    last.then_inc(a_full, 1)
                            if on("B"):
                                wait(pe, exp_done, st.at(lambda s: HEADS * TILES * s + TILES * slot + c - 1))
                                nc.tensor.matmul(b_ps[:, c % 2, :],
                                                 k_stack[par][0:B_ROWS, slot, c * P:(c + 1) * P],
                                                 q_stack[par][0:B_ROWS, slot, :],
                                                 start=True, stop=True).then_inc(b_full, 1)
                            if c == (TILES - 1 if slot % GROUP == 0 else 1):
                                value_products(st, par, on, slot)
                        for at, what, stage in SPARE_USES:
                            if at == slot and on(stage):
                                spare_use(st, what, par)

                steps(pe, step)

            @block.scalar
            def _(act):
                def split_high(st, i):
                    wait(act, parts_stored, st.at(lambda s: 32 * (s + 2)))
                    nc.scalar.activation(parts[i][:, 0, :], proj[:], ACT.Copy).then_inc(high_ready, 1)

                def split_mid(st, i):
                    n = lambda s: 2 * (s + 2) + i + 1
                    act.wait_ge(rest_ready, st.at(n))
                    nc.scalar.activation(parts[i][:, 1, :], rest[:], ACT.Copy).then_inc(mid_ready, 1)

                def spare_read(st, what):
                    if what == "xT":
                        act.wait_ge(spare_full, st.at(spare_index(what)))
                        nc.scalar.copy(x_normT[:], spare[:]).then_inc(spare_free, 1)
                    elif what in ("q", "k"):
                        i = "qk".index(what)
                        wait(act, rest_ready, st.at(lambda s: 2 * (s + 2) + i))
                        act.wait_ge(spare_full, st.at(spare_index(what)))
                        nc.scalar.activation(proj[:], spare[:], ACT.Identity, bias=qk_bias[:, i:i + 1],
                                             scale=(scale, 1.0)[i]).then_inc(spare_free, 1)
                        act.wait_ge(spare_free, st.at(spare_index(what)))
                        split_high(st, i)
                    elif what == "outT":
                        act.wait_ge(spare_full, st.at(spare_index(what)))
                        nc.scalar.copy(heads_outT[:], spare[:]).then_inc(spare_free, 1)

                def keep_heads(st, g, lag):
                    act.wait_ge(pv_done, st.at(lambda s: HEADS * (s - lag) + GROUP * (g + 1)))
                    before = ("heads2", "heads3", "heads0", "heads1")[g]
                    wait(act, spare_full, st.at(lambda s: spare_index(before)(s - lag)))
                    nc.scalar.copy(heads_raw[g % 2][:], o_ps[:]).then_inc(heads_kept, 1)

                def step(st, par, on):
                    for slot in range(SLOTS):
                        g = slot // GROUP - 2
                        if slot % GROUP == 0:
                            if g >= 0 and on("B"):
                                keep_heads(st, g, 0)
                            if g < 0 and on("tail"):
                                keep_heads(st, g + GROUPS, 1)
                        if on("B"):
                            wait(act, pv_done, st.at(lambda s: HEADS * s + GROUP * (slot // GROUP) - GROUP))
                            for c in range(TILES):
                                act.wait_ge(b_full, st.at(lambda s: HEADS * TILES * s + TILES * slot + c + 1))
                                nc.scalar.activation(probs[:, slot % (2 * GROUP), c, :], b_ps[:, c % 2, :],
                                                     ACT.Exp).then_inc(exp_done, 1)
                        for at, what, stage in SPARE_USES:
                            if at == slot and on(stage):
                                spare_read(st, what)
                        if on("front") and slot in (slot_of["q"] + 1, slot_of["k"] + 1):
                            split_mid(st, 0 if slot == slot_of["q"] + 1 else 1)

                steps(act, step)

            @block.gpsimd
            def _(pool):
                def rests(st, i):
                    n = lambda s: 2 * (s + 2) + i + 1
                    wait(pool, parts_ready, st.at(lambda s: 2 * (s + 2) + i))
                    pool.wait_ge(high_ready, st.at(n))
                    nc.gpsimd.tensor_tensor(rest[:], proj[:], parts[i][:, 0, :], ALU.subtract).then_inc(rest_ready, 1)

                def last_part(st, i):
                    n = lambda s: 2 * (s + 2) + i + 1
                    pool.wait_ge(mid_ready, st.at(n))
                    nc.gpsimd.tensor_tensor(parts[i][:, 2, :], rest[:], parts[i][:, 1, :],
                                            ALU.subtract).then_inc(parts_ready, 1)

                def step(st, par, on):
                    for slot in range(SLOTS):
                        for i, what in enumerate("qk"):
                            if on("front") and slot == slot_of[what] + 1:
                                rests(st, i)
                        if biased and on("B"):
                            pool.wait_ge(exp_done, st.at(lambda s: TILES * (HEADS * s + slot + 1)))
                            flat = probs[:, slot % (2 * GROUP), :, :].rearrange("p c q -> p (c q)")
                            diagonal = SEQ + P
                            first = flat[:, 0:(TILES - 1) * diagonal].rearrange("p (c q) -> p c q", q=diagonal)
                            first = first[:, :, 0:BAND]
                            table = band[:, slot:slot + 1, :].broadcast_to([P, TILES - 1, BAND])
                            nc.gpsimd.tensor_tensor(first, first, table, ALU.mult)
                            final = flat[:, (TILES - 1) * diagonal:(TILES - 1) * diagonal + P]
                            nc.gpsimd.tensor_tensor(final, final, band[:, slot, 0:P],
                                                    ALU.mult).then_inc(band_done, 1)
                        for i, what in enumerate("qk"):
                            if on("front") and slot == slot_of[what] + 1:
                                last_part(st, i)

                steps(pool, step)

            @block.vector
            def _(dve):
                def normalize(st):
                    wait(dve, spare_full, st.at(lambda s: spare_index("xT")(s - 1)))
                    x_b = tokens(x_sb, st.at(lambda s: TILES * (s + 2)))
                    mean = tokens(mv_all, st.at(lambda s: TILES * (s + 2)))
                    r = tokens(rstd, st.at(lambda s: TILES * (s + 2)))
                    for t in range(TILES):
                        last = nc.vector.tensor_scalar(x_norm[:, t, :], x_b[:, t, :], mean[:, t, 0:1], r[:, t:t + 1],
                                                       ALU.subtract, ALU.mult)
                    last.then_inc(x_normed, 1)

                def split_max(st, what):
                    h = 0 if what == "max_lo" else 1
                    batch = (lambda s: s + 1) if h == 0 else (lambda s: s)
                    base = lambda s: 6 * batch(s) + 3 * h
                    if h == 0:
                        wait(dve, max_stored[1], st.at(lambda s: 16 * PARTS * (s + 1)))
                    else:
                        wait(dve, max_stored[0], st.at(lambda s: 16 * PARTS * (s + 1)))
                    dve.wait_ge(spare_full, st.at(spare_index(what)))
                    scores_max = spare[0:half * TILES, 0:P]
                    nc.vector.tensor_scalar(max_parts[:, 0, :], scores_max, -1.0, None,
                                            ALU.mult).then_inc(max_chain, 1)
                    dve.wait_ge(max_chain, st.at(lambda s: base(s) + 1))
                    nc.vector.scalar_tensor_tensor(max_rest[:], scores_max, -1.0, max_parts[:, 0, :], ALU.mult,
                                                   ALU.subtract).then_inc(spare_free, 1)
                    dve.wait_ge(spare_free, st.at(spare_index(what)))
                    nc.vector.tensor_copy(max_parts[:, 1, :], max_rest[:]).then_inc(max_chain, 1)
                    dve.wait_ge(max_chain, st.at(lambda s: base(s) + 2))
                    nc.vector.tensor_tensor(max_parts[:, 2, :], max_rest[:], max_parts[:, 1, :],
                                            ALU.subtract).then_inc(max_chain, 1)

                def spare_read(st, what, par):
                    if what in ("max_lo", "max_hi"):
                        split_max(st, what)
                    elif what == "v":
                        wait(dve, v_ready, st.at(lambda s: s + 2))
                        dve.wait_ge(spare_full, st.at(spare_index(what)))
                        v = spare[:].rearrange("p (t h d) -> p t h d", t=TILES, d=HEAD_DIM)
                        for t in range(TILES):
                            last = nc.vector.tensor_tensor(v_stage[:, t, :, 0:HEAD_DIM], v[:, t],
                                                           bv_rows[:].rearrange("p (h d) -> p h d", d=HEAD_DIM),
                                                           ALU.add)
                        last.then_inc(spare_free, 1)
                    elif what[:-1] == "heads":
                        g = int(what[-1])
                        lag = 1 if g >= 2 else 0
                        if g == 0:
                            wait(dve, x_added, st.at(lambda s: s))
                        dve.wait_ge(spare_full, st.at(spare_index(what)))
                        rows = spare[:].rearrange("p (t j r) -> p t j r", t=TILES, j=GROUP)
                        nc.vector.reciprocal(recip[:], rows[:, :, :, HEAD_DIM:V_COLS]).then_inc(recip_ready, 1)
                        dve.wait_ge(recip_ready, st.at(lambda s: GROUPS * (s - lag) + g + 1))
                        out = heads_out[:, :, 32 * g:32 * g + 32].rearrange("p t (j d) -> p t j d", d=HEAD_DIM)
                        nc.vector.tensor_tensor(out, rows[:, :, :, 0:HEAD_DIM],
                                                recip[:].broadcast_to([P, TILES, GROUP, HEAD_DIM]),
                                                ALU.mult).then_inc(spare_free, 1)
                    elif what == "y":
                        dve.wait_ge(spare_full, st.at(spare_index(what)))
                        y = spare[:].rearrange("p (t e) -> p t e", e=EMBD)
                        bo = bo_rows[:].rearrange("p (o e) -> p o e", o=1).broadcast_to([P, TILES, EMBD])
                        nc.vector.tensor_tensor(heads_out[:], y, bo, ALU.add).then_inc(spare_free, 1)
                        dve.wait_ge(spare_free, st.at(spare_index(what)))
                        x_b = tokens(x_sb, st.at(lambda s: TILES * (s - 1)))
                        nc.vector.tensor_tensor(x_b, x_b, heads_out[:], ALU.add).then_inc(x_added, 1)
                        wait_apart(dve, x_added, st.at(lambda s: s), passed)
                        for t in range(TILES):
                            last = nc.vector.bn_stats(stats[:, t, :], x_b[:, t, :])
                        last.then_inc(stats_ready, 1)
                        wait_apart(dve, stats_ready, st.at(lambda s: s), passed)
                        for t in range(TILES):
                            last = nc.vector.bn_aggr(mv[:, t, :], stats[:, t, :])
                        last.then_inc(mv_ready, 1)
                        wait_apart(dve, mv_ready, st.at(lambda s: s), passed)
                        nc.vector.tensor_copy(tokens(mv_all, st.at(lambda s: TILES * (s - 1))),
                                              mv[:]).then_inc(mv_kept, 1)
                        dve.wait_ge(mv_kept, st.at(lambda s: s))

                def step(st, par, on):
                    for slot in range(SLOTS):
                        if on("A"):
                            for i in range(2):
                                dve.wait_ge(a_full, st.at(lambda s: PAIRS * (s + 1) + 2 * slot + i + 1))
                                nc.vector.reduce_max(row_max[:, TILES * slot + 2 * i:TILES * slot + 2 * i + 2],
                                                     a_ps[:, 2 * i:2 * i + 2, :], AX.X).then_inc(max_taken, 1)
                        if on("front") and slot == 0:
                            normalize(st)
                        for at, what, stage in SPARE_USES:
                            if at == slot and on(stage) and what not in ("xT", "q", "k", "outT"):
                                spare_read(st, what, par)
                        if on("A") and slot == 6:
                            wait(dve, pv_done, st.at(lambda s: HEADS * s))
                            dve.wait_ge(spare_free, st.at(lambda s: spare_index("v")(s - 1)))
                            nc.vector.tensor_copy(v_aug[1 - par][:], v_stage[:]).then_inc(v_ready, 1)

                steps(dve, step)


def setup_bias(nc, sems, tag, probs, work_a, work_b, q_stack, k_stack, band, rel_bias, spare):
    deltas = P - 1 + BAND
    bucket = bias_buckets(BAND)
    bucket = np.concatenate([np.full(P - 1, bucket[0]), bucket])
    edges = [0] + [i for i in range(1, deltas) if bucket[i] != bucket[i - 1]] + [deltas]
    with ExitStack() as ctx:
        def sb(name, shape, dt=F32):
            return ctx.enter_context(nc.sbuf_tensor(tag + name, shape, dt))

        def sem(name):
            return sems.new(tag + name)

        largest = sb("largest", [HEADS, 1])
        factors = work_a[0:HEADS, 0:deltas]
        by_head = work_b[0][0:HEADS, 0:BUCKETS]
        flip = work_b[1][:, 0:P]
        work = probs[:].rearrange("p a c q -> p (a c q)")
        const = work[0:HEADS, 0:TILES * SEQ].rearrange("p (c q) -> p c q", q=SEQ)
        rest = work[0:HEADS, TILES * SEQ:2 * TILES * SEQ].rearrange("p (c q) -> p c q", q=SEQ)
        const_parts = work[0:HEADS, 2 * TILES * SEQ:2 * TILES * SEQ + PARTS * TILES * SEQ // 2].bitcast(BF16)
        const_parts = const_parts.rearrange("p (i c q) -> p i c q", i=PARTS, q=SEQ)
        flipped = work[:, 8192:8192 + HEADS * BAND]
        tile_is = work[0:TILES, 12288:12288 + HEADS * SEQ // 2].bitcast(BF16).rearrange("p (h q) -> p h q", q=SEQ)
        factors_dram = nc.dram_tensor(tag + "factors_dram", (HEADS, deltas), F32, kind="Internal").ap()
        const_dram = nc.dram_tensor(tag + "const_dram", (HEADS, PARTS * TILES, SEQ), BF16, kind="Internal").ap()

        bias_loaded = sem("bias_loaded")
        chain = sem("bias_chain")
        run_ready = sem("run_ready")
        factors_ready = sem("factors_ready")
        factors_stored = sem("factors_stored")
        flipped_loaded = sem("flipped_loaded")
        const_zeroed = sem("const_zeroed")
        const_ready = sem("const_ready")
        const_stored = sem("const_stored")
        stacks_filled = sem("stacks_filled")
        q_filled = sem("q_filled")
        rows_loaded = sem("rows_loaded")
        flip_steps = sem("flip_steps")
        tiles_marked = sem("tiles_marked")
        band_full = sem("band_full")
        band_kept = sem("band_kept")
        with nc.Block() as block:
            @block.sync
            def _(sp):
                with nc.allow_non_contiguous_dma("a table of 512 values, transposed"):
                    sp.dma_start(by_head, rel_bias.rearrange("b h -> h b")).then_inc(bias_loaded, 16)
                sp.wait_ge(factors_ready, 1)
                sp.dma_start(factors_dram, factors).then_inc(factors_stored, 16)
                sp.wait_ge(factors_stored, 16)
                windows = bass.AP(tensor=factors_dram.tensor, offset=factors_dram.offset,
                                  ap=[[1, P], [deltas, HEADS], [1, BAND]])
                sp.dma_start(flipped.rearrange("p (h q) -> p h q", q=BAND), windows).then_inc(flipped_loaded, 16)
                sp.wait_ge(const_ready, 1)
                sp.dma_start(const_dram.rearrange("h r q -> h (r q)"),
                             const_parts.rearrange("p i c q -> p (i c q)")).then_inc(const_stored, 16)
                sp.wait_ge(const_stored, 16)
                sp.wait_ge(stacks_filled, 2)
                sp.wait_ge(q_filled, 2)
                sp.wait_ge(tiles_marked, 2)
                for which in range(2):
                    sp.dma_start(q_stack[which][CONST_ROW:CONST_ROW + PARTS * TILES, :, :],
                                 const_dram.rearrange("h r q -> r h q")).then_inc(rows_loaded, 16)
                    for i in range(PARTS):
                        row = CONST_ROW + i * TILES
                        sp.dma_start(k_stack[which][row:row + TILES, :, :], tile_is).then_inc(rows_loaded, 16)
                sp.wait_ge(rows_loaded, 16 * 2 * (1 + PARTS))

            @block.gpsimd
            def _(pool):
                for i in range(2):
                    nc.gpsimd.memset(words(k_stack[i][64:MAX_ROW]), 0.0).then_inc(stacks_filled, 1)
                    pool.wait_ge(stacks_filled, i + 1)
                nc.gpsimd.memset(flip, 0.0).then_inc(flip_steps, 1)
                pool.wait_ge(flip_steps, 1)
                nc.gpsimd.affine_select(out=flip, in_=flip, compare_op=ALU.not_equal, fill=1.0, base=-(P - 1),
                                        pattern=[[1, P]], channel_multiplier=1).then_inc(flip_steps, 1)
                pool.wait_ge(flip_steps, 2)
                nc.gpsimd.memset(tile_is, 1.0).then_inc(flip_steps, 1)
                pool.wait_ge(flip_steps, 3)
                nc.gpsimd.affine_select(out=tile_is, in_=tile_is, compare_op=ALU.is_ge, fill=0.0, base=0,
                                        pattern=[[0, HEADS], [1, SEQ]], channel_multiplier=-P).then_inc(tiles_marked, 1)
                pool.wait_ge(tiles_marked, 1)
                nc.gpsimd.affine_select(out=tile_is, in_=tile_is, compare_op=ALU.is_ge, fill=0.0, base=P - 1,
                                        pattern=[[0, HEADS], [-1, SEQ]], channel_multiplier=P).then_inc(tiles_marked, 1)

            @block.scalar
            def _(act):
                act.wait_ge(run_ready, 1)
                nc.scalar.activation(factors, factors, ACT.Exp).then_inc(factors_ready, 1)

            @block.tensor
            def _(pe):
                pe.wait_ge(flip_steps, 2)
                pe.wait_ge(flipped_loaded, 16)
                for n in range(HEADS * BAND // SEQ):
                    if n:
                        pe.wait_ge(band_kept, n)
                    nc.tensor.matmul(spare[:], flip, flipped[:, n * SEQ:(n + 1) * SEQ],
                                     start=True, stop=True).then_inc(band_full, 1)

            @block.vector
            def _(dve):
                links = [0]

                def link(instruction):
                    links[0] += 1
                    instruction.then_inc(chain, 1)
                    dve.wait_ge(chain, links[0])

                dve.wait_ge(bias_loaded, 16)
                link(nc.vector.tensor_scalar(by_head, by_head, 8.0, None, ALU.mult))
                link(nc.vector.reduce_max(largest[:], by_head, AX.X))
                link(nc.vector.tensor_scalar(by_head, by_head, largest[:], None, ALU.subtract))
                for lo, hi in zip(edges[:-1], edges[1:]):
                    b = int(bucket[lo])
                    last = nc.vector.tensor_copy(factors[:, lo:hi], by_head[:, b:b + 1].broadcast_to([HEADS, hi - lo]))
                last.then_inc(run_ready, 1)
                for i in range(2):
                    nc.vector.memset(words(q_stack[i][64:MAX_ROW]), 0.0).then_inc(q_filled, 1)
                link(nc.vector.memset(const, 0.0))
                for c in range(TILES):
                    if c:
                        near = by_head[:, 0:1].broadcast_to([HEADS, c * P])
                        last = nc.vector.tensor_copy(const[:, c, 0:c * P], near)
                    if c * P + BAND < SEQ:
                        far = by_head[:, BUCKETS - 1:BUCKETS].broadcast_to([HEADS, SEQ - c * P - BAND])
                        last = nc.vector.tensor_copy(const[:, c, c * P + BAND:SEQ], far)
                link(last)
                link(nc.vector.tensor_copy(const_parts[:, 0], const))
                link(nc.vector.tensor_tensor(rest, const, const_parts[:, 0], ALU.subtract))
                link(nc.vector.tensor_copy(const_parts[:, 1], rest))
                nc.vector.tensor_tensor(const_parts[:, 2], rest, const_parts[:, 1],
                                        ALU.subtract).then_inc(const_ready, 1)
                for n in range(HEADS * BAND // SEQ):
                    dve.wait_ge(band_full, n + 1)
                    nc.vector.tensor_copy(band[:].rearrange("p h q -> p (h q)")[:, n * SEQ:(n + 1) * SEQ],
                                          spare[:]).then_inc(band_kept, 1)


def ffn_phase(nc, sems, tag, x_sb, mv_all, rstd, ident, gate_w, w1, b1, w2, b2, out_dram):
    with ExitStack() as ctx:
        def sb(name, shape, dt=F32):
            return ctx.enter_context(nc.sbuf_tensor(tag + name, shape, dt))

        def sem(name):
            return sems.new(tag + name)

        norm = Norm(nc, sems, ctx, tag, mv_all, rstd)
        w1_sb = sb("w1", [P, EXPERTS, FFN_DIM])
        w2_sb = sb("w2", [P, EXPERTS, FFN_CHUNKS, EMBD])
        b1_sb = sb("b1", [P, EXPERTS * FFN_CHUNKS])
        b1_rows = sb("b1_rows", [EXPERTS * FFN_CHUNKS, P])
        b2_sb = sb("b2", [EXPERTS, EMBD])
        gate_rows = sb("gate_rows", [EXPERTS, EMBD])
        gate_sb = sb("gate", [P, EXPERTS])
        first_wins = sb("first_wins", [P, EXPERTS])
        x_norm = sb("x_norm", [P, TILES, EMBD])
        x_normT = sb("x_normT", [P, SEQ])
        hidden = sb("hidden", [P, 2, FFN_CHUNKS, SEQ])
        acc = sb("acc", [P, TILES, EMBD])
        gates = sb("gates", [P, TILES, EXPERTS])
        gatesT = sb("gatesT", [EXPERTS, SEQ])
        top = sb("top", [P, TILES, 1])
        prob = sb("prob", [P, TILES, EXPERTS])
        left = sb("left", [P, TILES, EXPERTS])
        key = sb("key", [P, TILES, EXPERTS])
        pick = [sb(f"pick{i}", [P, TILES, EXPERTS]) for i in range(2)]
        stats = sb("stats", [P, TILES, 6])
        mv = sb("mv", [P, TILES, 2])
        up_ps = ctx.enter_context(nc.psum_tensor(tag + "up_ps", [P, FFN_CHUNKS, SEQ], F32))
        down_ps = ctx.enter_context(nc.psum_tensor(tag + "down_ps", [P, 2, SEQ], F32))
        xT_ps = ctx.enter_context(nc.psum_tensor(tag + "xT_ps", [P, SEQ], F32))
        gate_ps = ctx.enter_context(nc.psum_tensor(tag + "gate_ps", [P, SEQ], F32))

        expert_loaded = [sem(f"expert_loaded{e}") for e in range(EXPERTS)]
        small_loaded = sem("small_loaded")
        small_full = sem("small_full")
        small_kept = sem("small_kept")
        x_normed = sem("x_normed")
        xT_full = sem("xT_full")
        xT_kept = sem("xT_kept")
        logits_full = sem("logits_full")
        logits_less = sem("logits_less")
        gate_exp = sem("gate_exp")
        gate_chain = sem("gate_chain")
        gates_ready = sem("gates_ready")
        gatesT_full = sem("gatesT_full")
        gatesT_kept = sem("gatesT_kept")
        b2_full = sem("b2_full")
        up_full = sem("up_full")
        relu_done = sem("relu_done")
        down_full = sem("down_full")
        acc_step = sem("acc_step")
        x_kept = sem("x_kept")
        stats_ready = sem("stats_ready")
        mv_ready = sem("mv_ready")
        mv_kept = sem("mv_kept")
        passed = sem("passed")
        out_stored = sem("out_stored")
        marks = sem("marks")
        acc_init = sem("acc_init")
        pick_chain = sem("pick_chain")
        CHAIN = 14

        def groups(eng, group):
            with eng.Fori(0, BATCH - 1) as reg:
                group(Step(0, 1, reg), False)
            group(Step(BATCH - 1), True)

        with nc.Block() as block:
            @block.sync
            def _(sp):
                sp.dma_start(gate_rows[:], gate_w).then_inc(small_loaded, 16)
                sp.dma_start(b1_rows[:], b1.rearrange("e (c f) -> (e c) f", f=P)).then_inc(small_loaded, 16)
                sp.dma_start(b2_sb[:], b2).then_inc(small_loaded, 16)
                for e in range(EXPERTS):
                    sp.dma_start(w1_sb[:, e, :], w1[e]).then_inc(expert_loaded[e], 16)
                    sp.dma_start(w2_sb[:, e, :, :], w2[e].rearrange("(c f) n -> f c n", f=P)
                                 ).then_inc(expert_loaded[e], 16)
                if out_dram is not None:
                    out_tiles = out_dram.rearrange("b (t p) e -> b p t e", p=P)

                    def group(st, final):
                        wait_apart(sp, x_kept, st.at(lambda u: u + 1), passed)
                        u = st.at(lambda u: u)
                        dst = out_tiles[u] if final else out_tiles[bass.ds(u, 1)].rearrange("o p t e -> (o p) t e")
                        sp.dma_start(dst, tokens(x_sb, st.at(lambda u: TILES * u))).then_inc(out_stored, 16)

                    groups(sp, group)
                    sp.wait_ge(out_stored, 16 * BATCH)

            @block.gpsimd
            def _(pool):
                for e in range(EXPERTS):
                    nc.gpsimd.memset(first_wins[:, e:e + 1], float(EXPERTS - e)).then_inc(marks, 1)

            @block.tensor
            def _(pe):
                pe.wait_ge(small_loaded, 48)
                nc.tensor.transpose(gate_ps[:, 0:EXPERTS], gate_rows[:], ident[0:EXPERTS, 0:EXPERTS])
                nc.tensor.transpose(gate_ps[:, P:P + EXPERTS * FFN_CHUNKS], b1_rows[:],
                                    ident[0:EXPERTS * FFN_CHUNKS, 0:EXPERTS * FFN_CHUNKS]).then_inc(small_full, 1)

                def transpose_x(st, lead):
                    pe.wait_ge(x_normed, st.at(lambda u: u + lead + 1))
                    wait(pe, xT_kept, st.at(lambda u: u + lead))
                    for t in range(TILES):
                        last = nc.tensor.transpose(xT_ps[:, t * P:(t + 1) * P], x_norm[:, t, :], ident[:])
                    last.then_inc(xT_full, 1)

                def up(st, e, first_group):
                    if first_group:
                        pe.wait_ge(expert_loaded[e], 32)
                    for c in range(FFN_CHUNKS):
                        wait(pe, relu_done, st.at(lambda u: FFN_CHUNKS * (EXPERTS * u + e - 1) + c + 1))
                        nc.tensor.matmul(up_ps[:, c, :], w1_sb[:, e, c * P:(c + 1) * P], x_normT[:],
                                         start=True, stop=True).then_inc(up_full, 1)

                def down(st, e):
                    pe.wait_ge(relu_done, st.at(lambda u: FFN_CHUNKS * (EXPERTS * u + e + 1)))
                    wait(pe, acc_step, st.at(lambda u: TILES * (EXPERTS * u + e - 1)))
                    for t in range(TILES):
                        for c in range(FFN_CHUNKS):
                            last = nc.tensor.matmul(down_ps[:, e % 2, t * P:(t + 1) * P],
                                                    hidden[:, e % 2, c, t * P:(t + 1) * P], w2_sb[:, e, c, :],
                                                    start=(c == 0), stop=(c == FFN_CHUNKS - 1))
                    last.then_inc(down_full, 1)

                def group(st, final, first_group=False):
                    pe.wait_ge(xT_kept, st.at(lambda u: u + 1))
                    wait(pe, acc_init, st.at(lambda u: u))
                    for t in range(TILES):
                        last = nc.tensor.matmul(gate_ps[:, t * EXPERTS:(t + 1) * EXPERTS],
                                                x_normT[:, t * P:(t + 1) * P], gate_sb[:], start=True, stop=True)
                    last.then_inc(logits_full, 1)
                    for e in range(EXPERTS):
                        up(st, e, first_group)
                        if e == 2:
                            pe.wait_ge(gates_ready, st.at(lambda u: u + 1))
                            for t in range(TILES):
                                last = nc.tensor.transpose(gate_ps[0:EXPERTS, t * P:(t + 1) * P], gates[:, t, :],
                                                           ident[:])
                            last.then_inc(gatesT_full, 1)
                        if e == EXPERTS - 1 and not final:
                            transpose_x(st, 1)
                        if e > 0:
                            down(st, e - 1)
                        if e == 2:
                            pe.wait_ge(gatesT_kept, st.at(lambda u: u + 1))
                            for t in range(TILES):
                                last = nc.tensor.matmul(gate_ps[:, t * P:(t + 1) * P], gatesT[:, t * P:(t + 1) * P],
                                                        b2_sb[:], start=True, stop=True)
                            last.then_inc(b2_full, 1)
                    down(st, EXPERTS - 1)

                pe.wait_ge(small_kept, 2)
                transpose_x(Step(0), 0)
                group(Step(0), False, True)
                with pe.Fori(0, BATCH - 2) as reg:
                    group(Step(1, 1, reg), False)
                group(Step(BATCH - 1), True)

            @block.scalar
            def _(act):
                norm.on_scalar(act)
                def keep_xT(st, lead):
                    wait(act, up_full, st.at(lambda u: EXPERTS * FFN_CHUNKS * (u + lead)))
                    act.wait_ge(xT_full, st.at(lambda u: u + lead + 1))
                    nc.scalar.copy(x_normT[:], xT_ps[:]).then_inc(xT_kept, 1)

                def group(st, final):
                    for e in range(EXPERTS):
                        if e == 1:
                            act.wait_ge(logits_less, st.at(lambda u: u + 1))
                            nc.scalar.activation(prob[:], left[:], ACT.Exp).then_inc(gate_exp, 1)
                        wait(act, down_full, st.at(lambda u: EXPERTS * u + e - 1))
                        for c in range(FFN_CHUNKS):
                            act.wait_ge(up_full, st.at(lambda u: FFN_CHUNKS * (EXPERTS * u + e) + c + 1))
                            nc.scalar.activation(hidden[:, e % 2, c, :], up_ps[:, c, :], ACT.Relu,
                                                 bias=b1_sb[:, e * FFN_CHUNKS + c:e * FFN_CHUNKS + c + 1]
                                                 ).then_inc(relu_done, 1)
                    if not final:
                        keep_xT(st, 1)

                act.wait_ge(small_kept, 2)
                keep_xT(Step(0), 0)
                group(Step(0), False)
                with act.Fori(0, BATCH - 2) as reg:
                    group(Step(1, 1, reg), False)
                group(Step(BATCH - 1), True)

            @block.vector
            def _(dve):
                norm.on_vector(dve)
                dve.wait_ge(small_full, 1)
                nc.vector.tensor_copy(gate_sb[:], gate_ps[:, 0:EXPERTS]).then_inc(small_kept, 1)
                nc.vector.tensor_copy(b1_sb[:], gate_ps[:, P:P + EXPERTS * FFN_CHUNKS]).then_inc(small_kept, 1)
                dve.wait_ge(small_kept, 2)
                dve.wait_ge(marks, EXPERTS)

                def normalize(st, lead):
                    wait(dve, xT_full, st.at(lambda u: u + lead))
                    x_b = tokens(x_sb, st.at(lambda u: TILES * (u + lead)))
                    mean = tokens(mv_all, st.at(lambda u: TILES * (u + lead)))
                    r = tokens(rstd, st.at(lambda u: TILES * (u + lead)))
                    for t in range(TILES):
                        last = nc.vector.tensor_scalar(x_norm[:, t, :], x_b[:, t, :], mean[:, t, 0:1], r[:, t:t + 1],
                                                       ALU.subtract, ALU.mult)
                    last.then_inc(x_normed, 1)

                def spread(v, n=EXPERTS):
                    return v.broadcast_to([P, TILES, n])

                def choose_gates(st):
                    links = [0]

                    def link(instruction):
                        links[0] += 1
                        n = links[0]
                        instruction.then_inc(gate_chain, 1)
                        dve.wait_ge(gate_chain, st.at(lambda u: CHAIN * u + n))

                    logits = gate_ps[:, 0:TILES * EXPERTS].rearrange("p (t e) -> p t e", e=EXPERTS)
                    wins = first_wins[:].rearrange("p (o e) -> p o e", o=1).broadcast_to([P, TILES, EXPERTS])
                    dve.wait_ge(logits_full, st.at(lambda u: u + 1))
                    link(nc.vector.reduce_max(top[:, :, 0], logits, AX.X))
                    nc.vector.tensor_tensor(left[:], logits, spread(top[:]), ALU.subtract).then_inc(logits_less, 1)
                    dve.wait_ge(gate_exp, st.at(lambda u: u + 1))
                    link(nc.vector.reduce_sum(top[:, :, 0], prob[:], AX.X))
                    link(nc.vector.reciprocal(top[:], top[:]))
                    link(nc.vector.tensor_tensor(prob[:], prob[:], spread(top[:]), ALU.mult))
                    for i, p in enumerate((prob, left)):
                        if i:
                            link(nc.vector.scalar_tensor_tensor(left[:], pick[0][:], -4.0, prob[:], ALU.mult, ALU.add))
                        link(nc.vector.reduce_max(top[:, :, 0], p[:], AX.X))
                        link(nc.vector.tensor_tensor(key[:], p[:], spread(top[:]), ALU.is_equal))
                        link(nc.vector.tensor_tensor(key[:], key[:], wins, ALU.mult))
                        link(nc.vector.reduce_max(top[:, :, 0], key[:], AX.X))
                        if i == 0:
                            link(nc.vector.tensor_tensor(pick[i][:], key[:], spread(top[:]), ALU.is_equal))
                        else:
                            nc.vector.tensor_tensor(pick[i][:], key[:], spread(top[:]),
                                                    ALU.is_equal).then_inc(pick_chain, 1)
                            dve.wait_ge(pick_chain, st.at(lambda u: 2 * u + 1))
                    assert links[0] == CHAIN, links
                    nc.vector.tensor_tensor(pick[0][:], pick[0][:], pick[1][:], ALU.add).then_inc(pick_chain, 1)
                    dve.wait_ge(pick_chain, st.at(lambda u: 2 * u + 2))
                    nc.vector.tensor_tensor(gates[:], pick[0][:], prob[:], ALU.mult).then_inc(gates_ready, 1)
                    dve.wait_ge(gates_ready, st.at(lambda u: u + 1))

                def group(st, final):
                    choose_gates(st)
                    if not final:
                        normalize(st, 1)
                    dve.wait_ge(gatesT_full, st.at(lambda u: u + 1))
                    nc.vector.tensor_copy(gatesT[:], gate_ps[0:EXPERTS, :]).then_inc(gatesT_kept, 1)
                    x_b = tokens(x_sb, st.at(lambda u: TILES * u))
                    dve.wait_ge(b2_full, st.at(lambda u: u + 1))
                    nc.vector.tensor_tensor(acc[:], x_b, gate_ps[:].rearrange("p (t e) -> p t e", e=EMBD),
                                            ALU.add).then_inc(acc_init, 1)
                    dve.wait_ge(acc_init, st.at(lambda u: u + 1))
                    for e in range(EXPERTS):
                        dve.wait_ge(down_full, st.at(lambda u: EXPERTS * u + e + 1))
                        for t in range(TILES):
                            if e:
                                dve.wait_ge(acc_step, st.at(lambda u: TILES * (EXPERTS * u + e - 1) + t + 1))
                            nc.vector.scalar_tensor_tensor(acc[:, t, :], down_ps[:, e % 2, t * P:(t + 1) * P],
                                                           gates[:, t, e:e + 1], acc[:, t, :], ALU.mult,
                                                           ALU.add).then_inc(acc_step, 1)
                    wait_apart(dve, acc_step, st.at(lambda u: TILES * EXPERTS * (u + 1)), passed)
                    nc.vector.tensor_copy(x_b, acc[:]).then_inc(x_kept, 1)
                    if out_dram is None:
                        for t in range(TILES):
                            last = nc.vector.bn_stats(stats[:, t, :], acc[:, t, :])
                        last.then_inc(stats_ready, 1)
                        wait_apart(dve, stats_ready, st.at(lambda u: u + 1), passed)
                        for t in range(TILES):
                            last = nc.vector.bn_aggr(mv[:, t, :], stats[:, t, :])
                        last.then_inc(mv_ready, 1)
                        wait_apart(dve, mv_ready, st.at(lambda u: u + 1), passed)
                        nc.vector.tensor_copy(tokens(mv_all, st.at(lambda u: TILES * u)), mv[:]).then_inc(mv_kept, 1)
                        dve.wait_ge(mv_kept, st.at(lambda u: u + 1))
                    dve.wait_ge(x_kept, st.at(lambda u: u + 1))

                normalize(Step(0), 0)
                groups(dve, group)


def hybrid(nc, x, wq, bq, wk, bk, wv, bv, wo, bo, rel_bias, wqkv, bqkv, wout, bout, gate_w, w1, b1, w2, b2, out):
    sems = Sems(nc)
    with ExitStack() as ctx:
        x_sb = ctx.enter_context(nc.sbuf_tensor("x_sb", [P, BATCH * TILES, EMBD], F32))
        mv_all = ctx.enter_context(nc.sbuf_tensor("mv_all", [P, BATCH * TILES, 2], F32))
        rstd = ctx.enter_context(nc.sbuf_tensor("rstd", [P, BATCH * TILES], F32))
        ident = ctx.enter_context(nc.sbuf_tensor("ident", [P, P], F32))

        def column(v):
            return v.rearrange("(e o) -> e o", o=1)

        def rows(v):
            return v.partition_broadcast(P)

        def by_head(v, which):
            part = slice(which * HEAD_DIM, (which + 1) * HEAD_DIM)
            if len(v.shape) == 2:
                return v.rearrange("e (h c) -> e h c", h=HEADS)[:, :, part]
            return v.rearrange("(h c) -> h c", h=HEADS)[:, part]

        load_phase(nc, sems, x, x_sb, mv_all, ident)
        sems.clear()
        attention_phase(nc, sems, "aa_", x_sb, mv_all, rstd, ident,
                        dict(wq=wq, wk=wk, wv=wv, wo=wo, bq=column(bq), bk=column(bk), bv=rows(bv), bo=rows(bo)),
                        rel_bias)
        sems.clear()
        ffn_phase(nc, sems, "f1_", x_sb, mv_all, rstd, ident, gate_w, w1, b1, w2, b2, None)
        sems.clear()
        with nc.allow_non_contiguous_dma("q and k biases, one value per partition"):
            attention_phase(nc, sems, "ab_", x_sb, mv_all, rstd, ident,
                            dict(wq=by_head(wqkv, 0), wk=by_head(wqkv, 1), wv=by_head(wqkv, 2), wo=wout,
                                 bq=by_head(bqkv, 0), bk=by_head(bqkv, 1), bv=rows(by_head(bqkv, 2)), bo=rows(bout)),
                            None)
        sems.clear()
        ffn_phase(nc, sems, "f2_", x_sb, mv_all, rstd, ident, gate_w, w1, b1, w2, b2, out)
        sems.clear()


_INS = ["L0_attn_a_hidden_states", "L0_attn_a_Wq", "L0_attn_a_bq", "L0_attn_a_Wk", "L0_attn_a_bk", "L0_attn_a_Wv",
        "L0_attn_a_bv", "L0_attn_a_Wo", "L0_attn_a_bo", "L0_attn_a_rel_bias", "L0_attn_b_Wqkv", "L0_attn_b_bqkv",
        "L0_attn_b_Wout", "L0_attn_b_bout", "L0_ffn_gate_w", "L0_ffn_w1", "L0_ffn_b1", "L0_ffn_w2", "L0_ffn_b2"]


def kernel(**inputs):
    import numpy as _np
    import concourse.bacc as _bacc
    from concourse import mybir as _mybir
    from concourse.bass_utils import run_bass_kernel_spmd as _run

    nc = _bacc.Bacc("TRN2", target_bir_lowering=False, num_devices=1)
    arrays, args = {}, []
    for name in _INS:
        a = _np.ascontiguousarray(inputs[name])
        arrays[f"in_{name}"] = a
        args.append(nc.dram_tensor(f"in_{name}", a.shape, _mybir.dt.from_np(a.dtype), kind="ExternalInput").ap())
    out = nc.dram_tensor("out_0", (BATCH, SEQ, EMBD), _mybir.dt.from_np(_np.dtype("float32")),
                         kind="ExternalOutput").ap()
    hybrid(nc, *args, out)
    r = _run(nc, [arrays], core_ids=[0])
    return r.results[0]["out_0"]
```

```python
import concourse.bass as bass
from concourse import mybir
from contextlib import ExitStack
import numpy as np

F32 = mybir.dt.float32
BF16 = mybir.dt.bfloat16
I32 = mybir.dt.int32
ALU = mybir.AluOpType
ACT = mybir.ActivationFunctionType
AX = mybir.AxisListType

BATCH, SEQ, EMBD = 16, 512, 128
P = 128
TILES = SEQ // P
HEADS, HEAD_DIM = 16, 8
GROUPS, GROUP = 4, 4
EXPERTS, FFN_DIM = 8, 512
FFN_CHUNKS = FFN_DIM // P
BUCKETS, MAX_DISTANCE = 32, 64
LN_EPS = 1e-5
PARTS = 3
PROD_ROWS = PARTS * PARTS * HEAD_DIM
CONST_ROW = PROD_ROWS
MAX_ROW = 96
A_ROWS = MAX_ROW
B_ROWS = MAX_ROW + PARTS
BAND = P + MAX_DISTANCE
CHUNK_TILES = 16
CHUNKS = BATCH * TILES // CHUNK_TILES
SLOT_TILES = (2 * CHUNK_TILES * P - EXPERTS) // P + EXPERTS
RING = 4
AHEAD = 5
LOADS = 4
ONES_WORD = float(np.array([0x3F803F80], np.uint32).view(np.float32)[0])
V_COLS = HEAD_DIM + 1


class Step:

    def __init__(self, first, stride=0, reg=None):
        self.first, self.stride, self.reg = first, stride, reg

    def at(self, count):
        base = count(self.first)
        if self.reg is None:
            return base
        rate = count(self.first + self.stride) - base
        return base + rate * self.reg


def wait(eng, sem, value):
    if isinstance(value, int) and value <= 0:
        return
    eng.wait_ge(sem, value)


class Sems:

    def __init__(self, nc):
        self.nc, self.held = nc, []

    def new(self, name):
        self.held.append(self.nc.alloc_semaphore(name))
        return self.held[-1]

    def clear(self):
        self.nc.clear_and_free_semaphores(self.held)
        self.nc.all_engine_barrier()
        self.held = []


def wait_apart(eng, sem, value, passed):
    eng.wait_ge(sem, value)
    eng.sem_inc(passed, 1)


def bias_buckets(limit):
    d = np.arange(limit)
    exact = BUCKETS // 2
    far = np.maximum(d, 1).astype(np.float32)
    large = exact + (np.log(far / np.float32(exact)) / np.float32(np.log(MAX_DISTANCE / exact))
                     * np.float32(BUCKETS - exact)).astype(np.int32)
    return np.where(d < exact, d, np.minimum(large, BUCKETS - 1))


def tokens(x, first):
    if isinstance(first, int):
        return x[:, first:first + TILES]
    return x[:, bass.ds(first, TILES)]


def words(stack):
    return stack.rearrange("p h q -> p (h q)").bitcast(F32)


def load_phase(nc, sems, x_dram, x_sb, mv_all, ident, sorted_dram):
    with ExitStack() as ctx:
        stats = ctx.enter_context(nc.sbuf_tensor("ld_stats", [P, BATCH * TILES, 6], F32))
        x_loaded = [sems.new(f"ld_x_loaded{i}") for i in range(LOADS)]
        stats_done = sems.new("ld_stats_done")
        zeros = ctx.enter_context(nc.sbuf_tensor("ld_zeros", [P, SLOT_TILES, EMBD], F32))
        zeroed = sems.new("ld_zeroed")
        zeros_stored = sems.new("ld_zeros_stored")
        ident_done = sems.new("ld_ident_done")
        x_tiles = x_dram.rearrange("b (t p) e -> p (b t) e", p=P)
        with nc.Block() as block:
            @block.sync
            def _(sp):
                n = BATCH * TILES // LOADS
                for i in range(LOADS):
                    sp.dma_start(x_sb[:, i * n:(i + 1) * n, :], x_tiles[:, i * n:(i + 1) * n, :]
                                 ).then_inc(x_loaded[i], 16)
                sp.wait_ge(zeroed, 1)
                for dram in sorted_dram:
                    sp.dma_start(dram.rearrange("(s p) e -> p s e", p=P), zeros[:]).then_inc(zeros_stored, 16)
                sp.wait_ge(zeros_stored, 32)

            @block.gpsimd
            def _(pool):
                nc.gpsimd.memset(zeros[:], 0.0).then_inc(zeroed, 1)
                nc.gpsimd.memset(ident[:], 0.0).then_inc(zeroed, 1)
                pool.wait_ge(zeroed, 2)
                nc.gpsimd.affine_select(out=ident[:], in_=ident[:], compare_op=ALU.not_equal, fill=1.0, base=0,
                                        pattern=[[-1, P]], channel_multiplier=1).then_inc(ident_done, 1)
                pool.wait_ge(ident_done, 1)

            @block.vector
            def _(dve):
                for i in range(LOADS):
                    dve.wait_ge(x_loaded[i], 16)
                    piece = range(i * BATCH * TILES // LOADS, (i + 1) * BATCH * TILES // LOADS)
                    for n in piece:
                        last = nc.vector.bn_stats(stats[:, n, :], x_sb[:, n, :])
                    last.then_inc(stats_done, 1)
                    dve.wait_ge(stats_done, i + 1)
                    for n in piece:
                        nc.vector.bn_aggr(mv_all[:, n, :], stats[:, n, :])


class Norm:

    def __init__(self, nc, sems, ctx, tag, mv_all, rstd):
        self.nc, self.mv_all, self.rstd = nc, mv_all, rstd
        self.var = ctx.enter_context(nc.sbuf_tensor(tag + "_var", [P, BATCH * TILES], F32))
        self.root = ctx.enter_context(nc.sbuf_tensor(tag + "_root", [P, BATCH * TILES], F32))
        self.var_ready = sems.new(tag + "_var_ready")
        self.root_ready = sems.new(tag + "_root_ready")
        self.chain = sems.new(tag + "_rstd_chain")

    def on_scalar(self, act):
        act.wait_ge(self.var_ready, 1)
        self.nc.scalar.activation(self.root[:], self.var[:], ACT.Sqrt).then_inc(self.root_ready, 1)

    def on_vector(self, dve):
        nc, var, root, rstd = self.nc, self.var, self.root, self.rstd
        nc.vector.tensor_scalar(var[:], self.mv_all[:, :, 1], LN_EPS, None, ALU.add).then_inc(self.var_ready, 1)
        dve.wait_ge(self.root_ready, 1)
        nc.vector.reciprocal(rstd[:], root[:]).then_inc(self.chain, 1)
        dve.wait_ge(self.chain, 1)
        nc.vector.tensor_tensor(root[:], rstd[:], rstd[:], ALU.mult).then_inc(self.chain, 1)
        dve.wait_ge(self.chain, 2)
        nc.vector.tensor_tensor(root[:], root[:], var[:], ALU.mult).then_inc(self.chain, 1)
        dve.wait_ge(self.chain, 3)
        nc.vector.tensor_scalar(root[:], root[:], -0.5, 1.5, ALU.mult, ALU.add).then_inc(self.chain, 1)
        dve.wait_ge(self.chain, 4)
        nc.vector.tensor_tensor(rstd[:], rstd[:], root[:], ALU.mult).then_inc(self.chain, 1)
        dve.wait_ge(self.chain, 5)


STAGE_LAG = {"front": 2, "A": 1, "B": 0, "tail": -1}
SLOTS = HEADS
SPARE_USES = [
    (1, "xT", "front"), (2, "max_hi", "B"), (3, "q", "front"), (4, "heads2", "tail"), (5, "k", "front"),
    (6, "heads3", "tail"), (7, "v", "front"), (8, "outT", "tail"), (9, "max_lo", "A"), (10, "y", "tail"),
    (12, "heads0", "B"), (14, "heads1", "B"),
]
SCALAR_SIDE = [
    (2, 1, "xT", "front"), (4, 1, "q", "front"), (4, 3, "q_high", "front"), (5, 3, "q_mid", "front"),
    (6, 1, "k", "front"), (6, 3, "k_high", "front"), (8, 1, "k_mid", "front"), (9, 1, "outT", "tail"),
]
VECTOR_SIDE = [
    (0, 0, "normalize", "front"), (2, 1, "max_hi.0", "B"), (3, 0, "max_hi.1", "B"), (3, 1, "max_hi.2", "B"),
    (4, 0, "max_hi.3", "B"), (4, 1, "heads2.0", "tail"), (5, 0, "heads2.1", "tail"), (6, 0, "v_aug", "A"),
    (6, 1, "heads3.0", "tail"), (7, 0, "heads3.1", "tail"), (7, 1, "v", "front"), (9, 1, "max_lo.0", "A"),
    (10, 0, "max_lo.1", "A"), (10, 1, "max_lo.2", "A"), (11, 0, "max_lo.3", "A"), (11, 1, "y.0", "tail"),
    (12, 0, "y.1", "tail"), (12, 1, "heads0.0", "B"), (13, 0, "heads0.1", "B"), (13, 1, "y.2", "tail"),
    (14, 0, "y.3", "tail"), (14, 1, "heads1.0", "B"), (15, 0, "heads1.1", "B"), (15, 1, "y.4", "tail"),
]
REST_SLOTS = {5: 0, 7: 1}
LAST_PART_SLOTS = {6: 0, 8: 1}


def active(stage, s):
    return 0 <= s + STAGE_LAG[stage] < BATCH


def spare_before(s):
    return sum(active(u[2], n) for n in range(-2, s) for u in SPARE_USES)


def spare_index(what):
    def count(s):
        n = spare_before(s)
        for _, name, stage in SPARE_USES:
            n += active(stage, s)
            if name == what:
                return n
    return count


def attention_phase(nc, sems, tag, x_sb, mv_all, rstd, ident, w_dram, rel_bias):
    scale = float(1.0 / np.sqrt(HEAD_DIM))
    biased = rel_bias is not None
    with ExitStack() as ctx:
        def sb(name, shape, dt=F32):
            return ctx.enter_context(nc.sbuf_tensor(tag + name, shape, dt))

        def sem(name):
            return sems.new(tag + name)

        norm = Norm(nc, sems, ctx, tag, mv_all, rstd)
        w_sb = sb("w", [P, 4, EMBD])
        qk_bias = sb("qk_bias", [P, 2])
        bv_rows = sb("bv_rows", [P, EMBD])
        bo_rows = sb("bo_rows", [P, EMBD])
        x_norm = sb("x_norm", [P, TILES, EMBD])
        x_normT = sb("x_normT", [P, SEQ])
        proj = sb("proj", [P, SEQ])
        rest = sb("rest", [P, SEQ])
        parts = [sb("q_parts", [P, PARTS, SEQ], BF16), sb("k_parts", [P, PARTS, SEQ], BF16)]
        v_stage = sb("v_stage", [P, TILES, HEADS, V_COLS])
        v_aug = [sb(f"v_aug{i}", [P, TILES, HEADS, V_COLS]) for i in range(2)]
        q_stack = [sb(f"q_stack{i}", [P, HEADS, SEQ], BF16) for i in range(2)]
        k_stack = [sb(f"k_stack{i}", [P, HEADS, SEQ], BF16) for i in range(2)]
        row_max = sb("row_max", [P, HEADS * TILES])
        max_rest = sb("max_rest", [HEADS * TILES // 2, P])
        max_parts = sb("max_parts", [HEADS * TILES // 2, PARTS, P], BF16)
        probs = sb("probs", [P, 2 * GROUP, TILES, SEQ])
        heads_raw = [sb(f"heads_raw{i}", [P, SEQ]) for i in range(2)]
        recip = sb("recip", [P, TILES, GROUP, 1])
        heads_out = sb("heads_out", [P, TILES, EMBD])
        heads_outT = sb("heads_outT", [P, SEQ])
        stats = sb("stats", [P, TILES, 6])
        mv = sb("mv", [P, TILES, 2])
        band = sb("band", [P, HEADS, BAND]) if biased else None
        a_ps = ctx.enter_context(nc.psum_tensor(tag + "a_ps", [P, TILES, SEQ], F32))
        b_ps = ctx.enter_context(nc.psum_tensor(tag + "b_ps", [P, 2, SEQ], F32))
        o_ps = ctx.enter_context(nc.psum_tensor(tag + "o_ps", [P, SEQ], F32))
        spare = ctx.enter_context(nc.psum_tensor(tag + "spare", [P, SEQ], F32))
        parts_dram = [nc.dram_tensor(f"{tag}parts_{n}", (EMBD, PARTS, SEQ), BF16, kind="Internal").ap() for n in "qk"]

        weights_loaded = sem("weights_loaded")
        filled = sem("filled")
        if biased:
            setup_bias(nc, sems, tag, probs, heads_outT, heads_raw, q_stack, k_stack, band, rel_bias, spare)
        with nc.Block() as block:
            @block.sync
            def _(sp):
                for i, n in enumerate(("wq", "wk", "wv", "wo")):
                    dst = w_sb[:, i, :]
                    if len(w_dram[n].shape) == 3:
                        dst = dst.rearrange("p (h d) -> p h d", d=HEAD_DIM)
                    sp.dma_start(dst, w_dram[n]).then_inc(weights_loaded, 16)
                for i, n in enumerate(("bq", "bk")):
                    sp.dma_start(qk_bias[:, i:i + 1], w_dram[n]).then_inc(weights_loaded, 16)
                bv_dst = bv_rows[:]
                if len(w_dram["bv"].shape) == 3:
                    bv_dst = bv_dst.rearrange("p (h d) -> p h d", d=HEAD_DIM)
                sp.dma_start(bv_dst, w_dram["bv"]).then_inc(weights_loaded, 16)
                sp.dma_start(bo_rows[:], w_dram["bo"]).then_inc(weights_loaded, 16)
                sp.wait_ge(weights_loaded, 16 * 8)

            @block.gpsimd
            def _(pool):
                if not biased:
                    for i in range(2):
                        nc.gpsimd.memset(words(k_stack[i][64:MAX_ROW]), 0.0).then_inc(filled, 1)
                        pool.wait_ge(filled, i + 1)
                nc.gpsimd.memset(words(k_stack[1][MAX_ROW:B_ROWS]), ONES_WORD)

            @block.scalar
            def _(act):
                norm.on_scalar(act)

            @block.vector
            def _(dve):
                norm.on_vector(dve)
                if not biased:
                    for i in range(2):
                        nc.vector.memset(words(q_stack[i][64:MAX_ROW]), 0.0)
                nc.vector.memset(o_ps[:], 0.0)
                nc.vector.memset(v_stage[:, :, :, HEAD_DIM:V_COLS], 1.0)
                nc.vector.memset(words(k_stack[0][MAX_ROW:B_ROWS]), ONES_WORD)
                dve.wait_ge(weights_loaded, 16 * 8)
                nc.vector.tensor_scalar(qk_bias[:, 0:1], qk_bias[:, 0:1], scale, None, ALU.mult)

        x_normed = sem("x_normed")
        spare_full = sem("spare_full")
        spare_free = sem("spare_free")
        high_ready = sem("high_ready")
        rest_ready = sem("rest_ready")
        mid_ready = sem("mid_ready")
        parts_ready = sem("parts_ready")
        parts_stored = sem("parts_stored")
        stack_loaded = [sem(f"stack_loaded{i}") for i in range(2)]
        v_ready = sem("v_ready")
        a_full = sem("a_full")
        max_taken = sem("max_taken")
        max_chain = sem("max_chain")
        max_stored = [sem(f"max_stored{i}") for i in range(2)]
        b_full = sem("b_full")
        exp_done = sem("exp_done")
        band_done = sem("band_done")
        pv_done = sem("pv_done")
        heads_kept = sem("heads_kept")
        recip_ready = sem("recip_ready")
        x_added = sem("x_added")
        stats_ready = sem("stats_ready")
        mv_ready = sem("mv_ready")
        mv_kept = sem("mv_kept")
        passed = sem("passed")

        band_rate = 1 if biased else 0
        per_half = PARTS + PARTS * PARTS
        half = HEADS // 2
        PAIRS = HEADS * TILES // 2

        def steps(eng, step, unrolled=2):
            for s in (-2, -1, 0):
                step(Step(s), s % 2, lambda stage, s=s: active(stage, s))
            with eng.Fori(0, (BATCH - 4) // unrolled) as reg:
                for i in range(unrolled):
                    step(Step(1 + i, unrolled, reg), (1 + i) % 2, lambda stage: True)
            for s in range(BATCH - 3, BATCH + 1):
                step(Step(s), s % 2, lambda stage, s=s: active(stage, s))

        with nc.Block() as block:
            @block.sync
            def _(sp):
                def load_stacks(which, h):
                    for i in range(PARTS):
                        row = i * PARTS * HEAD_DIM
                        rows = slice(row, row + PARTS * HEAD_DIM)
                        heads = slice(h * half, (h + 1) * half)
                        k_rows = parts_dram[1].rearrange("(h d) j n -> (d j) h n", d=HEAD_DIM)
                        q_rows = parts_dram[0].rearrange("(h d) j n -> d j h n", d=HEAD_DIM)
                        sp.dma_start(k_stack[which][rows, heads, :], k_rows[:, heads, :]).then_inc(stack_loaded[h], 16)
                        for j in range(PARTS):
                            dst = q_stack[which][row + j:row + j + PARTS * (HEAD_DIM - 1) + 1:PARTS, heads, :]
                            sp.dma_start(dst, q_rows[:, i, heads, :]).then_inc(stack_loaded[h], 16)

                def store_max(which, h, count):
                    sp.wait_ge(max_chain, count)
                    for i in range(PARTS):
                        sp.dma_start(q_stack[which][MAX_ROW + i:MAX_ROW + i + 1, h * half:(h + 1) * half, :],
                                     max_parts[:, i, :]).then_inc(max_stored[h], 16)

                def step(st, par, on):
                    if on("A"):
                        wait(sp, b_full, st.at(lambda s: HEADS * TILES * s))
                        load_stacks(1 - par, 1)
                    if on("B"):
                        store_max(par, 1, st.at(lambda s: 6 * s + 6))
                    if on("A"):
                        wait_apart(sp, stack_loaded[1], st.at(lambda s: 16 * per_half * (s + 2)), passed)
                    if on("front"):
                        for i in range(2):
                            sp.wait_ge(parts_ready, st.at(lambda s: 2 * (s + 2) + i + 1))
                            sp.dma_start(parts_dram[i], parts[i][:]).then_inc(parts_stored, 16)
                        wait_apart(sp, parts_stored, st.at(lambda s: 32 * (s + 3)), passed)
                        wait(sp, b_full, st.at(lambda s: HEADS * TILES * s + half * TILES))
                        load_stacks(par, 0)
                    if on("A"):
                        store_max(1 - par, 0, st.at(lambda s: 6 * (s + 1) + 3))
                    if on("front"):
                        wait_apart(sp, stack_loaded[0], st.at(lambda s: 16 * per_half * (s + 3)), passed)

                steps(sp, step)
                for h in range(2):
                    sp.wait_ge(stack_loaded[h], 16 * per_half * BATCH)
                    sp.wait_ge(max_stored[h], 16 * PARTS * BATCH)

            @block.tensor
            def _(pe):
                def use_spare(st, what):
                    wait(pe, spare_free, st.at(lambda s: spare_index(what)(s) - 1))

                def transposes(out, src, rows):
                    for t in range(TILES):
                        last = nc.tensor.transpose(out[0:rows, t * P:(t + 1) * P], src(t), ident[:])
                    return last

                def spare_use(st, what, par):
                    if what in ("max_lo", "max_hi"):
                        if what == "max_lo":
                            pe.wait_ge(max_taken, st.at(lambda s: PAIRS * (s + 1) + PAIRS // 2))
                            src = row_max[:, 0:half * TILES]
                        else:
                            pe.wait_ge(max_taken, st.at(lambda s: PAIRS * (s + 1)))
                            src = row_max[:, half * TILES:HEADS * TILES]
                        use_spare(st, what)
                        last = nc.tensor.transpose(spare[0:half * TILES, 0:P], src, ident[:])
                    elif what == "xT":
                        pe.wait_ge(x_normed, st.at(lambda s: s + 3))
                        use_spare(st, what)
                        last = transposes(spare, lambda t: x_norm[:, t, :], P)
                    elif what in ("q", "k", "v"):
                        use_spare(st, what)
                        if what == "v":
                            for t in range(TILES):
                                last = nc.tensor.matmul(spare[:, t * P:(t + 1) * P], x_normT[:, t * P:(t + 1) * P],
                                                        w_sb[:, 2, :], start=True, stop=True)
                        else:
                            last = nc.tensor.matmul(spare[:], w_sb[:, "qk".index(what), :], x_normT[:],
                                                    start=True, stop=True)
                    elif what[:-1] == "heads":
                        g = int(what[-1])
                        batch_of = (lambda s: s - 1) if g >= 2 else (lambda s: s)
                        pe.wait_ge(heads_kept, st.at(lambda s: GROUPS * batch_of(s) + g + 1))
                        use_spare(st, what)
                        last = transposes(spare, lambda t: heads_raw[g % 2][:, t * P:(t + 1) * P], P)
                    elif what == "outT":
                        use_spare(st, what)
                        last = transposes(spare, lambda t: heads_out[:, t, :], P)
                    elif what == "y":
                        use_spare(st, what)
                        for t in range(TILES):
                            last = nc.tensor.matmul(spare[:, t * P:(t + 1) * P], heads_outT[:, t * P:(t + 1) * P],
                                                    w_sb[:, 3, :], start=True, stop=True)
                    last.then_inc(spare_full, 1)

                def value_products(st, par, on, slot):
                    g, c = slot // GROUP - 1, slot % GROUP
                    if not (on("B") if g >= 0 else on("tail")):
                        return
                    g, lag, which = (g, 0, par) if g >= 0 else (GROUPS - 1, 1, 1 - par)
                    if c == 0:
                        if biased:
                            pe.wait_ge(band_done, st.at(lambda s: HEADS * (s - lag) + GROUP * (g + 1)))
                        else:
                            pe.wait_ge(exp_done, st.at(lambda s: TILES * (HEADS * (s - lag) + GROUP * (g + 1))))
                        pe.wait_ge(v_ready, st.at(lambda s: s - lag + 1))
                        wait(pe, heads_kept, st.at(lambda s: GROUPS * (s - lag) + g))
                    for j in range(GROUP):
                        h = GROUP * g + j
                        last = nc.tensor.matmul(o_ps[32 * j:32 * j + V_COLS, :], v_aug[which][:, c, h, :],
                                                probs[:, h % (2 * GROUP), c, :],
                                                start=(c == 0), stop=(c == TILES - 1))
                    last.then_inc(pv_done, 1)

                def step(st, par, on):
                    for slot in range(SLOTS):
                        if on("A") and slot % half == 0:
                            pe.wait_ge(stack_loaded[slot // half], st.at(lambda s: 16 * per_half * (s + 2)))
                        if on("B") and slot % half == 0:
                            pe.wait_ge(max_stored[slot // half], st.at(lambda s: 16 * PARTS * (s + 1)))
                        for c in range(TILES):
                            if on("A"):
                                if c % 2 == 0:
                                    wait(pe, max_taken, st.at(lambda s: PAIRS * (s + 1) + 2 * slot + c // 2 - 1))
                                last = nc.tensor.matmul(a_ps[:, c, :],
                                                        q_stack[1 - par][0:A_ROWS, slot, c * P:(c + 1) * P],
                                                        k_stack[1 - par][0:A_ROWS, slot, :], start=True, stop=True)
                                if c % 2 == 1:
                                    last.then_inc(a_full, 1)
                            if on("B"):
                                wait(pe, exp_done, st.at(lambda s: HEADS * TILES * s + TILES * slot + c - 1))
                                nc.tensor.matmul(b_ps[:, c % 2, :],
                                                 k_stack[par][0:B_ROWS, slot, c * P:(c + 1) * P],
                                                 q_stack[par][0:B_ROWS, slot, :],
                                                 start=True, stop=True).then_inc(b_full, 1)
                            if c == (TILES - 1 if slot % GROUP == 0 else 1):
                                value_products(st, par, on, slot)
                        for at, what, stage in SPARE_USES:
                            if at == slot and on(stage):
                                spare_use(st, what, par)

                steps(pe, step)

            @block.scalar
            def _(act):
                def split_high(st, i):
                    act.wait_ge(spare_free, st.at(spare_index("qk"[i])))
                    wait(act, parts_stored, st.at(lambda s: 32 * (s + 2)))
                    nc.scalar.activation(parts[i][:, 0, :], proj[:], ACT.Copy).then_inc(high_ready, 1)

                def split_mid(st, i):
                    n = lambda s: 2 * (s + 2) + i + 1
                    act.wait_ge(rest_ready, st.at(n))
                    nc.scalar.activation(parts[i][:, 1, :], rest[:], ACT.Copy).then_inc(mid_ready, 1)

                def spare_read(st, what):
                    if what == "xT":
                        act.wait_ge(spare_full, st.at(spare_index(what)))
                        nc.scalar.copy(x_normT[:], spare[:]).then_inc(spare_free, 1)
                    elif what in ("q", "k"):
                        i = "qk".index(what)
                        wait(act, rest_ready, st.at(lambda s: 2 * (s + 2) + i))
                        act.wait_ge(spare_full, st.at(spare_index(what)))
                        nc.scalar.activation(proj[:], spare[:], ACT.Identity, bias=qk_bias[:, i:i + 1],
                                             scale=(scale, 1.0)[i]).then_inc(spare_free, 1)
                    elif what == "outT":
                        act.wait_ge(spare_full, st.at(spare_index(what)))
                        nc.scalar.copy(heads_outT[:], spare[:]).then_inc(spare_free, 1)

                def side(st, what):
                    if what[1:] == "_high":
                        split_high(st, "qk".index(what[0]))
                    elif what[1:] == "_mid":
                        split_mid(st, "qk".index(what[0]))
                    else:
                        spare_read(st, what)

                def keep_heads(st, g, lag):
                    act.wait_ge(pv_done, st.at(lambda s: HEADS * (s - lag) + GROUP * (g + 1)))
                    before = ("heads2", "heads3", "heads0", "heads1")[g]
                    wait(act, spare_full, st.at(lambda s: spare_index(before)(s - lag)))
                    nc.scalar.copy(heads_raw[g % 2][:], o_ps[:]).then_inc(heads_kept, 1)

                def step(st, par, on):
                    for slot in range(SLOTS):
                        g = slot // GROUP - 2
                        if slot % GROUP == 0:
                            if g >= 0 and on("B"):
                                keep_heads(st, g, 0)
                            if g < 0 and on("tail"):
                                keep_heads(st, g + GROUPS, 1)
                        if on("B"):
                            wait(act, pv_done, st.at(lambda s: HEADS * s + GROUP * (slot // GROUP) - GROUP))
                        for c in range(TILES):
                            if on("B"):
                                act.wait_ge(b_full, st.at(lambda s: HEADS * TILES * s + TILES * slot + c + 1))
                                nc.scalar.activation(probs[:, slot % (2 * GROUP), c, :], b_ps[:, c % 2, :],
                                                     ACT.Exp).then_inc(exp_done, 1)
                            for at, tile, what, stage in SCALAR_SIDE:
                                if (at, tile) == (slot, c) and on(stage):
                                    side(st, what)

                steps(act, step)

            @block.gpsimd
            def _(pool):
                def rests(st, i):
                    n = lambda s: 2 * (s + 2) + i + 1
                    wait(pool, parts_ready, st.at(lambda s: 2 * (s + 2) + i))
                    pool.wait_ge(high_ready, st.at(n))
                    nc.gpsimd.tensor_tensor(rest[:], proj[:], parts[i][:, 0, :], ALU.subtract).then_inc(rest_ready, 1)

                def last_part(st, i):
                    n = lambda s: 2 * (s + 2) + i + 1
                    pool.wait_ge(mid_ready, st.at(n))
                    nc.gpsimd.tensor_tensor(parts[i][:, 2, :], rest[:], parts[i][:, 1, :],
                                            ALU.subtract).then_inc(parts_ready, 1)

                def step(st, par, on):
                    for slot in range(SLOTS):
                        if on("front") and slot in REST_SLOTS:
                            rests(st, REST_SLOTS[slot])
                        if on("front") and slot in LAST_PART_SLOTS:
                            last_part(st, LAST_PART_SLOTS[slot])
                        if biased and on("B"):
                            pool.wait_ge(exp_done, st.at(lambda s: TILES * (HEADS * s + slot + 1)))
                            flat = probs[:, slot % (2 * GROUP), :, :].rearrange("p c q -> p (c q)")
                            diagonal = SEQ + P
                            first = flat[:, 0:(TILES - 1) * diagonal].rearrange("p (c q) -> p c q", q=diagonal)
                            first = first[:, :, 0:BAND]
                            table = band[:, slot:slot + 1, :].broadcast_to([P, TILES - 1, BAND])
                            nc.gpsimd.tensor_tensor(first, first, table, ALU.mult)
                            final = flat[:, (TILES - 1) * diagonal:(TILES - 1) * diagonal + P]
                            nc.gpsimd.tensor_tensor(final, final, band[:, slot, 0:P],
                                                    ALU.mult).then_inc(band_done, 1)

                steps(pool, step)

            @block.vector
            def _(dve):
                def normalize(st):
                    wait(dve, spare_full, st.at(lambda s: spare_index("xT")(s - 1)))
                    x_b = tokens(x_sb, st.at(lambda s: TILES * (s + 2)))
                    mean = tokens(mv_all, st.at(lambda s: TILES * (s + 2)))
                    r = tokens(rstd, st.at(lambda s: TILES * (s + 2)))
                    for t in range(TILES):
                        last = nc.vector.tensor_scalar(x_norm[:, t, :], x_b[:, t, :], mean[:, t, 0:1], r[:, t:t + 1],
                                                       ALU.subtract, ALU.mult)
                    last.then_inc(x_normed, 1)

                def split_max(st, what, piece):
                    h = 0 if what == "max_lo" else 1
                    batch = (lambda s: s + 1) if h == 0 else (lambda s: s)
                    base = lambda s: 6 * batch(s) + 3 * h
                    scores_max = spare[0:half * TILES, 0:P]
                    if piece == 0:
                        wait(dve, max_stored[1 - h], st.at(lambda s: 16 * PARTS * (s + 1)))
                        dve.wait_ge(spare_full, st.at(spare_index(what)))
                        nc.vector.tensor_scalar(max_parts[:, 0, :], scores_max, -1.0, None,
                                                ALU.mult).then_inc(max_chain, 1)
                    elif piece == 1:
                        dve.wait_ge(max_chain, st.at(lambda s: base(s) + 1))
                        nc.vector.scalar_tensor_tensor(max_rest[:], scores_max, -1.0, max_parts[:, 0, :], ALU.mult,
                                                       ALU.subtract).then_inc(spare_free, 1)
                    elif piece == 2:
                        dve.wait_ge(spare_free, st.at(spare_index(what)))
                        nc.vector.tensor_copy(max_parts[:, 1, :], max_rest[:]).then_inc(max_chain, 1)
                    else:
                        dve.wait_ge(max_chain, st.at(lambda s: base(s) + 2))
                        nc.vector.tensor_tensor(max_parts[:, 2, :], max_rest[:], max_parts[:, 1, :],
                                                ALU.subtract).then_inc(max_chain, 1)

                def stage_values(st):
                    wait(dve, v_ready, st.at(lambda s: s + 2))
                    dve.wait_ge(spare_full, st.at(spare_index("v")))
                    v = spare[:].rearrange("p (t h d) -> p t h d", t=TILES, d=HEAD_DIM)
                    for t in range(TILES):
                        last = nc.vector.tensor_tensor(v_stage[:, t, :, 0:HEAD_DIM], v[:, t],
                                                       bv_rows[:].rearrange("p (h d) -> p h d", d=HEAD_DIM), ALU.add)
                    last.then_inc(spare_free, 1)

                def pass_values(st, par):
                    wait(dve, pv_done, st.at(lambda s: HEADS * s))
                    dve.wait_ge(spare_free, st.at(lambda s: spare_index("v")(s - 1)))
                    nc.vector.tensor_copy(v_aug[1 - par][:], v_stage[:]).then_inc(v_ready, 1)

                def finish_heads(st, what, piece):
                    g = int(what[-1])
                    lag = 1 if g >= 2 else 0
                    rows = spare[:].rearrange("p (t j r) -> p t j r", t=TILES, j=GROUP)
                    if piece == 0:
                        dve.wait_ge(spare_full, st.at(spare_index(what)))
                        nc.vector.reciprocal(recip[:], rows[:, :, :, HEAD_DIM:V_COLS]).then_inc(recip_ready, 1)
                    else:
                        if g == 0:
                            wait(dve, x_added, st.at(lambda s: s))
                        dve.wait_ge(recip_ready, st.at(lambda s: GROUPS * (s - lag) + g + 1))
                        out = heads_out[:, :, 32 * g:32 * g + 32].rearrange("p t (j d) -> p t j d", d=HEAD_DIM)
                        nc.vector.tensor_tensor(out, rows[:, :, :, 0:HEAD_DIM],
                                                recip[:].broadcast_to([P, TILES, GROUP, HEAD_DIM]),
                                                ALU.mult).then_inc(spare_free, 1)

                def add_to_x(st, piece):
                    x_b = tokens(x_sb, st.at(lambda s: TILES * (s - 1)))
                    if piece == 0:
                        dve.wait_ge(spare_full, st.at(spare_index("y")))
                        y = spare[:].rearrange("p (t e) -> p t e", e=EMBD)
                        bo = bo_rows[:].rearrange("p (o e) -> p o e", o=1).broadcast_to([P, TILES, EMBD])
                        nc.vector.tensor_tensor(heads_out[:], y, bo, ALU.add).then_inc(spare_free, 1)
                    elif piece == 1:
                        dve.wait_ge(spare_free, st.at(spare_index("y")))
                        nc.vector.tensor_tensor(x_b, x_b, heads_out[:], ALU.add).then_inc(x_added, 1)
                    elif piece == 2:
                        wait_apart(dve, x_added, st.at(lambda s: s), passed)
                        for t in range(TILES):
                            last = nc.vector.bn_stats(stats[:, t, :], x_b[:, t, :])
                        last.then_inc(stats_ready, 1)
                    elif piece == 3:
                        wait_apart(dve, stats_ready, st.at(lambda s: s), passed)
                        for t in range(TILES):
                            last = nc.vector.bn_aggr(mv[:, t, :], stats[:, t, :])
                        last.then_inc(mv_ready, 1)
                    else:
                        wait_apart(dve, mv_ready, st.at(lambda s: s), passed)
                        nc.vector.tensor_copy(tokens(mv_all, st.at(lambda s: TILES * (s - 1))),
                                              mv[:]).then_inc(mv_kept, 1)

                def side(st, par, what):
                    what, _, piece = what.partition(".")
                    if what == "normalize":
                        normalize(st)
                    elif what in ("max_lo", "max_hi"):
                        split_max(st, what, int(piece))
                    elif what == "v":
                        stage_values(st)
                    elif what == "v_aug":
                        pass_values(st, par)
                    elif what == "y":
                        add_to_x(st, int(piece))
                    else:
                        finish_heads(st, what, int(piece))

                def step(st, par, on):
                    for slot in range(SLOTS):
                        for i in range(2):
                            if on("A"):
                                dve.wait_ge(a_full, st.at(lambda s: PAIRS * (s + 1) + 2 * slot + i + 1))
                                nc.vector.reduce_max(row_max[:, TILES * slot + 2 * i:TILES * slot + 2 * i + 2],
                                                     a_ps[:, 2 * i:2 * i + 2, :], AX.X).then_inc(max_taken, 1)
                            for at, pair, what, stage in VECTOR_SIDE:
                                if (at, pair) == (slot, i) and on(stage):
                                    side(st, par, what)
                    if on("tail"):
                        dve.wait_ge(mv_kept, st.at(lambda s: s))

                steps(dve, step)


def setup_bias(nc, sems, tag, probs, work_a, work_b, q_stack, k_stack, band, rel_bias, spare):
    deltas = P - 1 + BAND
    bucket = bias_buckets(BAND)
    bucket = np.concatenate([np.full(P - 1, bucket[0]), bucket])
    edges = [0] + [i for i in range(1, deltas) if bucket[i] != bucket[i - 1]] + [deltas]
    with ExitStack() as ctx:
        def sb(name, shape, dt=F32):
            return ctx.enter_context(nc.sbuf_tensor(tag + name, shape, dt))

        def sem(name):
            return sems.new(tag + name)

        largest = sb("largest", [HEADS, 1])
        factors = work_a[0:HEADS, 0:deltas]
        by_head = work_b[0][0:HEADS, 0:BUCKETS]
        flip = work_b[1][:, 0:P]
        work = probs[:].rearrange("p a c q -> p (a c q)")
        const = work[0:HEADS, 0:TILES * SEQ].rearrange("p (c q) -> p c q", q=SEQ)
        rest = work[0:HEADS, TILES * SEQ:2 * TILES * SEQ].rearrange("p (c q) -> p c q", q=SEQ)
        const_parts = work[0:HEADS, 2 * TILES * SEQ:2 * TILES * SEQ + PARTS * TILES * SEQ // 2].bitcast(BF16)
        const_parts = const_parts.rearrange("p (i c q) -> p i c q", i=PARTS, q=SEQ)
        flipped = work[:, 8192:8192 + HEADS * BAND]
        tile_is = work[0:TILES, 12288:12288 + HEADS * SEQ // 2].bitcast(BF16).rearrange("p (h q) -> p h q", q=SEQ)
        factors_dram = nc.dram_tensor(tag + "factors_dram", (HEADS, deltas), F32, kind="Internal").ap()
        const_dram = nc.dram_tensor(tag + "const_dram", (HEADS, PARTS * TILES, SEQ), BF16, kind="Internal").ap()

        bias_loaded = sem("bias_loaded")
        chain = sem("bias_chain")
        run_ready = sem("run_ready")
        factors_ready = sem("factors_ready")
        factors_stored = sem("factors_stored")
        flipped_loaded = sem("flipped_loaded")
        const_zeroed = sem("const_zeroed")
        const_ready = sem("const_ready")
        const_stored = sem("const_stored")
        stacks_filled = sem("stacks_filled")
        q_filled = sem("q_filled")
        rows_loaded = sem("rows_loaded")
        flip_steps = sem("flip_steps")
        tiles_marked = sem("tiles_marked")
        band_full = sem("band_full")
        band_kept = sem("band_kept")
        with nc.Block() as block:
            @block.sync
            def _(sp):
                with nc.allow_non_contiguous_dma("a table of 512 values, transposed"):
                    sp.dma_start(by_head, rel_bias.rearrange("b h -> h b")).then_inc(bias_loaded, 16)
                sp.wait_ge(factors_ready, 1)
                sp.dma_start(factors_dram, factors).then_inc(factors_stored, 16)
                sp.wait_ge(factors_stored, 16)
                windows = bass.AP(tensor=factors_dram.tensor, offset=factors_dram.offset,
                                  ap=[[1, P], [deltas, HEADS], [1, BAND]])
                sp.dma_start(flipped.rearrange("p (h q) -> p h q", q=BAND), windows).then_inc(flipped_loaded, 16)
                sp.wait_ge(const_ready, 1)
                sp.dma_start(const_dram.rearrange("h r q -> h (r q)"),
                             const_parts.rearrange("p i c q -> p (i c q)")).then_inc(const_stored, 16)
                sp.wait_ge(const_stored, 16)
                sp.wait_ge(stacks_filled, 2)
                sp.wait_ge(q_filled, 2)
                sp.wait_ge(tiles_marked, 2)
                for which in range(2):
                    sp.dma_start(q_stack[which][CONST_ROW:CONST_ROW + PARTS * TILES, :, :],
                                 const_dram.rearrange("h r q -> r h q")).then_inc(rows_loaded, 16)
                    for i in range(PARTS):
                        row = CONST_ROW + i * TILES
                        sp.dma_start(k_stack[which][row:row + TILES, :, :], tile_is).then_inc(rows_loaded, 16)
                sp.wait_ge(rows_loaded, 16 * 2 * (1 + PARTS))

            @block.gpsimd
            def _(pool):
                for i in range(2):
                    nc.gpsimd.memset(words(k_stack[i][64:MAX_ROW]), 0.0).then_inc(stacks_filled, 1)
                    pool.wait_ge(stacks_filled, i + 1)
                nc.gpsimd.memset(flip, 0.0).then_inc(flip_steps, 1)
                pool.wait_ge(flip_steps, 1)
                nc.gpsimd.affine_select(out=flip, in_=flip, compare_op=ALU.not_equal, fill=1.0, base=-(P - 1),
                                        pattern=[[1, P]], channel_multiplier=1).then_inc(flip_steps, 1)
                pool.wait_ge(flip_steps, 2)
                nc.gpsimd.memset(tile_is, 1.0).then_inc(flip_steps, 1)
                pool.wait_ge(flip_steps, 3)
                nc.gpsimd.affine_select(out=tile_is, in_=tile_is, compare_op=ALU.is_ge, fill=0.0, base=0,
                                        pattern=[[0, HEADS], [1, SEQ]], channel_multiplier=-P).then_inc(tiles_marked, 1)
                pool.wait_ge(tiles_marked, 1)
                nc.gpsimd.affine_select(out=tile_is, in_=tile_is, compare_op=ALU.is_ge, fill=0.0, base=P - 1,
                                        pattern=[[0, HEADS], [-1, SEQ]], channel_multiplier=P).then_inc(tiles_marked, 1)

            @block.scalar
            def _(act):
                act.wait_ge(run_ready, 1)
                nc.scalar.activation(factors, factors, ACT.Exp).then_inc(factors_ready, 1)

            @block.tensor
            def _(pe):
                pe.wait_ge(flip_steps, 2)
                pe.wait_ge(flipped_loaded, 16)
                for n in range(HEADS * BAND // SEQ):
                    if n:
                        pe.wait_ge(band_kept, n)
                    nc.tensor.matmul(spare[:], flip, flipped[:, n * SEQ:(n + 1) * SEQ],
                                     start=True, stop=True).then_inc(band_full, 1)

            @block.vector
            def _(dve):
                links = [0]

                def link(instruction):
                    links[0] += 1
                    instruction.then_inc(chain, 1)
                    dve.wait_ge(chain, links[0])

                dve.wait_ge(bias_loaded, 16)
                link(nc.vector.tensor_scalar(by_head, by_head, 8.0, None, ALU.mult))
                link(nc.vector.reduce_max(largest[:], by_head, AX.X))
                link(nc.vector.tensor_scalar(by_head, by_head, largest[:], None, ALU.subtract))
                for lo, hi in zip(edges[:-1], edges[1:]):
                    b = int(bucket[lo])
                    last = nc.vector.tensor_copy(factors[:, lo:hi], by_head[:, b:b + 1].broadcast_to([HEADS, hi - lo]))
                last.then_inc(run_ready, 1)
                for i in range(2):
                    nc.vector.memset(words(q_stack[i][64:MAX_ROW]), 0.0).then_inc(q_filled, 1)
                link(nc.vector.memset(const, 0.0))
                for c in range(TILES):
                    if c:
                        near = by_head[:, 0:1].broadcast_to([HEADS, c * P])
                        last = nc.vector.tensor_copy(const[:, c, 0:c * P], near)
                    if c * P + BAND < SEQ:
                        far = by_head[:, BUCKETS - 1:BUCKETS].broadcast_to([HEADS, SEQ - c * P - BAND])
                        last = nc.vector.tensor_copy(const[:, c, c * P + BAND:SEQ], far)
                link(last)
                link(nc.vector.tensor_copy(const_parts[:, 0], const))
                link(nc.vector.tensor_tensor(rest, const, const_parts[:, 0], ALU.subtract))
                link(nc.vector.tensor_copy(const_parts[:, 1], rest))
                nc.vector.tensor_tensor(const_parts[:, 2], rest, const_parts[:, 1],
                                        ALU.subtract).then_inc(const_ready, 1)
                for n in range(HEADS * BAND // SEQ):
                    dve.wait_ge(band_full, n + 1)
                    nc.vector.tensor_copy(band[:].rearrange("p h q -> p (h q)")[:, n * SEQ:(n + 1) * SEQ],
                                          spare[:]).then_inc(band_kept, 1)


def ffn_phase(nc, sems, tag, x_sb, mv_all, rstd, ident, rows_dram, gate_w, w1, b1, w2, b2, out_dram):
    with ExitStack() as ctx:
        def sb(name, shape, dt=F32):
            return ctx.enter_context(nc.sbuf_tensor(tag + name, shape, dt))

        def sem(name):
            return sems.new(tag + name)

        def ps(name, banks):
            return ctx.enter_context(nc.psum_tensor(tag + name, [P, banks, SEQ], F32))

        norm = Norm(nc, sems, ctx, tag, mv_all, rstd)
        w1_sb = sb("w1", [P, EXPERTS, FFN_DIM])
        w2_sb = sb("w2", [P, EXPERTS, FFN_CHUNKS, EMBD])
        b1_rows = sb("b1_rows", [P, EXPERTS, FFN_DIM])
        b2_rows = sb("b2_rows", [P, EXPERTS, EMBD])
        gate_rows = sb("gate_rows", [EXPERTS, EMBD])
        gate_sb = sb("gate", [P, EXPERTS])
        before = sb("before", [P, P])
        ones = sb("ones", [P, P])
        first_wins = sb("first_wins", [P, EXPERTS])
        lower = sb("lower", [P, EXPERTS, EXPERTS])
        tile_starts = sb("tile_starts", [P, EXPERTS, CHUNK_TILES])
        slot_tile_int = sb("slot_tile_int", [1, SLOT_TILES, EXPERTS], I32)
        slot_tile = sb("slot_tile", [1, SLOT_TILES, EXPERTS])
        ALL_TILES = BATCH * TILES
        x_norm = sb("x_norm", [P, ALL_TILES, EMBD])
        x_normT = sb("x_normT", [P, 2, SEQ])
        shape = [P, ALL_TILES, EXPERTS]
        top = sb("top", [P, ALL_TILES, 1])
        prob, left, key, counts_a, counts_b, place = [sb(n, shape) for n in (
            "prob", "left", "key", "counts_a", "counts_b", "place")]
        pick = [sb(f"pick{i}", shape) for i in range(2)]
        filled_tiles = sb("filled_tiles", [P, CHUNKS, EXPERTS, CHUNK_TILES])
        tiles_of = sb("tiles_of", [P, CHUNKS, EXPERTS])
        tiles_lower = sb("tiles_lower", [P, CHUNKS, EXPERTS, EXPERTS])
        first_tile = sb("first_tile", [P, CHUNKS, EXPERTS])
        end_tile = sb("end_tile", [P, CHUNKS, EXPERTS])
        past = sb("past", [1, CHUNKS, SLOT_TILES, EXPERTS])
        expert_f = sb("expert_f", [1, CHUNKS * SLOT_TILES])
        expert_of = sb("expert_of", [1, CHUNKS * SLOT_TILES], I32)
        slot_f = sb("slot_f", [P, 2, ALL_TILES])
        slot_of = sb("slot_of", [P, 2, ALL_TILES], I32)
        gates = sb("gates", [P, 2, ALL_TILES])
        xs = sb("xs", [P, RING, EMBD])
        xsT = sb("xsT", [P, 2, P])
        hidden = sb("hidden", [P, 2, FFN_DIM])
        hiddenT = sb("hiddenT", [P, 2, FFN_DIM])
        ys = sb("ys", [P, RING, EMBD])
        results = sb("results", [P, 2, 2, CHUNK_TILES, EMBD])
        stats = sb("stats", [P, CHUNK_TILES, 6])
        xT_ps, gate_ps = ps("xT_ps", 1), ps("gate_ps", 1)
        up_ps, upT_ps, down_ps = ps("up_ps", 2), ps("upT_ps", 2), ps("down_ps", 2)
        xs_dram, ys_dram = rows_dram

        weights_loaded = [sem(f"weights_loaded{e}") for e in range(EXPERTS)]
        small_loaded = sem("small_loaded")
        bias_loaded = sem("bias_loaded")
        gate_full = sem("gate_full")
        gate_kept = sem("gate_kept")
        marks = sem("marks")
        marks_v = sem("marks_v")
        x_normed = sem("x_normed")
        xT_full = sem("xT_full")
        xT_kept = sem("xT_kept")
        logits_full = sem("logits_full")
        logits_less = sem("logits_less")
        gate_exp = sem("gate_exp")
        chain = sem("chain")
        picked = sem("picked")
        counted = sem("counted")
        routed = sem("routed")
        experts_ready = sem("experts_ready")
        scattered = [sem(f"scattered{c}") for c in range(CHUNKS)]
        gathered = [sem(f"gathered{c}") for c in range(CHUNKS)]
        xs_loaded = [sem(f"xs_loaded{i}") for i in range(RING)]
        ys_stored = [sem(f"ys_stored{i}") for i in range(RING)]
        up_full = sem("up_full")
        hidden_ready = sem("hidden_ready")
        upT_full = sem("upT_full")
        relu_done = sem("relu_done")
        down_full = sem("down_full")
        ys_ready = sem("ys_ready")
        combined = sem("combined")
        out_stored = sem("out_stored")
        passed = sem("passed")

        FRONTS = [(0, 1), (1, CHUNKS)]
        front_ps = [(gate_ps[:, 0], up_ps[:, 0], up_ps[:, 1]), (down_ps[:, 0], upT_ps[:, 0], upT_ps[:, 1])]

        xT_banks = [xT_ps[:, 0], down_ps[:, 1]]

        def front_batches(f):
            return [c * CHUNK_TILES // TILES for c in FRONTS[f]]

        xT_before = [BATCH + c * SLOT_TILES for c in range(CHUNKS + 1)]

        def slot_steps(c, step, begin=lambda c, st, s0: None):
            first, last = RING + 2, SLOT_TILES - 1 - AHEAD
            assert (last - first + 1) % RING == 0

            def on_at(s):
                return lambda ahead: 0 <= s + ahead < SLOT_TILES
            def run(eng):
                for s in range(-2, first):
                    if (s + 2) % RING == 0:
                        begin(c, Step(s), s)
                    step(eng, c, Step(s), s, on_at(s))
                with eng.Fori(0, (last - first + 1) // RING) as reg:
                    begin(c, Step(first, RING, reg), first)
                    for i in range(RING):
                        step(eng, c, Step(first + i, RING, reg), first + i, lambda ahead: True)
                for s in range(last + 1, SLOT_TILES + 1):
                    if (s - last - 1) % RING == 0:
                        begin(c, Step(s), s)
                    step(eng, c, Step(s), s, on_at(s))
            return run

        def number(c, ahead):
            return lambda s: c * SLOT_TILES + s + ahead

        def ring_before(c, ahead, buffer):
            return lambda s: (number(c, ahead)(s) - buffer) // RING

        def experts(engine, c, st, s0, ahead):
            steps = [s for s in range(s0, s0 + RING) if st.reg is not None or 0 <= s + ahead < SLOT_TILES]
            if not steps:
                return {}
            n = st.at(lambda s: number(c, ahead)(s) + steps[0] - s0)
            _, values = nc.values_load_multi_w_load_instructions(
                expert_of[0:1, bass.ds(n, len(steps))], engines=[engine],
                min_val=0, max_val=EXPERTS - 1,
                skip_runtime_bounds_check_because="a count of experts, at least 0, of which find_experts() takes "
                                                  "the minimum with the last expert")
            return dict(zip(steps, values))

        with nc.Block() as block:
            @block.sync
            def _(sp):
                sp.dma_start(gate_rows[:], gate_w).then_inc(small_loaded, 16)
                sp.dma_start(b1_rows[:], b1.partition_broadcast(P)).then_inc(bias_loaded, 16)
                sp.dma_start(b2_rows[:], b2.partition_broadcast(P)).then_inc(bias_loaded, 16)
                for e in range(EXPERTS):
                    sp.dma_start(w1_sb[:, e, :], w1[e]).then_inc(weights_loaded[e], 16)
                    sp.dma_start(w2_sb[:, e, :, :], w2[e].rearrange("(c f) n -> f c n", f=P)
                                 ).then_inc(weights_loaded[e], 16)

                def dram_rows(dram, st, c, ahead):
                    n = st.at(lambda s: s + ahead)
                    tiles = dram[c % 2].rearrange("(s p) e -> s p e", p=P)
                    return tiles[n] if isinstance(n, int) else tiles[bass.ds(n, 1)].rearrange("o p e -> (o p) e")

                def load(st, c, ahead, buffer):
                    sp.dma_start(xs[:, buffer, :], dram_rows(xs_dram, st, c, ahead)).then_inc(xs_loaded[buffer], 16)

                def step(eng, c, st, s0, on):
                    if on(AHEAD):
                        sp.wait_ge(xT_full, st.at(lambda s: xT_before[c] + s + AHEAD - RING + 1))
                        load(st, c, AHEAD, number(c, AHEAD)(s0) % RING)
                    if on(-1):
                        buffer = number(c, -1)(s0) % RING
                        sp.wait_ge(ys_ready, st.at(lambda s: number(c, -1)(s) + 1))
                        sp.dma_start(dram_rows(ys_dram, st, c, -1), ys[:, buffer, :]).then_inc(ys_stored[buffer], 16)

                for c in range(CHUNKS):
                    sp.wait_ge(scattered[c], 16 * 2 * CHUNK_TILES)
                    if c >= 2:
                        sp.wait_ge(gathered[c - 2], 16 * 2 * CHUNK_TILES)
                    if c:
                        sp.wait_ge(xT_full, xT_before[c])
                    for s in range(AHEAD - 2):
                        load(Step(s), c, 0, number(c, 0)(s) % RING)
                    slot_steps(c, step)(sp)
                for i in range(RING):
                    sp.wait_ge(ys_stored[i], 16 * (CHUNKS * SLOT_TILES // RING))
                if out_dram is not None:
                    out_tiles = out_dram.rearrange("b (t p) e -> p (b t) e", p=P)
                    for c in range(CHUNKS):
                        sp.wait_ge(combined, c + 1)
                        span = slice(c * CHUNK_TILES, (c + 1) * CHUNK_TILES)
                        sp.dma_start(out_tiles[:, span, :], x_sb[:, span, :]).then_inc(out_stored, 16)
                    sp.wait_ge(out_stored, 16 * CHUNKS)

            @block.gpsimd
            def _(pool):
                links = [0]

                def link(instruction):
                    links[0] += 1
                    instruction.then_inc(marks, 1)
                    pool.wait_ge(marks, links[0])

                link(nc.gpsimd.memset(ones[:], 1.0))
                link(nc.gpsimd.memset(before[:], 1.0))
                link(nc.gpsimd.affine_select(out=before[:], in_=before[:], compare_op=ALU.is_gt, fill=0.0, base=0,
                                             pattern=[[1, P]], channel_multiplier=-1))
                link(nc.gpsimd.iota(slot_tile_int[:], [[1, SLOT_TILES], [0, EXPERTS]], base=0, channel_multiplier=0))

                def slots(c, i, t):
                    n = c * CHUNK_TILES + t
                    return slot_of[:, i, n:n + 1]

                def scatter(c):
                    pool.wait_ge(routed, min(c, 1) + 1)
                    for t in range(CHUNK_TILES):
                        for i in range(2):
                            nc.gpsimd.indirect_dma_start(
                                out=xs_dram[c % 2], in_=x_norm[:, c * CHUNK_TILES + t, :], in_offset=None,
                                out_offset=bass.IndirectOffsetOnAxis(ap=slots(c, i, t), axis=0)
                            ).then_inc(scattered[c], 16)

                def gather(c):
                    for i in range(RING):
                        pool.wait_ge(ys_stored[i], 16 * (((c + 1) * SLOT_TILES + RING - 1 - i) // RING))
                    wait(pool, combined, c - 1)
                    for t in range(CHUNK_TILES):
                        for i in range(2):
                            nc.gpsimd.indirect_dma_start(
                                out=results[:, c % 2, i, t, :], out_offset=None, in_=ys_dram[c % 2],
                                in_offset=bass.IndirectOffsetOnAxis(ap=slots(c, i, t), axis=0)
                            ).then_inc(gathered[c], 16)

                pool.wait_ge(x_normed, BATCH)
                scatter(0)
                scatter(1)
                for c in range(CHUNKS):
                    gather(c)
                    if c + 2 < CHUNKS:
                        scatter(c + 2)

            @block.tensor
            def _(pe):
                pe.wait_ge(small_loaded, 16)
                nc.tensor.transpose(gate_ps[:, 0, 0:EXPERTS], gate_rows[:],
                                    ident[0:EXPERTS, 0:EXPERTS]).then_inc(gate_full, 1)
                pe.wait_ge(gate_kept, 1)
                pe.wait_ge(marks, 4)

                def transposes(q):
                    pe.wait_ge(x_normed, q + 1)
                    wait(pe, xT_kept, q - 1)
                    for t in range(TILES):
                        last = nc.tensor.transpose(xT_banks[q % 2][:, t * P:(t + 1) * P],
                                                   x_norm[:, q * TILES + t, :], ident[:])
                    last.then_inc(xT_full, 1)

                def logits(q):
                    f = 0 if q < front_batches(0)[1] else 1
                    pe.wait_ge(xT_kept, q + 1)
                    for t in range(TILES):
                        col = ((q - front_batches(f)[0]) * TILES + t) * EXPERTS
                        last = nc.tensor.matmul(front_ps[f][0][:, col:col + EXPERTS],
                                                x_normT[:, q % 2, t * P:(t + 1) * P], gate_sb[:],
                                                start=True, stop=True)
                    last.then_inc(logits_full, 1)

                def count_rows(f):
                    _, in_front, in_tile = front_ps[f]
                    lo, hi = front_batches(f)
                    pe.wait_ge(picked, f + 1)
                    choices = key[:, lo * TILES:hi * TILES, :].rearrange("p t e -> p (t e)")
                    n = (hi - lo) * TILES * EXPERTS
                    nc.tensor.matmul(in_front[:, 0:n], before[:], choices, start=True, stop=True)
                    nc.tensor.matmul(in_tile[:, 0:n], ones[:], choices, start=True, stop=True).then_inc(counted, 1)

                up_expert, down_expert = {}, {}

                def begin(c, st, s0):
                    up_expert.update(experts(mybir.EngineType.PE, c, st, s0, 1))
                    down_expert.update(experts(mybir.EngineType.PE, c, st, s0, -1))

                def step(eng, c, st, s0, on):
                    if on(2) or on(1):
                        pe.wait_ge(xT_kept, st.at(lambda s: xT_before[c] + s + 2))
                    if on(2):
                        buffer = number(c, 2)(s0) % RING
                        pe.wait_ge(xs_loaded[buffer], st.at(lambda s: 16 * (ring_before(c, 2, buffer)(s) + 1)))
                        nc.tensor.transpose(xT_ps[:, 0, 0:P], xs[:, buffer, :], ident[:]).then_inc(xT_full, 1)
                    if on(1):
                        parity, e = number(c, 1)(s0) % 2, up_expert[s0]
                        nc.tensor.matmul(up_ps[:, parity, :], xsT[:, parity, :],
                                         w1_sb[:, bass.ds(e, 1), :].rearrange("p o n -> p (o n)"),
                                         start=True, stop=True).then_inc(up_full, 1)
                    if on(0):
                        parity = number(c, 0)(s0) % 2
                        pe.wait_ge(hidden_ready, st.at(lambda s: number(c, 0)(s) + 1))
                        for f in range(FFN_CHUNKS):
                            last = nc.tensor.transpose(upT_ps[:, parity, f * P:(f + 1) * P],
                                                       hidden[:, parity, f * P:(f + 1) * P], ident[:])
                        last.then_inc(upT_full, 1)
                    if on(-1):
                        parity, e = number(c, -1)(s0) % 2, down_expert[s0]
                        pe.wait_ge(relu_done, st.at(lambda s: number(c, -1)(s) + 1))
                        wait(pe, ys_ready, st.at(lambda s: number(c, -1)(s) - 1))
                        for f in range(FFN_CHUNKS):
                            last = nc.tensor.matmul(down_ps[:, parity, 0:EMBD], hiddenT[:, parity, f * P:(f + 1) * P],
                                                    w2_sb[:, bass.ds(e, 1), f, :].rearrange("p o n -> p (o n)"),
                                                    start=(f == 0), stop=(f == FFN_CHUNKS - 1))
                        last.then_inc(down_full, 1)

                for q in range(BATCH + 1):
                    if q < BATCH:
                        transposes(q)
                    if q:
                        logits(q - 1)
                    if q == front_batches(0)[1] + 3:
                        count_rows(0)
                count_rows(1)
                for e in range(EXPERTS):
                    pe.wait_ge(weights_loaded[e], 32)
                pe.wait_ge(experts_ready, 1)
                for c in range(CHUNKS):
                    slot_steps(c, step, begin)(pe)

            @block.scalar
            def _(act):
                norm.on_scalar(act)

                def exponentials(f):
                    act.wait_ge(logits_less, f + 1)
                    lo, hi = [b * TILES for b in front_batches(f)]
                    nc.scalar.activation(prob[:, lo:hi, :], left[:, lo:hi, :], ACT.Exp).then_inc(gate_exp, 1)

                def step(eng, c, st, s0, on):
                    if on(2):
                        parity = number(c, 2)(s0) % 2
                        act.wait_ge(xT_full, st.at(lambda s: xT_before[c] + s + 3))
                        wait(act, up_full, st.at(lambda s: number(c, 2)(s) - 1))
                        nc.scalar.copy(xsT[:, parity, :], xT_ps[:, 0, 0:P]).then_inc(xT_kept, 1)
                    if on(0):
                        parity = number(c, 0)(s0) % 2
                        act.wait_ge(upT_full, st.at(lambda s: number(c, 0)(s) + 1))
                        wait(act, down_full, st.at(lambda s: number(c, 0)(s) - 1))
                        nc.scalar.activation(hiddenT[:, parity, :], upT_ps[:, parity, :],
                                             ACT.Relu).then_inc(relu_done, 1)

                for q in range(BATCH):
                    wait(act, logits_full, q - 1)
                    act.wait_ge(xT_full, q + 1)
                    nc.scalar.copy(x_normT[:, q % 2, :], xT_banks[q % 2]).then_inc(xT_kept, 1)
                    if q == front_batches(0)[1]:
                        exponentials(0)
                exponentials(1)
                for c in range(CHUNKS):
                    slot_steps(c, step)(act)

            @block.vector
            def _(dve):
                norm.on_vector(dve)
                links = [0]

                def link(instruction):
                    links[0] += 1
                    instruction.then_inc(chain, 1)
                    dve.wait_ge(chain, links[0])

                dve.wait_ge(gate_full, 1)
                nc.vector.tensor_copy(gate_sb[:], gate_ps[:, 0, 0:EXPERTS]).then_inc(gate_kept, 1)
                dve.wait_ge(marks, 4)
                nc.vector.tensor_copy(slot_tile[:], slot_tile_int[:])
                for e in range(EXPERTS):
                    nc.vector.memset(first_wins[:, e:e + 1], float(EXPERTS - e))
                    if e:
                        nc.vector.memset(lower[:, e, 0:e], 1.0)
                    nc.vector.memset(lower[:, e, e:EXPERTS], 0.0)
                for t in range(CHUNK_TILES):
                    last = nc.vector.memset(tile_starts[:, :, t:t + 1], float(P * t))
                link(last)

                def front(f):
                    (lo, hi), (c0, c1) = [b * TILES for b in front_batches(f)], FRONTS[f]
                    tiles, chunks = hi - lo, c1 - c0
                    part = [P, tiles, EXPERTS]
                    logits, in_front, in_tile = [b[:, 0:tiles * EXPERTS].rearrange("p (t e) -> p t e", e=EXPERTS)
                                                 for b in front_ps[f]]
                    prob_, left_, key_, place_ = [v[:, lo:hi, :] for v in (prob, left, key, place)]
                    pick_ = [v[:, lo:hi, :] for v in pick]
                    top_ = top[:, lo:hi, :]
                    best = top[:, lo:hi, 0]

                    def spread(v):
                        return v.broadcast_to(part)

                    def by_chunk(v):
                        return v.rearrange("p (c t) e -> p c t e", c=chunks)

                    wins = first_wins[:].rearrange("p (o e) -> p o e", o=1).broadcast_to(part)
                    dve.wait_ge(logits_full, hi // TILES)
                    link(nc.vector.reduce_max(best, logits, AX.X))
                    nc.vector.tensor_tensor(left_, logits, spread(top_), ALU.subtract).then_inc(logits_less, 1)
                    dve.wait_ge(gate_exp, f + 1)
                    link(nc.vector.reduce_sum(best, prob_, AX.X))
                    link(nc.vector.reciprocal(best, best))
                    link(nc.vector.tensor_tensor(prob_, prob_, spread(top_), ALU.mult))
                    for i, p in enumerate((prob_, left_)):
                        if i:
                            link(nc.vector.scalar_tensor_tensor(left_, pick_[0], -4.0, prob_, ALU.mult, ALU.add))
                        link(nc.vector.reduce_max(best, p, AX.X))
                        nc.vector.tensor_copy(gates[:, i, lo:hi], best)
                        link(nc.vector.tensor_tensor(key_, p, spread(top_), ALU.is_equal))
                        link(nc.vector.tensor_tensor(key_, key_, wins, ALU.mult))
                        link(nc.vector.reduce_max(best, key_, AX.X))
                        link(nc.vector.tensor_tensor(pick_[i], key_, spread(top_), ALU.is_equal))
                    nc.vector.tensor_tensor(key_, pick_[0], pick_[1], ALU.add).then_inc(picked, 1)
                    dve.wait_ge(counted, f + 1)
                    link(nc.vector.tensor_copy(counts_a[:, lo:hi, :], in_tile))
                    a, b, reach = by_chunk(counts_a[:, lo:hi, :]), by_chunk(counts_b[:, lo:hi, :]), 1
                    while reach < CHUNK_TILES:
                        nc.vector.tensor_copy(b[:, :, 0:reach, :], a[:, :, 0:reach, :])
                        link(nc.vector.tensor_tensor(b[:, :, reach:, :], a[:, :, reach:, :],
                                                     a[:, :, 0:CHUNK_TILES - reach, :], ALU.add))
                        a, b, reach = b, a, 2 * reach
                    link(nc.vector.tensor_tensor(place_, a.rearrange("p c t e -> p (c t) e"), in_tile, ALU.subtract))
                    link(nc.vector.tensor_tensor(place_, place_, in_front, ALU.add))
                    for c in range(c0, c1):
                        total = a[:, c - c0, CHUNK_TILES - 1, :].rearrange("p (e o) -> p e o", o=1)
                        last = nc.vector.tensor_tensor(filled_tiles[:, c], total.broadcast_to([P, EXPERTS, CHUNK_TILES]),
                                                       tile_starts[:], ALU.is_gt)
                    link(last)
                    link(nc.vector.reduce_sum(tiles_of[:, c0:c1, :], filled_tiles[:, c0:c1], AX.X))
                    for c in range(c0, c1):
                        others = tiles_of[:, c:c + 1, :].broadcast_to([P, EXPERTS, EXPERTS])
                        last = nc.vector.tensor_tensor(tiles_lower[:, c], lower[:], others, ALU.mult)
                    link(last)
                    link(nc.vector.reduce_sum(first_tile[:, c0:c1, :], tiles_lower[:, c0:c1], AX.X))
                    link(nc.vector.tensor_tensor(end_tile[:, c0:c1, :], first_tile[:, c0:c1, :], tiles_of[:, c0:c1, :],
                                                 ALU.add))
                    for c in range(c0, c1):
                        firsts = first_tile[:, c:c + 1, :].broadcast_to([P, CHUNK_TILES, EXPERTS])
                        last = nc.vector.scalar_tensor_tensor(
                            place[:, c * CHUNK_TILES:(c + 1) * CHUNK_TILES, :], firsts, float(P),
                            place[:, c * CHUNK_TILES:(c + 1) * CHUNK_TILES, :], ALU.mult, ALU.add)
                    link(last)
                    for i in range(2):
                        link(nc.vector.tensor_tensor(key_, pick_[i], place_, ALU.mult))
                        link(nc.vector.reduce_sum(slot_f[:, i, lo:hi], key_, AX.X))
                    nc.vector.tensor_copy(slot_of[:, :, lo:hi], slot_f[:, :, lo:hi]).then_inc(routed, 1)
                    dve.wait_ge(routed, f + 1)

                def find_experts():
                    for c in range(CHUNKS):
                        ends = end_tile[0:1, c:c + 1, :].broadcast_to([1, SLOT_TILES, EXPERTS])
                        last = nc.vector.tensor_tensor(past[:, c], slot_tile[:], ends, ALU.is_ge)
                    link(last)
                    link(nc.vector.reduce_sum(expert_f[:], past[:].rearrange("p c s e -> p (c s) e"), AX.X))
                    nc.vector.tensor_scalar(expert_of[:], expert_f[:], float(EXPERTS - 1), None,
                                            ALU.min).then_inc(experts_ready, 1)
                    dve.wait_ge(experts_ready, 1)

                up_expert, down_expert = {}, {}

                def begin(c, st, s0):
                    up_expert.update(experts(mybir.EngineType.DVE, c, st, s0, 1))
                    down_expert.update(experts(mybir.EngineType.DVE, c, st, s0, -1))

                def step(eng, c, st, s0, on):
                    if on(1):
                        parity, e = number(c, 1)(s0) % 2, up_expert[s0]
                        wait(dve, upT_full, st.at(lambda s: number(c, 1)(s) - 1))
                        dve.wait_ge(up_full, st.at(lambda s: number(c, 1)(s) + 1))
                        nc.vector.tensor_tensor(hidden[:, parity, :], up_ps[:, parity, :],
                                                b1_rows[:, bass.ds(e, 1), :].rearrange("p o n -> p (o n)"),
                                                ALU.add).then_inc(hidden_ready, 1)
                    if on(-1):
                        parity, buffer, e = number(c, -1)(s0) % 2, number(c, -1)(s0) % RING, down_expert[s0]
                        wait(dve, ys_stored[buffer], st.at(lambda s: 16 * ring_before(c, -1, buffer)(s)))
                        dve.wait_ge(down_full, st.at(lambda s: number(c, -1)(s) + 1))
                        nc.vector.tensor_tensor(ys[:, buffer, :], down_ps[:, parity, 0:EMBD],
                                                b2_rows[:, bass.ds(e, 1), :].rearrange("p o n -> p (o n)"),
                                                ALU.add).then_inc(ys_ready, 1)

                def combine(c, part):
                    tiles = range(c * CHUNK_TILES, (c + 1) * CHUNK_TILES)
                    if part == 0:
                        dve.wait_ge(gathered[c], 16 * 2 * CHUNK_TILES)
                    if part < 4:
                        i, h = part // 2, part % 2 * CHUNK_TILES // 2
                        for t in range(h, h + CHUNK_TILES // 2):
                            n = tiles[t]
                            last = nc.vector.scalar_tensor_tensor(x_sb[:, n, :], results[:, c % 2, i, t, :],
                                                                  gates[:, i, n:n + 1], x_sb[:, n, :],
                                                                  ALU.mult, ALU.add)
                        if part == 3:
                            last.then_inc(combined, 1)
                            dve.wait_ge(combined, c + 1)
                        else:
                            link(last)
                    elif out_dram is None:
                        for t, n in enumerate(tiles):
                            if part == 4:
                                last = nc.vector.bn_stats(stats[:, t, :], x_sb[:, n, :])
                            else:
                                last = nc.vector.bn_aggr(mv_all[:, n, :], stats[:, t, :])
                        link(last)

                def step_and_combine(eng, c, st, s0, on):
                    step(eng, c, st, s0, on)
                    part = s0 - (SLOT_TILES + 1 - 6)
                    if c and st.reg is None and part >= 0:
                        combine(c - 1, part)

                for t in range(ALL_TILES):
                    last = nc.vector.tensor_scalar(x_norm[:, t, :], x_sb[:, t, :], mv_all[:, t, 0:1],
                                                   rstd[:, t:t + 1], ALU.subtract, ALU.mult)
                    if t % TILES == TILES - 1:
                        last.then_inc(x_normed, 1)
                front(0)
                front(1)
                find_experts()
                dve.wait_ge(bias_loaded, 32)
                for c in range(CHUNKS):
                    slot_steps(c, step_and_combine, begin)(dve)
                for part in range(6):
                    combine(CHUNKS - 1, part)


def hybrid(nc, x, wq, bq, wk, bk, wv, bv, wo, bo, rel_bias, wqkv, bqkv, wout, bout, gate_w, w1, b1, w2, b2, out):
    sems = Sems(nc)
    with ExitStack() as ctx:
        x_sb = ctx.enter_context(nc.sbuf_tensor("x_sb", [P, BATCH * TILES, EMBD], F32))
        mv_all = ctx.enter_context(nc.sbuf_tensor("mv_all", [P, BATCH * TILES, 2], F32))
        rstd = ctx.enter_context(nc.sbuf_tensor("rstd", [P, BATCH * TILES], F32))
        ident = ctx.enter_context(nc.sbuf_tensor("ident", [P, P], F32))

        def column(v):
            return v.rearrange("(e o) -> e o", o=1)

        def rows(v):
            return v.partition_broadcast(P)

        def by_head(v, which):
            part = slice(which * HEAD_DIM, (which + 1) * HEAD_DIM)
            if len(v.shape) == 2:
                return v.rearrange("e (h c) -> e h c", h=HEADS)[:, :, part]
            return v.rearrange("(h c) -> h c", h=HEADS)[:, part]

        rows_dram = [[nc.dram_tensor(f"{n}_dram{i}", (SLOT_TILES * P, EMBD), F32, kind="Internal").ap()
                      for i in range(2)] for n in ("sorted", "results")]
        load_phase(nc, sems, x, x_sb, mv_all, ident, rows_dram[0])
        sems.clear()
        attention_phase(nc, sems, "aa_", x_sb, mv_all, rstd, ident,
                        dict(wq=wq, wk=wk, wv=wv, wo=wo, bq=column(bq), bk=column(bk), bv=rows(bv), bo=rows(bo)),
                        rel_bias)
        sems.clear()
        ffn_phase(nc, sems, "f1_", x_sb, mv_all, rstd, ident, rows_dram, gate_w, w1, b1, w2, b2, None)
        sems.clear()
        with nc.allow_non_contiguous_dma("q and k biases, one value per partition"):
            attention_phase(nc, sems, "ab_", x_sb, mv_all, rstd, ident,
                            dict(wq=by_head(wqkv, 0), wk=by_head(wqkv, 1), wv=by_head(wqkv, 2), wo=wout,
                                 bq=by_head(bqkv, 0), bk=by_head(bqkv, 1), bv=rows(by_head(bqkv, 2)), bo=rows(bout)),
                            None)
        sems.clear()
        ffn_phase(nc, sems, "f2_", x_sb, mv_all, rstd, ident, rows_dram, gate_w, w1, b1, w2, b2, out)
        sems.clear()


_INS = ["L0_attn_a_hidden_states", "L0_attn_a_Wq", "L0_attn_a_bq", "L0_attn_a_Wk", "L0_attn_a_bk", "L0_attn_a_Wv",
        "L0_attn_a_bv", "L0_attn_a_Wo", "L0_attn_a_bo", "L0_attn_a_rel_bias", "L0_attn_b_Wqkv", "L0_attn_b_bqkv",
        "L0_attn_b_Wout", "L0_attn_b_bout", "L0_ffn_gate_w", "L0_ffn_w1", "L0_ffn_b1", "L0_ffn_w2", "L0_ffn_b2"]


def kernel(**inputs):
    import numpy as _np
    import concourse.bacc as _bacc
    from concourse import mybir as _mybir
    from concourse.bass_utils import run_bass_kernel_spmd as _run

    nc = _bacc.Bacc("TRN2", target_bir_lowering=False, num_devices=1)
    arrays, args = {}, []
    for name in _INS:
        a = _np.ascontiguousarray(inputs[name])
        arrays[f"in_{name}"] = a
        args.append(nc.dram_tensor(f"in_{name}", a.shape, _mybir.dt.from_np(a.dtype), kind="ExternalInput").ap())
    out = nc.dram_tensor("out_0", (BATCH, SEQ, EMBD), _mybir.dt.from_np(_np.dtype("float32")),
                         kind="ExternalOutput").ap()
    hybrid(nc, *args, out)
    r = _run(nc, [arrays], core_ids=[0])
    return r.results[0]["out_0"]
```

```python
import concourse.bass as bass
from concourse import mybir
from contextlib import ExitStack
import numpy as np

F32 = mybir.dt.float32
BF16 = mybir.dt.bfloat16
I32 = mybir.dt.int32
ALU = mybir.AluOpType
ACT = mybir.ActivationFunctionType
AX = mybir.AxisListType

BATCH, SEQ, EMBD = 16, 512, 128
P = 128
TILES = SEQ // P
HEADS, HEAD_DIM = 16, 8
GROUPS, GROUP = 4, 4
EXPERTS, FFN_DIM = 8, 512
FFN_CHUNKS = FFN_DIM // P
BUCKETS, MAX_DISTANCE = 32, 64
LN_EPS = 1e-5
PARTS = 3
PROD_ROWS = PARTS * PARTS * HEAD_DIM
CONST_ROW = PROD_ROWS
MAX_ROW = 96
A_ROWS = MAX_ROW
B_ROWS = MAX_ROW + PARTS
BAND = P + MAX_DISTANCE
CHUNK_TILES = (20, 32, 12)
CHUNKS = len(CHUNK_TILES)
CHUNK_START = [sum(CHUNK_TILES[:c]) for c in range(CHUNKS + 1)]
assert CHUNK_START[-1] == BATCH * TILES and all(n % TILES == 0 for n in CHUNK_TILES)
SLOT_TILES = [(2 * n * P - EXPERTS) // P + EXPERTS for n in CHUNK_TILES]
SLOT_START = [sum(SLOT_TILES[:c]) for c in range(CHUNKS + 1)]
RING = 4
AHEAD = 5
COMBINE_PARTS = 12
LOADS = 4
ONES_WORD = float(np.array([0x3F803F80], np.uint32).view(np.float32)[0])
V_COLS = HEAD_DIM + 1


class Step:

    def __init__(self, first, stride=0, reg=None):
        self.first, self.stride, self.reg = first, stride, reg

    def at(self, count):
        base = count(self.first)
        if self.reg is None:
            return base
        rate = count(self.first + self.stride) - base
        return base + rate * self.reg


def wait(eng, sem, value):
    if isinstance(value, int) and value <= 0:
        return
    eng.wait_ge(sem, value)


class Sems:

    def __init__(self, nc):
        self.nc, self.held = nc, []

    def new(self, name):
        self.held.append(self.nc.alloc_semaphore(name))
        return self.held[-1]

    def clear(self):
        self.nc.clear_and_free_semaphores(self.held)
        self.nc.all_engine_barrier()
        self.held = []


def wait_apart(eng, sem, value, passed):
    eng.wait_ge(sem, value)
    eng.sem_inc(passed, 1)


def bias_buckets(limit):
    d = np.arange(limit)
    exact = BUCKETS // 2
    far = np.maximum(d, 1).astype(np.float32)
    large = exact + (np.log(far / np.float32(exact)) / np.float32(np.log(MAX_DISTANCE / exact))
                     * np.float32(BUCKETS - exact)).astype(np.int32)
    return np.where(d < exact, d, np.minimum(large, BUCKETS - 1))


def tokens(x, first):
    if isinstance(first, int):
        return x[:, first:first + TILES]
    return x[:, bass.ds(first, TILES)]


def words(stack):
    return stack.rearrange("p h q -> p (h q)").bitcast(F32)


def load_phase(nc, sems, x_dram, x_sb, mv_all, ident, sorted_dram, zeros, zeros_stored):
    with ExitStack() as ctx:
        stats = ctx.enter_context(nc.sbuf_tensor("ld_stats", [P, BATCH * TILES, 6], F32))
        x_loaded = [sems.new(f"ld_x_loaded{i}") for i in range(LOADS)]
        stats_done = sems.new("ld_stats_done")
        zeroed = sems.new("ld_zeroed")
        ident_done = sems.new("ld_ident_done")
        x_tiles = x_dram.rearrange("b (t p) e -> p (b t) e", p=P)
        with nc.Block() as block:
            @block.sync
            def _(sp):
                n = BATCH * TILES // LOADS
                for i in range(LOADS):
                    sp.dma_start(x_sb[:, i * n:(i + 1) * n, :], x_tiles[:, i * n:(i + 1) * n, :]
                                 ).then_inc(x_loaded[i], 16)
                sp.wait_ge(zeroed, 1)
                for dram in sorted_dram:
                    tiles = dram.rearrange("(s p) e -> p s e", p=P)
                    sp.dma_start(tiles, zeros[:].broadcast_to([P, tiles.shape[1], EMBD])).then_inc(zeros_stored, 16)

            @block.gpsimd
            def _(pool):
                nc.gpsimd.memset(zeros[:], 0.0).then_inc(zeroed, 1)
                nc.gpsimd.memset(ident[:], 0.0).then_inc(zeroed, 1)
                pool.wait_ge(zeroed, 2)
                nc.gpsimd.affine_select(out=ident[:], in_=ident[:], compare_op=ALU.not_equal, fill=1.0, base=0,
                                        pattern=[[-1, P]], channel_multiplier=1).then_inc(ident_done, 1)
                pool.wait_ge(ident_done, 1)

            @block.vector
            def _(dve):
                for i in range(LOADS):
                    dve.wait_ge(x_loaded[i], 16)
                    piece = range(i * BATCH * TILES // LOADS, (i + 1) * BATCH * TILES // LOADS)
                    for n in piece:
                        last = nc.vector.bn_stats(stats[:, n, :], x_sb[:, n, :])
                    last.then_inc(stats_done, 1)
                    dve.wait_ge(stats_done, i + 1)
                    for n in piece:
                        nc.vector.bn_aggr(mv_all[:, n, :], stats[:, n, :])


class Norm:

    def __init__(self, nc, sems, ctx, tag, mv_all, rstd):
        self.nc, self.mv_all, self.rstd = nc, mv_all, rstd
        self.var = ctx.enter_context(nc.sbuf_tensor(tag + "_var", [P, BATCH * TILES], F32))
        self.root = ctx.enter_context(nc.sbuf_tensor(tag + "_root", [P, BATCH * TILES], F32))
        self.var_ready = sems.new(tag + "_var_ready")
        self.root_ready = sems.new(tag + "_root_ready")
        self.chain = sems.new(tag + "_rstd_chain")

    def on_scalar(self, act):
        act.wait_ge(self.var_ready, 1)
        self.nc.scalar.activation(self.root[:], self.var[:], ACT.Sqrt).then_inc(self.root_ready, 1)

    def on_vector(self, dve):
        nc, var, root, rstd = self.nc, self.var, self.root, self.rstd
        nc.vector.tensor_scalar(var[:], self.mv_all[:, :, 1], LN_EPS, None, ALU.add).then_inc(self.var_ready, 1)
        dve.wait_ge(self.root_ready, 1)
        nc.vector.reciprocal(rstd[:], root[:]).then_inc(self.chain, 1)
        dve.wait_ge(self.chain, 1)
        nc.vector.tensor_tensor(root[:], rstd[:], rstd[:], ALU.mult).then_inc(self.chain, 1)
        dve.wait_ge(self.chain, 2)
        nc.vector.tensor_tensor(root[:], root[:], var[:], ALU.mult).then_inc(self.chain, 1)
        dve.wait_ge(self.chain, 3)
        nc.vector.tensor_scalar(root[:], root[:], -0.5, 1.5, ALU.mult, ALU.add).then_inc(self.chain, 1)
        dve.wait_ge(self.chain, 4)
        nc.vector.tensor_tensor(rstd[:], rstd[:], root[:], ALU.mult).then_inc(self.chain, 1)
        dve.wait_ge(self.chain, 5)


STAGE_LAG = {"front": 2, "A": 1, "B": 0, "tail": -1}
SLOTS = HEADS
SPARE_USES = [
    (1, "xT", "front"), (2, "max_hi", "B"), (3, "q", "front"), (4, "heads2", "tail"), (5, "k", "front"),
    (6, "heads3", "tail"), (7, "v", "front"), (8, "outT", "tail"), (9, "max_lo", "A"), (10, "y", "tail"),
    (12, "heads0", "B"), (14, "heads1", "B"),
]
SCALAR_SIDE = [
    (2, 1, "xT", "front"), (4, 1, "q", "front"), (4, 3, "q_high", "front"), (5, 3, "q_mid", "front"),
    (6, 1, "k", "front"), (6, 3, "k_high", "front"), (8, 1, "k_mid", "front"), (9, 1, "outT", "tail"),
]
VECTOR_SIDE = [
    (0, 0, "normalize", "front"), (2, 1, "max_hi.0", "B"), (3, 0, "max_hi.1", "B"), (3, 1, "max_hi.2", "B"),
    (4, 0, "max_hi.3", "B"), (4, 1, "heads2.0", "tail"), (5, 0, "heads2.1", "tail"), (6, 0, "v_aug", "A"),
    (6, 1, "heads3.0", "tail"), (7, 0, "heads3.1", "tail"), (7, 1, "v", "front"), (9, 1, "max_lo.0", "A"),
    (10, 0, "max_lo.1", "A"), (10, 1, "max_lo.2", "A"), (11, 0, "max_lo.3", "A"), (11, 1, "y.0", "tail"),
    (12, 0, "y.1", "tail"), (12, 1, "heads0.0", "B"), (13, 0, "heads0.1", "B"), (13, 1, "y.2", "tail"),
    (14, 0, "y.3", "tail"), (14, 1, "heads1.0", "B"), (15, 0, "heads1.1", "B"), (15, 1, "y.4", "tail"),
]
REST_SLOTS = {5: 0, 7: 1}
LAST_PART_SLOTS = {6: 0, 8: 1}


def active(stage, s):
    return 0 <= s + STAGE_LAG[stage] < BATCH


def spare_before(s):
    return sum(active(u[2], n) for n in range(-2, s) for u in SPARE_USES)


def spare_index(what):
    def count(s):
        n = spare_before(s)
        for _, name, stage in SPARE_USES:
            n += active(stage, s)
            if name == what:
                return n
    return count


def attention_phase(nc, sems, tag, x_sb, mv_all, rstd, ident, w_dram, rel_bias):
    scale = float(1.0 / np.sqrt(HEAD_DIM))
    biased = rel_bias is not None
    with ExitStack() as ctx:
        def sb(name, shape, dt=F32):
            return ctx.enter_context(nc.sbuf_tensor(tag + name, shape, dt))

        def sem(name):
            return sems.new(tag + name)

        norm = Norm(nc, sems, ctx, tag, mv_all, rstd)
        w_sb = sb("w", [P, 4, EMBD])
        qk_bias = sb("qk_bias", [P, 2])
        bv_rows = sb("bv_rows", [P, EMBD])
        bo_rows = sb("bo_rows", [P, EMBD])
        x_norm = sb("x_norm", [P, TILES, EMBD])
        x_normT = sb("x_normT", [P, SEQ])
        proj = sb("proj", [P, SEQ])
        rest = sb("rest", [P, SEQ])
        parts = [sb("q_parts", [P, PARTS, SEQ], BF16), sb("k_parts", [P, PARTS, SEQ], BF16)]
        v_stage = sb("v_stage", [P, TILES, HEADS, V_COLS])
        v_aug = [sb(f"v_aug{i}", [P, TILES, HEADS, V_COLS]) for i in range(2)]
        q_stack = [sb(f"q_stack{i}", [P, HEADS, SEQ], BF16) for i in range(2)]
        k_stack = [sb(f"k_stack{i}", [P, HEADS, SEQ], BF16) for i in range(2)]
        row_max = sb("row_max", [P, HEADS * TILES])
        max_rest = sb("max_rest", [HEADS * TILES // 2, P])
        max_parts = sb("max_parts", [HEADS * TILES // 2, PARTS, P], BF16)
        probs = sb("probs", [P, 2 * GROUP, TILES, SEQ])
        heads_raw = [sb(f"heads_raw{i}", [P, SEQ]) for i in range(2)]
        recip = sb("recip", [P, TILES, GROUP, 1])
        heads_out = sb("heads_out", [P, TILES, EMBD])
        heads_outT = sb("heads_outT", [P, SEQ])
        stats = sb("stats", [P, TILES, 6])
        mv = sb("mv", [P, TILES, 2])
        band = sb("band", [P, HEADS, BAND]) if biased else None
        a_ps = ctx.enter_context(nc.psum_tensor(tag + "a_ps", [P, TILES, SEQ], F32))
        b_ps = ctx.enter_context(nc.psum_tensor(tag + "b_ps", [P, 2, SEQ], F32))
        o_ps = ctx.enter_context(nc.psum_tensor(tag + "o_ps", [P, SEQ], F32))
        spare = ctx.enter_context(nc.psum_tensor(tag + "spare", [P, SEQ], F32))
        parts_dram = [nc.dram_tensor(f"{tag}parts_{n}", (EMBD, PARTS, SEQ), BF16, kind="Internal").ap() for n in "qk"]

        weights_loaded = sem("weights_loaded")
        filled = sem("filled")
        if biased:
            setup_bias(nc, sems, tag, probs, heads_outT, heads_raw, q_stack, k_stack, band, rel_bias, spare)
        with nc.Block() as block:
            @block.sync
            def _(sp):
                for i, n in enumerate(("wq", "wk", "wv", "wo")):
                    dst = w_sb[:, i, :]
                    if len(w_dram[n].shape) == 3:
                        dst = dst.rearrange("p (h d) -> p h d", d=HEAD_DIM)
                    sp.dma_start(dst, w_dram[n]).then_inc(weights_loaded, 16)
                for i, n in enumerate(("bq", "bk")):
                    sp.dma_start(qk_bias[:, i:i + 1], w_dram[n]).then_inc(weights_loaded, 16)
                bv_dst = bv_rows[:]
                if len(w_dram["bv"].shape) == 3:
                    bv_dst = bv_dst.rearrange("p (h d) -> p h d", d=HEAD_DIM)
                sp.dma_start(bv_dst, w_dram["bv"]).then_inc(weights_loaded, 16)
                sp.dma_start(bo_rows[:], w_dram["bo"]).then_inc(weights_loaded, 16)
                sp.wait_ge(weights_loaded, 16 * 8)

            @block.gpsimd
            def _(pool):
                if not biased:
                    for i in range(2):
                        nc.gpsimd.memset(words(k_stack[i][64:MAX_ROW]), 0.0).then_inc(filled, 1)
                        pool.wait_ge(filled, i + 1)
                nc.gpsimd.memset(words(k_stack[1][MAX_ROW:B_ROWS]), ONES_WORD)

            @block.scalar
            def _(act):
                norm.on_scalar(act)

            @block.vector
            def _(dve):
                norm.on_vector(dve)
                if not biased:
                    for i in range(2):
                        nc.vector.memset(words(q_stack[i][64:MAX_ROW]), 0.0)
                nc.vector.memset(o_ps[:], 0.0)
                nc.vector.memset(v_stage[:, :, :, HEAD_DIM:V_COLS], 1.0)
                nc.vector.memset(words(k_stack[0][MAX_ROW:B_ROWS]), ONES_WORD)
                dve.wait_ge(weights_loaded, 16 * 8)
                nc.vector.tensor_scalar(qk_bias[:, 0:1], qk_bias[:, 0:1], scale, None, ALU.mult)

        x_normed = sem("x_normed")
        spare_full = sem("spare_full")
        spare_free = sem("spare_free")
        high_ready = sem("high_ready")
        rest_ready = sem("rest_ready")
        mid_ready = sem("mid_ready")
        parts_ready = sem("parts_ready")
        parts_stored = sem("parts_stored")
        stack_loaded = [sem(f"stack_loaded{i}") for i in range(2)]
        v_ready = sem("v_ready")
        a_full = sem("a_full")
        max_taken = sem("max_taken")
        max_chain = sem("max_chain")
        max_stored = [sem(f"max_stored{i}") for i in range(2)]
        b_full = sem("b_full")
        exp_done = sem("exp_done")
        band_done = sem("band_done")
        pv_done = sem("pv_done")
        heads_kept = sem("heads_kept")
        recip_ready = sem("recip_ready")
        x_added = sem("x_added")
        stats_ready = sem("stats_ready")
        mv_ready = sem("mv_ready")
        mv_kept = sem("mv_kept")
        passed = sem("passed")

        band_rate = 1 if biased else 0
        per_half = PARTS + PARTS * PARTS
        half = HEADS // 2
        PAIRS = HEADS * TILES // 2

        def steps(eng, step, unrolled=2):
            for s in (-2, -1, 0):
                step(Step(s), s % 2, lambda stage, s=s: active(stage, s))
            with eng.Fori(0, (BATCH - 4) // unrolled) as reg:
                for i in range(unrolled):
                    step(Step(1 + i, unrolled, reg), (1 + i) % 2, lambda stage: True)
            for s in range(BATCH - 3, BATCH + 1):
                step(Step(s), s % 2, lambda stage, s=s: active(stage, s))

        with nc.Block() as block:
            @block.sync
            def _(sp):
                def load_stacks(which, h):
                    for i in range(PARTS):
                        row = i * PARTS * HEAD_DIM
                        rows = slice(row, row + PARTS * HEAD_DIM)
                        heads = slice(h * half, (h + 1) * half)
                        k_rows = parts_dram[1].rearrange("(h d) j n -> (d j) h n", d=HEAD_DIM)
                        q_rows = parts_dram[0].rearrange("(h d) j n -> d j h n", d=HEAD_DIM)
                        sp.dma_start(k_stack[which][rows, heads, :], k_rows[:, heads, :]).then_inc(stack_loaded[h], 16)
                        for j in range(PARTS):
                            dst = q_stack[which][row + j:row + j + PARTS * (HEAD_DIM - 1) + 1:PARTS, heads, :]
                            sp.dma_start(dst, q_rows[:, i, heads, :]).then_inc(stack_loaded[h], 16)

                def store_max(which, h, count):
                    sp.wait_ge(max_chain, count)
                    for i in range(PARTS):
                        sp.dma_start(q_stack[which][MAX_ROW + i:MAX_ROW + i + 1, h * half:(h + 1) * half, :],
                                     max_parts[:, i, :]).then_inc(max_stored[h], 16)

                def step(st, par, on):
                    if on("A"):
                        wait(sp, b_full, st.at(lambda s: HEADS * TILES * s))
                        load_stacks(1 - par, 1)
                    if on("B"):
                        store_max(par, 1, st.at(lambda s: 6 * s + 6))
                    if on("A"):
                        wait_apart(sp, stack_loaded[1], st.at(lambda s: 16 * per_half * (s + 2)), passed)
                    if on("front"):
                        for i in range(2):
                            sp.wait_ge(parts_ready, st.at(lambda s: 2 * (s + 2) + i + 1))
                            sp.dma_start(parts_dram[i], parts[i][:]).then_inc(parts_stored, 16)
                        wait_apart(sp, parts_stored, st.at(lambda s: 32 * (s + 3)), passed)
                        wait(sp, b_full, st.at(lambda s: HEADS * TILES * s + half * TILES))
                        load_stacks(par, 0)
                    if on("A"):
                        store_max(1 - par, 0, st.at(lambda s: 6 * (s + 1) + 3))
                    if on("front"):
                        wait_apart(sp, stack_loaded[0], st.at(lambda s: 16 * per_half * (s + 3)), passed)

                steps(sp, step)
                for h in range(2):
                    sp.wait_ge(stack_loaded[h], 16 * per_half * BATCH)
                    sp.wait_ge(max_stored[h], 16 * PARTS * BATCH)

            @block.tensor
            def _(pe):
                def use_spare(st, what):
                    wait(pe, spare_free, st.at(lambda s: spare_index(what)(s) - 1))

                def transposes(out, src, rows):
                    for t in range(TILES):
                        last = nc.tensor.transpose(out[0:rows, t * P:(t + 1) * P], src(t), ident[:])
                    return last

                def spare_use(st, what, par):
                    if what in ("max_lo", "max_hi"):
                        if what == "max_lo":
                            pe.wait_ge(max_taken, st.at(lambda s: PAIRS * (s + 1) + PAIRS // 2))
                            src = row_max[:, 0:half * TILES]
                        else:
                            pe.wait_ge(max_taken, st.at(lambda s: PAIRS * (s + 1)))
                            src = row_max[:, half * TILES:HEADS * TILES]
                        use_spare(st, what)
                        last = nc.tensor.transpose(spare[0:half * TILES, 0:P], src, ident[:])
                    elif what == "xT":
                        pe.wait_ge(x_normed, st.at(lambda s: s + 3))
                        use_spare(st, what)
                        last = transposes(spare, lambda t: x_norm[:, t, :], P)
                    elif what in ("q", "k", "v"):
                        use_spare(st, what)
                        if what == "v":
                            for t in range(TILES):
                                last = nc.tensor.matmul(spare[:, t * P:(t + 1) * P], x_normT[:, t * P:(t + 1) * P],
                                                        w_sb[:, 2, :], start=True, stop=True)
                        else:
                            last = nc.tensor.matmul(spare[:], w_sb[:, "qk".index(what), :], x_normT[:],
                                                    start=True, stop=True)
                    elif what[:-1] == "heads":
                        g = int(what[-1])
                        batch_of = (lambda s: s - 1) if g >= 2 else (lambda s: s)
                        pe.wait_ge(heads_kept, st.at(lambda s: GROUPS * batch_of(s) + g + 1))
                        use_spare(st, what)
                        last = transposes(spare, lambda t: heads_raw[g % 2][:, t * P:(t + 1) * P], P)
                    elif what == "outT":
                        use_spare(st, what)
                        last = transposes(spare, lambda t: heads_out[:, t, :], P)
                    elif what == "y":
                        use_spare(st, what)
                        for t in range(TILES):
                            last = nc.tensor.matmul(spare[:, t * P:(t + 1) * P], heads_outT[:, t * P:(t + 1) * P],
                                                    w_sb[:, 3, :], start=True, stop=True)
                    last.then_inc(spare_full, 1)

                def value_products(st, par, on, slot):
                    g, c = slot // GROUP - 1, slot % GROUP
                    if not (on("B") if g >= 0 else on("tail")):
                        return
                    g, lag, which = (g, 0, par) if g >= 0 else (GROUPS - 1, 1, 1 - par)
                    if c == 0:
                        if biased:
                            pe.wait_ge(band_done, st.at(lambda s: HEADS * (s - lag) + GROUP * (g + 1)))
                        else:
                            pe.wait_ge(exp_done, st.at(lambda s: TILES * (HEADS * (s - lag) + GROUP * (g + 1))))
                        pe.wait_ge(v_ready, st.at(lambda s: s - lag + 1))
                        wait(pe, heads_kept, st.at(lambda s: GROUPS * (s - lag) + g))
                    for j in range(GROUP):
                        h = GROUP * g + j
                        last = nc.tensor.matmul(o_ps[32 * j:32 * j + V_COLS, :], v_aug[which][:, c, h, :],
                                                probs[:, h % (2 * GROUP), c, :],
                                                start=(c == 0), stop=(c == TILES - 1))
                    last.then_inc(pv_done, 1)

                def step(st, par, on):
                    for slot in range(SLOTS):
                        if on("A") and slot % half == 0:
                            pe.wait_ge(stack_loaded[slot // half], st.at(lambda s: 16 * per_half * (s + 2)))
                        if on("B") and slot % half == 0:
                            pe.wait_ge(max_stored[slot // half], st.at(lambda s: 16 * PARTS * (s + 1)))
                        for c in range(TILES):
                            if on("A"):
                                if c % 2 == 0:
                                    wait(pe, max_taken, st.at(lambda s: PAIRS * (s + 1) + 2 * slot + c // 2 - 1))
                                last = nc.tensor.matmul(a_ps[:, c, :],
                                                        q_stack[1 - par][0:A_ROWS, slot, c * P:(c + 1) * P],
                                                        k_stack[1 - par][0:A_ROWS, slot, :], start=True, stop=True)
                                if c % 2 == 1:
                                    last.then_inc(a_full, 1)
                            if on("B"):
                                wait(pe, exp_done, st.at(lambda s: HEADS * TILES * s + TILES * slot + c - 1))
                                nc.tensor.matmul(b_ps[:, c % 2, :],
                                                 k_stack[par][0:B_ROWS, slot, c * P:(c + 1) * P],
                                                 q_stack[par][0:B_ROWS, slot, :],
                                                 start=True, stop=True).then_inc(b_full, 1)
                            if c == (TILES - 1 if slot % GROUP == 0 else 1):
                                value_products(st, par, on, slot)
                        for at, what, stage in SPARE_USES:
                            if at == slot and on(stage):
                                spare_use(st, what, par)

                steps(pe, step)

            @block.scalar
            def _(act):
                def split_high(st, i):
                    act.wait_ge(spare_free, st.at(spare_index("qk"[i])))
                    wait(act, parts_stored, st.at(lambda s: 32 * (s + 2)))
                    nc.scalar.activation(parts[i][:, 0, :], proj[:], ACT.Copy).then_inc(high_ready, 1)

                def split_mid(st, i):
                    n = lambda s: 2 * (s + 2) + i + 1
                    act.wait_ge(rest_ready, st.at(n))
                    nc.scalar.activation(parts[i][:, 1, :], rest[:], ACT.Copy).then_inc(mid_ready, 1)

                def spare_read(st, what):
                    if what == "xT":
                        act.wait_ge(spare_full, st.at(spare_index(what)))
                        nc.scalar.copy(x_normT[:], spare[:]).then_inc(spare_free, 1)
                    elif what in ("q", "k"):
                        i = "qk".index(what)
                        wait(act, rest_ready, st.at(lambda s: 2 * (s + 2) + i))
                        act.wait_ge(spare_full, st.at(spare_index(what)))
                        nc.scalar.activation(proj[:], spare[:], ACT.Identity, bias=qk_bias[:, i:i + 1],
                                             scale=(scale, 1.0)[i]).then_inc(spare_free, 1)
                    elif what == "outT":
                        act.wait_ge(spare_full, st.at(spare_index(what)))
                        nc.scalar.copy(heads_outT[:], spare[:]).then_inc(spare_free, 1)

                def side(st, what):
                    if what[1:] == "_high":
                        split_high(st, "qk".index(what[0]))
                    elif what[1:] == "_mid":
                        split_mid(st, "qk".index(what[0]))
                    else:
                        spare_read(st, what)

                def keep_heads(st, g, lag):
                    act.wait_ge(pv_done, st.at(lambda s: HEADS * (s - lag) + GROUP * (g + 1)))
                    before = ("heads2", "heads3", "heads0", "heads1")[g]
                    wait(act, spare_full, st.at(lambda s: spare_index(before)(s - lag)))
                    nc.scalar.copy(heads_raw[g % 2][:], o_ps[:]).then_inc(heads_kept, 1)

                def step(st, par, on):
                    for slot in range(SLOTS):
                        g = slot // GROUP - 2
                        if slot % GROUP == 0:
                            if g >= 0 and on("B"):
                                keep_heads(st, g, 0)
                            if g < 0 and on("tail"):
                                keep_heads(st, g + GROUPS, 1)
                        if on("B"):
                            wait(act, pv_done, st.at(lambda s: HEADS * s + GROUP * (slot // GROUP) - GROUP))
                        for c in range(TILES):
                            if on("B"):
                                act.wait_ge(b_full, st.at(lambda s: HEADS * TILES * s + TILES * slot + c + 1))
                                nc.scalar.activation(probs[:, slot % (2 * GROUP), c, :], b_ps[:, c % 2, :],
                                                     ACT.Exp).then_inc(exp_done, 1)
                            for at, tile, what, stage in SCALAR_SIDE:
                                if (at, tile) == (slot, c) and on(stage):
                                    side(st, what)

                steps(act, step)

            @block.gpsimd
            def _(pool):
                def rests(st, i):
                    n = lambda s: 2 * (s + 2) + i + 1
                    wait(pool, parts_ready, st.at(lambda s: 2 * (s + 2) + i))
                    pool.wait_ge(high_ready, st.at(n))
                    nc.gpsimd.tensor_tensor(rest[:], proj[:], parts[i][:, 0, :], ALU.subtract).then_inc(rest_ready, 1)

                def last_part(st, i):
                    n = lambda s: 2 * (s + 2) + i + 1
                    pool.wait_ge(mid_ready, st.at(n))
                    nc.gpsimd.tensor_tensor(parts[i][:, 2, :], rest[:], parts[i][:, 1, :],
                                            ALU.subtract).then_inc(parts_ready, 1)

                def step(st, par, on):
                    for slot in range(SLOTS):
                        if on("front") and slot in REST_SLOTS:
                            rests(st, REST_SLOTS[slot])
                        if on("front") and slot in LAST_PART_SLOTS:
                            last_part(st, LAST_PART_SLOTS[slot])
                        if biased and on("B"):
                            pool.wait_ge(exp_done, st.at(lambda s: TILES * (HEADS * s + slot + 1)))
                            flat = probs[:, slot % (2 * GROUP), :, :].rearrange("p c q -> p (c q)")
                            diagonal = SEQ + P
                            first = flat[:, 0:(TILES - 1) * diagonal].rearrange("p (c q) -> p c q", q=diagonal)
                            first = first[:, :, 0:BAND]
                            table = band[:, slot:slot + 1, :].broadcast_to([P, TILES - 1, BAND])
                            nc.gpsimd.tensor_tensor(first, first, table, ALU.mult)
                            final = flat[:, (TILES - 1) * diagonal:(TILES - 1) * diagonal + P]
                            nc.gpsimd.tensor_tensor(final, final, band[:, slot, 0:P],
                                                    ALU.mult).then_inc(band_done, 1)

                steps(pool, step)

            @block.vector
            def _(dve):
                def normalize(st):
                    wait(dve, spare_full, st.at(lambda s: spare_index("xT")(s - 1)))
                    x_b = tokens(x_sb, st.at(lambda s: TILES * (s + 2)))
                    mean = tokens(mv_all, st.at(lambda s: TILES * (s + 2)))
                    r = tokens(rstd, st.at(lambda s: TILES * (s + 2)))
                    for t in range(TILES):
                        last = nc.vector.tensor_scalar(x_norm[:, t, :], x_b[:, t, :], mean[:, t, 0:1], r[:, t:t + 1],
                                                       ALU.subtract, ALU.mult)
                    last.then_inc(x_normed, 1)

                def split_max(st, what, piece):
                    h = 0 if what == "max_lo" else 1
                    batch = (lambda s: s + 1) if h == 0 else (lambda s: s)
                    base = lambda s: 6 * batch(s) + 3 * h
                    scores_max = spare[0:half * TILES, 0:P]
                    if piece == 0:
                        wait(dve, max_stored[1 - h], st.at(lambda s: 16 * PARTS * (s + 1)))
                        dve.wait_ge(spare_full, st.at(spare_index(what)))
                        nc.vector.tensor_scalar(max_parts[:, 0, :], scores_max, -1.0, None,
                                                ALU.mult).then_inc(max_chain, 1)
                    elif piece == 1:
                        dve.wait_ge(max_chain, st.at(lambda s: base(s) + 1))
                        nc.vector.scalar_tensor_tensor(max_rest[:], scores_max, -1.0, max_parts[:, 0, :], ALU.mult,
                                                       ALU.subtract).then_inc(spare_free, 1)
                    elif piece == 2:
                        dve.wait_ge(spare_free, st.at(spare_index(what)))
                        nc.vector.tensor_copy(max_parts[:, 1, :], max_rest[:]).then_inc(max_chain, 1)
                    else:
                        dve.wait_ge(max_chain, st.at(lambda s: base(s) + 2))
                        nc.vector.tensor_tensor(max_parts[:, 2, :], max_rest[:], max_parts[:, 1, :],
                                                ALU.subtract).then_inc(max_chain, 1)

                def stage_values(st):
                    wait(dve, v_ready, st.at(lambda s: s + 2))
                    dve.wait_ge(spare_full, st.at(spare_index("v")))
                    v = spare[:].rearrange("p (t h d) -> p t h d", t=TILES, d=HEAD_DIM)
                    for t in range(TILES):
                        last = nc.vector.tensor_tensor(v_stage[:, t, :, 0:HEAD_DIM], v[:, t],
                                                       bv_rows[:].rearrange("p (h d) -> p h d", d=HEAD_DIM), ALU.add)
                    last.then_inc(spare_free, 1)

                def pass_values(st, par):
                    wait(dve, pv_done, st.at(lambda s: HEADS * s))
                    dve.wait_ge(spare_free, st.at(lambda s: spare_index("v")(s - 1)))
                    nc.vector.tensor_copy(v_aug[1 - par][:], v_stage[:]).then_inc(v_ready, 1)

                def finish_heads(st, what, piece):
                    g = int(what[-1])
                    lag = 1 if g >= 2 else 0
                    rows = spare[:].rearrange("p (t j r) -> p t j r", t=TILES, j=GROUP)
                    if piece == 0:
                        dve.wait_ge(spare_full, st.at(spare_index(what)))
                        nc.vector.reciprocal(recip[:], rows[:, :, :, HEAD_DIM:V_COLS]).then_inc(recip_ready, 1)
                    else:
                        if g == 0:
                            wait(dve, x_added, st.at(lambda s: s))
                        dve.wait_ge(recip_ready, st.at(lambda s: GROUPS * (s - lag) + g + 1))
                        out = heads_out[:, :, 32 * g:32 * g + 32].rearrange("p t (j d) -> p t j d", d=HEAD_DIM)
                        nc.vector.tensor_tensor(out, rows[:, :, :, 0:HEAD_DIM],
                                                recip[:].broadcast_to([P, TILES, GROUP, HEAD_DIM]),
                                                ALU.mult).then_inc(spare_free, 1)

                def add_to_x(st, piece):
                    x_b = tokens(x_sb, st.at(lambda s: TILES * (s - 1)))
                    if piece == 0:
                        dve.wait_ge(spare_full, st.at(spare_index("y")))
                        y = spare[:].rearrange("p (t e) -> p t e", e=EMBD)
                        bo = bo_rows[:].rearrange("p (o e) -> p o e", o=1).broadcast_to([P, TILES, EMBD])
                        nc.vector.tensor_tensor(heads_out[:], y, bo, ALU.add).then_inc(spare_free, 1)
                    elif piece == 1:
                        dve.wait_ge(spare_free, st.at(spare_index("y")))
                        nc.vector.tensor_tensor(x_b, x_b, heads_out[:], ALU.add).then_inc(x_added, 1)
                    elif piece == 2:
                        wait_apart(dve, x_added, st.at(lambda s: s), passed)
                        for t in range(TILES):
                            last = nc.vector.bn_stats(stats[:, t, :], x_b[:, t, :])
                        last.then_inc(stats_ready, 1)
                    elif piece == 3:
                        wait_apart(dve, stats_ready, st.at(lambda s: s), passed)
                        for t in range(TILES):
                            last = nc.vector.bn_aggr(mv[:, t, :], stats[:, t, :])
                        last.then_inc(mv_ready, 1)
                    else:
                        wait_apart(dve, mv_ready, st.at(lambda s: s), passed)
                        nc.vector.tensor_copy(tokens(mv_all, st.at(lambda s: TILES * (s - 1))),
                                              mv[:]).then_inc(mv_kept, 1)

                def side(st, par, what):
                    what, _, piece = what.partition(".")
                    if what == "normalize":
                        normalize(st)
                    elif what in ("max_lo", "max_hi"):
                        split_max(st, what, int(piece))
                    elif what == "v":
                        stage_values(st)
                    elif what == "v_aug":
                        pass_values(st, par)
                    elif what == "y":
                        add_to_x(st, int(piece))
                    else:
                        finish_heads(st, what, int(piece))

                def step(st, par, on):
                    for slot in range(SLOTS):
                        for i in range(2):
                            if on("A"):
                                dve.wait_ge(a_full, st.at(lambda s: PAIRS * (s + 1) + 2 * slot + i + 1))
                                nc.vector.reduce_max(row_max[:, TILES * slot + 2 * i:TILES * slot + 2 * i + 2],
                                                     a_ps[:, 2 * i:2 * i + 2, :], AX.X).then_inc(max_taken, 1)
                            for at, pair, what, stage in VECTOR_SIDE:
                                if (at, pair) == (slot, i) and on(stage):
                                    side(st, par, what)
                    if on("tail"):
                        dve.wait_ge(mv_kept, st.at(lambda s: s))

                steps(dve, step)


def setup_bias(nc, sems, tag, probs, work_a, work_b, q_stack, k_stack, band, rel_bias, spare):
    deltas = P - 1 + BAND
    bucket = bias_buckets(BAND)
    bucket = np.concatenate([np.full(P - 1, bucket[0]), bucket])
    edges = [0] + [i for i in range(1, deltas) if bucket[i] != bucket[i - 1]] + [deltas]
    with ExitStack() as ctx:
        def sb(name, shape, dt=F32):
            return ctx.enter_context(nc.sbuf_tensor(tag + name, shape, dt))

        def sem(name):
            return sems.new(tag + name)

        largest = sb("largest", [HEADS, 1])
        factors = work_a[0:HEADS, 0:deltas]
        by_head = work_b[0][0:HEADS, 0:BUCKETS]
        flip = work_b[1][:, 0:P]
        work = probs[:].rearrange("p a c q -> p (a c q)")
        const = work[0:HEADS, 0:TILES * SEQ].rearrange("p (c q) -> p c q", q=SEQ)
        rest = work[0:HEADS, TILES * SEQ:2 * TILES * SEQ].rearrange("p (c q) -> p c q", q=SEQ)
        const_parts = work[0:HEADS, 2 * TILES * SEQ:2 * TILES * SEQ + PARTS * TILES * SEQ // 2].bitcast(BF16)
        const_parts = const_parts.rearrange("p (i c q) -> p i c q", i=PARTS, q=SEQ)
        flipped = work[:, 8192:8192 + HEADS * BAND]
        tile_is = work[0:TILES, 12288:12288 + SEQ // 2].bitcast(BF16)
        factors_dram = nc.dram_tensor(tag + "factors_dram", (HEADS, deltas), F32, kind="Internal").ap()
        const_dram = nc.dram_tensor(tag + "const_dram", (HEADS, PARTS * TILES, SEQ), BF16, kind="Internal").ap()

        bias_loaded = sem("bias_loaded")
        chain = sem("bias_chain")
        run_ready = sem("run_ready")
        factors_ready = sem("factors_ready")
        factors_stored = sem("factors_stored")
        flipped_loaded = sem("flipped_loaded")
        const_ready = sem("const_ready")
        const_stored = sem("const_stored")
        stacks_filled = sem("stacks_filled")
        q_filled = sem("q_filled")
        rows_loaded = sem("rows_loaded")
        flip_steps = sem("flip_steps")
        tiles_marked = sem("tiles_marked")
        band_full = sem("band_full")
        band_kept = sem("band_kept")
        with nc.Block() as block:
            @block.sync
            def _(sp):
                with nc.allow_non_contiguous_dma("a table of 512 values, transposed"):
                    sp.dma_start(by_head, rel_bias.rearrange("b h -> h b")).then_inc(bias_loaded, 16)
                sp.wait_ge(factors_ready, 1)
                sp.dma_start(factors_dram, factors).then_inc(factors_stored, 16)
                sp.wait_ge(factors_stored, 16)
                windows = bass.AP(tensor=factors_dram.tensor, offset=factors_dram.offset,
                                  ap=[[1, P], [deltas, HEADS], [1, BAND]])
                sp.dma_start(flipped.rearrange("p (h q) -> p h q", q=BAND), windows).then_inc(flipped_loaded, 16)
                sp.wait_ge(const_ready, 1)
                sp.dma_start(const_dram.rearrange("h r q -> h (r q)"),
                             const_parts.rearrange("p i c q -> p (i c q)")).then_inc(const_stored, 16)
                sp.wait_ge(const_stored, 16)
                sp.wait_ge(stacks_filled, 2)
                sp.wait_ge(q_filled, 2)
                sp.wait_ge(tiles_marked, 2)
                for which in range(2):
                    sp.dma_start(q_stack[which][CONST_ROW:CONST_ROW + PARTS * TILES, :, :],
                                 const_dram.rearrange("h r q -> r h q")).then_inc(rows_loaded, 16)
                    for i in range(PARTS):
                        row = CONST_ROW + i * TILES
                        heads = tile_is.rearrange("p (o q) -> p o q", o=1).broadcast_to([TILES, HEADS, SEQ])
                        sp.dma_start(k_stack[which][row:row + TILES, :, :], heads).then_inc(rows_loaded, 16)
                sp.wait_ge(rows_loaded, 16 * 2 * (1 + PARTS))

            @block.gpsimd
            def _(pool):
                for i in range(2):
                    nc.gpsimd.memset(words(k_stack[i][64:MAX_ROW]), 0.0).then_inc(stacks_filled, 1)
                    pool.wait_ge(stacks_filled, i + 1)
                nc.gpsimd.memset(flip, 0.0).then_inc(flip_steps, 1)
                pool.wait_ge(flip_steps, 1)
                nc.gpsimd.affine_select(out=flip, in_=flip, compare_op=ALU.not_equal, fill=1.0, base=-(P - 1),
                                        pattern=[[1, P]], channel_multiplier=1).then_inc(flip_steps, 1)
                pool.wait_ge(flip_steps, 2)
                nc.gpsimd.memset(tile_is, 1.0).then_inc(flip_steps, 1)
                pool.wait_ge(flip_steps, 3)
                nc.gpsimd.affine_select(out=tile_is, in_=tile_is, compare_op=ALU.is_ge, fill=0.0, base=0,
                                        pattern=[[1, SEQ]], channel_multiplier=-P).then_inc(tiles_marked, 1)
                pool.wait_ge(tiles_marked, 1)
                nc.gpsimd.affine_select(out=tile_is, in_=tile_is, compare_op=ALU.is_ge, fill=0.0, base=P - 1,
                                        pattern=[[-1, SEQ]], channel_multiplier=P).then_inc(tiles_marked, 1)
                for i in range(2):
                    nc.gpsimd.memset(words(q_stack[i][64:MAX_ROW]), 0.0).then_inc(q_filled, 1)

            @block.scalar
            def _(act):
                act.wait_ge(run_ready, 1)
                nc.scalar.activation(factors, factors, ACT.Exp).then_inc(factors_ready, 1)
                for n in range(HEADS * BAND // SEQ):
                    act.wait_ge(band_full, n + 1)
                    nc.scalar.copy(band[:].rearrange("p h q -> p (h q)")[:, n * SEQ:(n + 1) * SEQ],
                                   spare[:]).then_inc(band_kept, 1)

            @block.tensor
            def _(pe):
                pe.wait_ge(flip_steps, 2)
                pe.wait_ge(flipped_loaded, 16)
                for n in range(HEADS * BAND // SEQ):
                    if n:
                        pe.wait_ge(band_kept, n)
                    nc.tensor.matmul(spare[:], flip, flipped[:, n * SEQ:(n + 1) * SEQ],
                                     start=True, stop=True).then_inc(band_full, 1)

            @block.vector
            def _(dve):
                links = [0]

                def link(instruction):
                    links[0] += 1
                    instruction.then_inc(chain, 1)
                    dve.wait_ge(chain, links[0])

                dve.wait_ge(bias_loaded, 16)
                link(nc.vector.tensor_scalar(by_head, by_head, 8.0, None, ALU.mult))
                link(nc.vector.reduce_max(largest[:], by_head, AX.X))
                link(nc.vector.tensor_scalar(by_head, by_head, largest[:], None, ALU.subtract))
                for lo, hi in zip(edges[:-1], edges[1:]):
                    b = int(bucket[lo])
                    last = nc.vector.tensor_copy(factors[:, lo:hi], by_head[:, b:b + 1].broadcast_to([HEADS, hi - lo]))
                last.then_inc(run_ready, 1)
                link(nc.vector.memset(const, 0.0))
                for c in range(TILES):
                    if c:
                        near = by_head[:, 0:1].broadcast_to([HEADS, c * P])
                        last = nc.vector.tensor_copy(const[:, c, 0:c * P], near)
                    if c * P + BAND < SEQ:
                        far = by_head[:, BUCKETS - 1:BUCKETS].broadcast_to([HEADS, SEQ - c * P - BAND])
                        last = nc.vector.tensor_copy(const[:, c, c * P + BAND:SEQ], far)
                link(last)
                link(nc.vector.tensor_copy(const_parts[:, 0], const))
                link(nc.vector.tensor_tensor(rest, const, const_parts[:, 0], ALU.subtract))
                link(nc.vector.tensor_copy(const_parts[:, 1], rest))
                nc.vector.tensor_tensor(const_parts[:, 2], rest, const_parts[:, 1],
                                        ALU.subtract).then_inc(const_ready, 1)


def ffn_phase(nc, sems, tag, x_sb, mv_all, rstd, ident, rows_dram, zeros_stored, gate_w, w1, b1, w2, b2, out_dram):
    with ExitStack() as ctx:
        def sb(name, shape, dt=F32):
            return ctx.enter_context(nc.sbuf_tensor(tag + name, shape, dt))

        def sem(name):
            return sems.new(tag + name)

        def ps(name, banks):
            return ctx.enter_context(nc.psum_tensor(tag + name, [P, banks, SEQ], F32))

        norm = Norm(nc, sems, ctx, tag, mv_all, rstd)
        w1_sb = sb("w1", [P, EXPERTS, FFN_DIM])
        w2_sb = sb("w2", [P, EXPERTS, FFN_CHUNKS, EMBD])
        b2_rows = sb("b2_rows", [P, EXPERTS, EMBD])
        small_rows = sb("small_rows", [EXPERTS + EXPERTS * FFN_CHUNKS, EMBD])
        small_cols = sb("small_cols", [P, EXPERTS + EXPERTS * FFN_CHUNKS])
        gate_sb = small_cols[:, 0:EXPERTS]
        b1_cols = small_cols[:, EXPERTS:].rearrange("p (e c) -> p e c", e=EXPERTS)
        before = sb("before", [P, P])
        ones = sb("ones", [P, P])
        first_wins = sb("first_wins", [P, EXPERTS])
        lower = sb("lower", [P, EXPERTS, EXPERTS])
        tile_starts = sb("tile_starts", [P, EXPERTS, max(CHUNK_TILES)])
        slot_tile_int = sb("slot_tile_int", [1, max(SLOT_TILES), EXPERTS], I32)
        slot_tile = sb("slot_tile", [1, max(SLOT_TILES), EXPERTS])
        ALL_TILES = BATCH * TILES
        row_space = sb("row_space", [P, ALL_TILES + 2 * CHUNK_TILES[0], EMBD])
        x_norm = row_space[:, 0:ALL_TILES, :]
        results_start = [ALL_TILES] + [2 * (CHUNK_START[c] - CHUNK_TILES[0]) for c in range(1, CHUNKS)]
        assert results_start[-1] + 2 * CHUNK_TILES[-1] <= ALL_TILES + 2 * CHUNK_TILES[0]
        x_normT = sb("x_normT", [P, 2, SEQ])
        shape = [P, ALL_TILES, EXPERTS]
        top = sb("top", [P, ALL_TILES, 1])
        prob, left, key, counts_a, counts_b, place = [sb(n, shape) for n in (
            "prob", "left", "key", "counts_a", "counts_b", "place")]
        pick = [sb(f"pick{i}", shape) for i in range(2)]
        filled_tiles = sb("filled_tiles", [P, CHUNKS, EXPERTS, max(CHUNK_TILES)])
        tiles_of = sb("tiles_of", [P, CHUNKS, EXPERTS])
        tiles_lower = sb("tiles_lower", [P, CHUNKS, EXPERTS, EXPERTS])
        first_tile = sb("first_tile", [P, CHUNKS, EXPERTS])
        end_tile = sb("end_tile", [P, CHUNKS, EXPERTS])
        past = sb("past", [1, SLOT_START[-1], EXPERTS])
        expert_f = sb("expert_f", [1, SLOT_START[-1]])
        expert_of = sb("expert_of", [1, SLOT_START[-1]], I32)
        slot_f = sb("slot_f", [P, 2, ALL_TILES])
        slot_of = sb("slot_of", [P, 2, ALL_TILES], I32)
        gates = sb("gates", [P, 2, ALL_TILES])
        xs = sb("xs", [P, RING, EMBD])
        xsT = sb("xsT", [P, 2, P])
        w1_now = sb("w1_now", [P, 2, FFN_DIM])
        hiddenT = sb("hiddenT", [P, 2, FFN_DIM])
        ys = sb("ys", [P, RING, EMBD])
        stats = sb("stats", [P, max(CHUNK_TILES), 6])
        xT_ps, gate_ps = ps("xT_ps", 1), ps("gate_ps", 1)
        count_ps, up_ps, down_ps = ps("count_ps", 2), ps("up_ps", 2), ps("down_ps", 2)
        xs_dram, ys_dram = rows_dram

        weights_loaded = [sem(f"weights_loaded{e}") for e in range(EXPERTS)]
        small_loaded = sem("small_loaded")
        bias_loaded = sem("bias_loaded")
        gate_full = sem("gate_full")
        gate_kept = sem("gate_kept")
        marks = sem("marks")
        marks_v = sem("marks_v")
        x_normed = sem("x_normed")
        xT_full = sem("xT_full")
        xT_kept = sem("xT_kept")
        logits_full = sem("logits_full")
        logits_less = sem("logits_less")
        gate_exp = sem("gate_exp")
        chain = sem("chain")
        picked = sem("picked")
        counted = sem("counted")
        routed = sem("routed")
        experts_ready = sem("experts_ready")
        scattered = [sem(f"scattered{c}") for c in range(CHUNKS)]
        gathered = [sem(f"gathered{c}") for c in range(CHUNKS)]
        xs_loaded = [sem(f"xs_loaded{i}") for i in range(RING)]
        ys_stored = [sem(f"ys_stored{i}") for i in range(RING)]
        w1_ready = sem("w1_ready")
        up_full = sem("up_full")
        relu_done = sem("relu_done")
        down_full = sem("down_full")
        ys_ready = sem("ys_ready")
        combined = sem("combined")
        out_stored = sem("out_stored")
        passed = sem("passed")

        FRONTS = [(0, 1), (1, CHUNKS)]
        front_ps = [(gate_ps[:, 0], count_ps[:, 0], count_ps[:, 1]), (down_ps[:, 0], up_ps[:, 0], up_ps[:, 1])]

        xT_banks = [xT_ps[:, 0], down_ps[:, 1]]

        def front_batches(f):
            return [CHUNK_START[c] // TILES for c in FRONTS[f]]

        xT_before = [BATCH + n for n in SLOT_START]

        def result(c, i, t):
            return row_space[:, results_start[c] + i * CHUNK_TILES[c] + t, :]

        def slot_steps(c, step, begin=lambda c, st, s0: None):
            first, last = RING + 2, SLOT_TILES[c] - 1 - AHEAD
            assert (last - first + 1) % RING == 0

            def on_at(s):
                return lambda ahead: 0 <= s + ahead < SLOT_TILES[c]
            def run(eng):
                for s in range(-2, first):
                    if (s + 2) % RING == 0:
                        begin(c, Step(s), s)
                    step(eng, c, Step(s), s, on_at(s))
                with eng.Fori(0, (last - first + 1) // RING) as reg:
                    begin(c, Step(first, RING, reg), first)
                    for i in range(RING):
                        step(eng, c, Step(first + i, RING, reg), first + i, lambda ahead: True)
                for s in range(last + 1, SLOT_TILES[c] + 1):
                    if (s - last - 1) % RING == 0:
                        begin(c, Step(s), s)
                    step(eng, c, Step(s), s, on_at(s))
            return run

        def number(c, ahead):
            return lambda s: SLOT_START[c] + s + ahead

        def ring_before(c, ahead, buffer):
            return lambda s: (number(c, ahead)(s) - buffer) // RING

        def experts(engine, c, st, s0, ahead):
            steps = [s for s in range(s0, s0 + RING) if st.reg is not None or 0 <= s + ahead < SLOT_TILES[c]]
            if not steps:
                return {}
            n = st.at(lambda s: number(c, ahead)(s) + steps[0] - s0)
            _, values = nc.values_load_multi_w_load_instructions(
                expert_of[0:1, bass.ds(n, len(steps))], engines=[engine],
                min_val=0, max_val=EXPERTS - 1,
                skip_runtime_bounds_check_because="a count of experts, at least 0, of which find_experts() takes "
                                                  "the minimum with the last expert")
            return dict(zip(steps, values))

        with nc.Block() as block:
            @block.sync
            def _(sp):
                sp.dma_start(small_rows[0:EXPERTS, :], gate_w).then_inc(small_loaded, 16)
                sp.dma_start(small_rows[EXPERTS:, :], b1.rearrange("e (c f) -> (e c) f", f=P)
                             ).then_inc(small_loaded, 16)
                sp.dma_start(b2_rows[:], b2.partition_broadcast(P)).then_inc(bias_loaded, 16)
                for e in range(EXPERTS):
                    sp.dma_start(w1_sb[:, e, :], w1[e]).then_inc(weights_loaded[e], 16)
                    sp.dma_start(w2_sb[:, e, :, :], w2[e].rearrange("(c f) n -> f c n", f=P)
                                 ).then_inc(weights_loaded[e], 16)

                def dram_rows(dram, st, c, ahead):
                    n = st.at(lambda s: s + ahead)
                    tiles = dram[c % 2].rearrange("(s p) e -> s p e", p=P)
                    return tiles[n] if isinstance(n, int) else tiles[bass.ds(n, 1)].rearrange("o p e -> (o p) e")

                def load(st, c, ahead, buffer):
                    sp.dma_start(xs[:, buffer, :], dram_rows(xs_dram, st, c, ahead)).then_inc(xs_loaded[buffer], 16)

                def step(eng, c, st, s0, on):
                    if on(AHEAD):
                        sp.wait_ge(xT_full, st.at(lambda s: xT_before[c] + s + AHEAD - RING + 1))
                        load(st, c, AHEAD, number(c, AHEAD)(s0) % RING)
                    if on(-1):
                        buffer = number(c, -1)(s0) % RING
                        sp.wait_ge(ys_ready, st.at(lambda s: number(c, -1)(s) + 1))
                        sp.dma_start(dram_rows(ys_dram, st, c, -1), ys[:, buffer, :]).then_inc(ys_stored[buffer], 16)

                for c in range(CHUNKS):
                    sp.wait_ge(scattered[c], 16 * 2 * CHUNK_TILES[c])
                    if c >= 2:
                        sp.wait_ge(gathered[c - 2], 16 * 2 * CHUNK_TILES[c - 2])
                    if c:
                        sp.wait_ge(xT_full, xT_before[c])
                    for s in range(AHEAD - 2):
                        load(Step(s), c, 0, number(c, 0)(s) % RING)
                    slot_steps(c, step)(sp)
                for i in range(RING):
                    sp.wait_ge(ys_stored[i], 16 * ((SLOT_START[-1] + RING - 1 - i) // RING))
                if out_dram is not None:
                    out_tiles = out_dram.rearrange("b (t p) e -> p (b t) e", p=P)
                    for c in range(CHUNKS):
                        sp.wait_ge(combined, c + 1)
                        span = slice(CHUNK_START[c], CHUNK_START[c + 1])
                        sp.dma_start(out_tiles[:, span, :], x_sb[:, span, :]).then_inc(out_stored, 16)
                    sp.wait_ge(out_stored, 16 * CHUNKS)

            @block.gpsimd
            def _(pool):
                links = [0]

                def link(instruction):
                    links[0] += 1
                    instruction.then_inc(marks, 1)
                    pool.wait_ge(marks, links[0])

                link(nc.gpsimd.memset(ones[:], 1.0))
                link(nc.gpsimd.memset(before[:], 1.0))
                link(nc.gpsimd.affine_select(out=before[:], in_=before[:], compare_op=ALU.is_gt, fill=0.0, base=0,
                                             pattern=[[1, P]], channel_multiplier=-1))
                link(nc.gpsimd.iota(slot_tile_int[:], [[1, max(SLOT_TILES)], [0, EXPERTS]], base=0, channel_multiplier=0))

                def slots(c, i, t):
                    n = CHUNK_START[c] + t
                    return slot_of[:, i, n:n + 1]

                def scatter(c):
                    pool.wait_ge(routed, min(c, 1) + 1)
                    for t in range(CHUNK_TILES[c]):
                        for i in range(2):
                            nc.gpsimd.indirect_dma_start(
                                out=xs_dram[c % 2], in_=x_norm[:, CHUNK_START[c] + t, :], in_offset=None,
                                out_offset=bass.IndirectOffsetOnAxis(ap=slots(c, i, t), axis=0)
                            ).then_inc(scattered[c], 16)

                def gather(c):
                    for i in range(RING):
                        pool.wait_ge(ys_stored[i], 16 * ((SLOT_START[c + 1] + RING - 1 - i) // RING))
                    if c == 1:
                        for later in range(1, CHUNKS):
                            pool.wait_ge(scattered[later], 16 * 2 * CHUNK_TILES[later])
                    if c and results_start[c] + 2 * CHUNK_TILES[c] > ALL_TILES:
                        pool.wait_ge(combined, 1)
                    for t in range(CHUNK_TILES[c]):
                        for i in range(2):
                            nc.gpsimd.indirect_dma_start(
                                out=result(c, i, t), out_offset=None, in_=ys_dram[c % 2],
                                in_offset=bass.IndirectOffsetOnAxis(ap=slots(c, i, t), axis=0)
                            ).then_inc(gathered[c], 16)

                pool.wait_ge(x_normed, BATCH)
                if zeros_stored is not None:
                    pool.wait_ge(zeros_stored, 32)
                scatter(0)
                scatter(1)
                for c in range(CHUNKS):
                    gather(c)
                    if c + 2 < CHUNKS:
                        scatter(c + 2)

            @block.tensor
            def _(pe):
                pe.wait_ge(small_loaded, 32)
                n = small_rows.shape[0]
                nc.tensor.transpose(gate_ps[:, 0, 0:n], small_rows[:], ident[0:n, 0:n]).then_inc(gate_full, 1)
                pe.wait_ge(gate_kept, 1)
                pe.wait_ge(marks, 4)

                def transposes(q):
                    pe.wait_ge(x_normed, q + 1)
                    wait(pe, xT_kept, q - 1)
                    for t in range(TILES):
                        last = nc.tensor.transpose(xT_banks[q % 2][:, t * P:(t + 1) * P],
                                                   x_norm[:, q * TILES + t, :], ident[:])
                    last.then_inc(xT_full, 1)

                def logits(q):
                    f = 0 if q < front_batches(0)[1] else 1
                    pe.wait_ge(xT_kept, q + 1)
                    for t in range(TILES):
                        col = ((q - front_batches(f)[0]) * TILES + t) * EXPERTS
                        last = nc.tensor.matmul(front_ps[f][0][:, col:col + EXPERTS],
                                                x_normT[:, q % 2, t * P:(t + 1) * P], gate_sb,
                                                start=True, stop=True)
                    last.then_inc(logits_full, 1)

                def count_rows(f):
                    _, in_front, in_tile = front_ps[f]
                    lo, hi = front_batches(f)
                    pe.wait_ge(picked, f + 1)
                    choices = key[:, lo * TILES:hi * TILES, :].rearrange("p t e -> p (t e)")
                    n = (hi - lo) * TILES * EXPERTS
                    nc.tensor.matmul(in_front[:, 0:n], before[:], choices, start=True, stop=True)
                    nc.tensor.matmul(in_tile[:, 0:n], ones[:], choices, start=True, stop=True).then_inc(counted, 1)

                down_expert = {}

                def begin(c, st, s0):
                    down_expert.update(experts(mybir.EngineType.PE, c, st, s0, -1))

                def step(eng, c, st, s0, on):
                    if on(2) or on(1):
                        pe.wait_ge(xT_kept, st.at(lambda s: xT_before[c] + s + 2))
                    if on(2):
                        buffer = number(c, 2)(s0) % RING
                        pe.wait_ge(xs_loaded[buffer], st.at(lambda s: 16 * (ring_before(c, 2, buffer)(s) + 1)))
                        nc.tensor.transpose(xT_ps[:, 0, 0:P], xs[:, buffer, :], ident[:]).then_inc(xT_full, 1)
                    if on(1):
                        parity = number(c, 1)(s0) % 2
                        pe.wait_ge(w1_ready, st.at(lambda s: number(c, 1)(s) + 1))
                        wait(pe, relu_done, st.at(lambda s: number(c, 1)(s) - 1))
                        for f in range(FFN_CHUNKS):
                            span = slice(f * P, (f + 1) * P)
                            last = nc.tensor.matmul(up_ps[:, parity, span], w1_now[:, parity, span],
                                                    xsT[:, parity, :], start=True, stop=True)
                        last.then_inc(up_full, 1)
                    if on(-1):
                        parity, e = number(c, -1)(s0) % 2, down_expert[s0]
                        if not on(1):
                            pe.wait_ge(relu_done, st.at(lambda s: number(c, -1)(s) + 1))
                        wait(pe, ys_ready, st.at(lambda s: number(c, -1)(s) - 1))
                        for f in range(FFN_CHUNKS):
                            last = nc.tensor.matmul(down_ps[:, parity, 0:EMBD], hiddenT[:, parity, f * P:(f + 1) * P],
                                                    w2_sb[:, bass.ds(e, 1), f, :].rearrange("p o n -> p (o n)"),
                                                    start=(f == 0), stop=(f == FFN_CHUNKS - 1))
                        last.then_inc(down_full, 1)

                for q in range(BATCH + 1):
                    if q < BATCH:
                        transposes(q)
                    if q:
                        logits(q - 1)
                    if q == front_batches(0)[1] + 3:
                        count_rows(0)
                count_rows(1)
                for e in range(EXPERTS):
                    pe.wait_ge(weights_loaded[e], 32)
                pe.wait_ge(experts_ready, 1)
                for c in range(CHUNKS):
                    slot_steps(c, step, begin)(pe)

            @block.scalar
            def _(act):
                norm.on_scalar(act)

                def exponentials(f):
                    act.wait_ge(logits_less, f + 1)
                    lo, hi = [b * TILES for b in front_batches(f)]
                    nc.scalar.activation(prob[:, lo:hi, :], left[:, lo:hi, :], ACT.Exp).then_inc(gate_exp, 1)

                up_expert = {}

                def begin(c, st, s0):
                    up_expert.update(experts(mybir.EngineType.Activation, c, st, s0, 1))

                def step(eng, c, st, s0, on):
                    if on(2):
                        parity = number(c, 2)(s0) % 2
                        act.wait_ge(xT_full, st.at(lambda s: xT_before[c] + s + 3))
                        wait(act, up_full, st.at(lambda s: number(c, 2)(s) - 1))
                        nc.scalar.copy(xsT[:, parity, :], xT_ps[:, 0, 0:P]).then_inc(xT_kept, 1)
                    if on(1):
                        parity, e = number(c, 1)(s0) % 2, up_expert[s0]
                        act.wait_ge(up_full, st.at(lambda s: number(c, 1)(s) + 1))
                        wait(act, down_full, st.at(lambda s: number(c, 1)(s) - 1))
                        for f in range(FFN_CHUNKS):
                            span = slice(f * P, (f + 1) * P)
                            last = nc.scalar.activation(hiddenT[:, parity, span], up_ps[:, parity, span], ACT.Relu,
                                                        bias=b1_cols[:, bass.ds(e, 1), f])
                        last.then_inc(relu_done, 1)

                for q in range(BATCH):
                    wait(act, logits_full, q - 1)
                    act.wait_ge(xT_full, q + 1)
                    nc.scalar.copy(x_normT[:, q % 2, :], xT_banks[q % 2]).then_inc(xT_kept, 1)
                    if q == front_batches(0)[1]:
                        exponentials(0)
                exponentials(1)
                act.wait_ge(experts_ready, 1)
                for c in range(CHUNKS):
                    slot_steps(c, step, begin)(act)

            @block.vector
            def _(dve):
                norm.on_vector(dve)
                links = [0]

                def link(instruction):
                    links[0] += 1
                    instruction.then_inc(chain, 1)
                    dve.wait_ge(chain, links[0])

                dve.wait_ge(gate_full, 1)
                nc.vector.tensor_copy(small_cols[:], gate_ps[:, 0, 0:small_cols.shape[1]]).then_inc(gate_kept, 1)
                dve.wait_ge(marks, 4)
                nc.vector.tensor_copy(slot_tile[:], slot_tile_int[:])
                for e in range(EXPERTS):
                    nc.vector.memset(first_wins[:, e:e + 1], float(EXPERTS - e))
                    if e:
                        nc.vector.memset(lower[:, e, 0:e], 1.0)
                    nc.vector.memset(lower[:, e, e:EXPERTS], 0.0)
                for t in range(max(CHUNK_TILES)):
                    last = nc.vector.memset(tile_starts[:, :, t:t + 1], float(P * t))
                link(last)

                def front(f):
                    lo, hi = [b * TILES for b in front_batches(f)]
                    tiles, chunks = hi - lo, range(*FRONTS[f])
                    spans = {c: slice(CHUNK_START[c], CHUNK_START[c + 1]) for c in chunks}
                    part = [P, tiles, EXPERTS]
                    logits, in_front, in_tile = [b[:, 0:tiles * EXPERTS].rearrange("p (t e) -> p t e", e=EXPERTS)
                                                 for b in front_ps[f]]
                    prob_, left_, key_, place_ = [v[:, lo:hi, :] for v in (prob, left, key, place)]
                    pick_ = [v[:, lo:hi, :] for v in pick]
                    top_ = top[:, lo:hi, :]
                    best = top[:, lo:hi, 0]

                    def spread(v):
                        return v.broadcast_to(part)

                    wins = first_wins[:].rearrange("p (o e) -> p o e", o=1).broadcast_to(part)
                    dve.wait_ge(logits_full, hi // TILES)
                    link(nc.vector.reduce_max(best, logits, AX.X))
                    nc.vector.tensor_tensor(left_, logits, spread(top_), ALU.subtract).then_inc(logits_less, 1)
                    dve.wait_ge(gate_exp, f + 1)
                    link(nc.vector.reduce_sum(best, prob_, AX.X))
                    link(nc.vector.reciprocal(best, best))
                    link(nc.vector.tensor_tensor(prob_, prob_, spread(top_), ALU.mult))
                    for i, p in enumerate((prob_, left_)):
                        if i:
                            link(nc.vector.scalar_tensor_tensor(left_, pick_[0], -4.0, prob_, ALU.mult, ALU.add))
                        link(nc.vector.reduce_max(best, p, AX.X))
                        nc.vector.tensor_copy(gates[:, i, lo:hi], best)
                        link(nc.vector.tensor_tensor(key_, p, spread(top_), ALU.is_equal))
                        link(nc.vector.tensor_tensor(key_, key_, wins, ALU.mult))
                        link(nc.vector.reduce_max(best, key_, AX.X))
                        link(nc.vector.tensor_tensor(pick_[i], key_, spread(top_), ALU.is_equal))
                    nc.vector.tensor_tensor(key_, pick_[0], pick_[1], ALU.add).then_inc(picked, 1)
                    dve.wait_ge(counted, f + 1)
                    link(nc.vector.tensor_copy(counts_a[:, lo:hi, :], in_tile))
                    sums, reach = {c: (counts_a[:, spans[c], :], counts_b[:, spans[c], :]) for c in chunks}, 1
                    while reach < max(CHUNK_TILES[c] for c in chunks):
                        for c in chunks:
                            a, b = sums[c]
                            if reach < CHUNK_TILES[c]:
                                nc.vector.tensor_copy(b[:, 0:reach, :], a[:, 0:reach, :])
                                last = nc.vector.tensor_tensor(b[:, reach:, :], a[:, reach:, :],
                                                               a[:, 0:CHUNK_TILES[c] - reach, :], ALU.add)
                                sums[c] = b, a
                        link(last)
                        reach *= 2
                    for c in chunks:
                        own = in_tile[:, CHUNK_START[c] - lo:CHUNK_START[c + 1] - lo, :]
                        last = nc.vector.tensor_tensor(place[:, spans[c], :], sums[c][0], own, ALU.subtract)
                    link(last)
                    link(nc.vector.tensor_tensor(place_, place_, in_front, ALU.add))
                    for c in chunks:
                        n = CHUNK_TILES[c]
                        total = sums[c][0][:, n - 1, :].rearrange("p (e o) -> p e o", o=1)
                        last = nc.vector.tensor_tensor(filled_tiles[:, c, :, 0:n], total.broadcast_to([P, EXPERTS, n]),
                                                       tile_starts[:, :, 0:n], ALU.is_gt)
                    link(last)
                    for c in chunks:
                        last = nc.vector.reduce_sum(tiles_of[:, c, :], filled_tiles[:, c, :, 0:CHUNK_TILES[c]], AX.X)
                    link(last)
                    for c in chunks:
                        others = tiles_of[:, c:c + 1, :].broadcast_to([P, EXPERTS, EXPERTS])
                        last = nc.vector.tensor_tensor(tiles_lower[:, c], lower[:], others, ALU.mult)
                    link(last)
                    c0, c1 = FRONTS[f]
                    link(nc.vector.reduce_sum(first_tile[:, c0:c1, :], tiles_lower[:, c0:c1], AX.X))
                    link(nc.vector.tensor_tensor(end_tile[:, c0:c1, :], first_tile[:, c0:c1, :], tiles_of[:, c0:c1, :],
                                                 ALU.add))
                    for c in chunks:
                        firsts = first_tile[:, c:c + 1, :].broadcast_to([P, CHUNK_TILES[c], EXPERTS])
                        last = nc.vector.scalar_tensor_tensor(place[:, spans[c], :], firsts, float(P),
                                                              place[:, spans[c], :], ALU.mult, ALU.add)
                    link(last)
                    for i in range(2):
                        link(nc.vector.tensor_tensor(key_, pick_[i], place_, ALU.mult))
                        link(nc.vector.reduce_sum(slot_f[:, i, lo:hi], key_, AX.X))
                    nc.vector.tensor_copy(slot_of[:, :, lo:hi], slot_f[:, :, lo:hi]).then_inc(routed, 1)
                    dve.wait_ge(routed, f + 1)

                def find_experts():
                    for c in range(CHUNKS):
                        ends = end_tile[0:1, c:c + 1, :].broadcast_to([1, SLOT_TILES[c], EXPERTS])
                        last = nc.vector.tensor_tensor(past[:, SLOT_START[c]:SLOT_START[c + 1], :],
                                                       slot_tile[:, 0:SLOT_TILES[c], :], ends, ALU.is_ge)
                    link(last)
                    link(nc.vector.reduce_sum(expert_f[:], past[:], AX.X))
                    nc.vector.tensor_scalar(expert_of[:], expert_f[:], float(EXPERTS - 1), None,
                                            ALU.min).then_inc(experts_ready, 1)
                    dve.wait_ge(experts_ready, 1)

                next_expert, down_expert = {}, {}

                def begin(c, st, s0):
                    next_expert.update(experts(mybir.EngineType.DVE, c, st, s0, 2))
                    down_expert.update(experts(mybir.EngineType.DVE, c, st, s0, -1))

                def step(eng, c, st, s0, on):
                    if on(2):
                        parity, e = number(c, 2)(s0) % 2, next_expert[s0]
                        wait(dve, up_full, st.at(lambda s: number(c, 2)(s) - 1))
                        nc.vector.tensor_copy(w1_now[:, parity, :], w1_sb[:, bass.ds(e, 1), :].rearrange(
                            "p o n -> p (o n)")).then_inc(w1_ready, 1)
                    if on(-1):
                        parity, buffer, e = number(c, -1)(s0) % 2, number(c, -1)(s0) % RING, down_expert[s0]
                        wait(dve, ys_stored[buffer], st.at(lambda s: 16 * ring_before(c, -1, buffer)(s)))
                        dve.wait_ge(down_full, st.at(lambda s: number(c, -1)(s) + 1))
                        nc.vector.tensor_tensor(ys[:, buffer, :], down_ps[:, parity, 0:EMBD],
                                                b2_rows[:, bass.ds(e, 1), :].rearrange("p o n -> p (o n)"),
                                                ALU.add).then_inc(ys_ready, 1)

                def combine(c, part):
                    tiles = range(CHUNK_START[c], CHUNK_START[c + 1])
                    quarter, half = len(tiles) // 4, len(tiles) // 2
                    if part == 0:
                        dve.wait_ge(gathered[c], 16 * 2 * len(tiles))
                    if part < 8:
                        i, q = part // 4, part % 4 * quarter
                        for t in range(q, q + quarter):
                            n = tiles[t]
                            last = nc.vector.scalar_tensor_tensor(x_sb[:, n, :], result(c, i, t),
                                                                  gates[:, i, n:n + 1], x_sb[:, n, :],
                                                                  ALU.mult, ALU.add)
                        if part == 7:
                            last.then_inc(combined, 1)
                            dve.wait_ge(combined, c + 1)
                        else:
                            link(last)
                    elif out_dram is None:
                        h = part % 2 * half
                        for t in range(h, h + half):
                            n = tiles[t]
                            if part < 10:
                                last = nc.vector.bn_stats(stats[:, t, :], x_sb[:, n, :])
                            else:
                                last = nc.vector.bn_aggr(mv_all[:, n, :], stats[:, t, :])
                        link(last)

                def step_and_combine(eng, c, st, s0, on):
                    step(eng, c, st, s0, on)
                    at_end = COMBINE_PARTS // 2
                    if c == 1 and st.reg is None and s0 > SLOT_TILES[c] - at_end:
                        combine(0, s0 - (SLOT_TILES[c] + 1 - at_end))
                    if c == 2 and st.reg is None and 0 <= s0 < COMBINE_PARTS - at_end:
                        combine(0, at_end + s0)

                for t in range(ALL_TILES):
                    last = nc.vector.tensor_scalar(x_norm[:, t, :], x_sb[:, t, :], mv_all[:, t, 0:1],
                                                   rstd[:, t:t + 1], ALU.subtract, ALU.mult)
                    if t % TILES == TILES - 1:
                        last.then_inc(x_normed, 1)
                front(0)
                front(1)
                find_experts()
                dve.wait_ge(bias_loaded, 16)
                for e in range(EXPERTS):
                    dve.wait_ge(weights_loaded[e], 32)
                for c in range(CHUNKS):
                    slot_steps(c, step_and_combine, begin)(dve)
                for c in range(1, CHUNKS):
                    for part in range(COMBINE_PARTS):
                        combine(c, part)


def hybrid(nc, x, wq, bq, wk, bk, wv, bv, wo, bo, rel_bias, wqkv, bqkv, wout, bout, gate_w, w1, b1, w2, b2, out):
    sems = Sems(nc)
    with ExitStack() as ctx:
        x_sb = ctx.enter_context(nc.sbuf_tensor("x_sb", [P, BATCH * TILES, EMBD], F32))
        mv_all = ctx.enter_context(nc.sbuf_tensor("mv_all", [P, BATCH * TILES, 2], F32))
        rstd = ctx.enter_context(nc.sbuf_tensor("rstd", [P, BATCH * TILES], F32))
        ident = ctx.enter_context(nc.sbuf_tensor("ident", [P, P], F32))

        def column(v):
            return v.rearrange("(e o) -> e o", o=1)

        def rows(v):
            return v.partition_broadcast(P)

        def by_head(v, which):
            part = slice(which * HEAD_DIM, (which + 1) * HEAD_DIM)
            if len(v.shape) == 2:
                return v.rearrange("e (h c) -> e h c", h=HEADS)[:, :, part]
            return v.rearrange("(h c) -> h c", h=HEADS)[:, part]

        rows_dram = [[nc.dram_tensor(f"{n}_dram{i}", (max(SLOT_TILES[i::2]) * P, EMBD), F32, kind="Internal").ap()
                      for i in range(2)] for n in ("sorted", "results")]
        zeros = ctx.enter_context(nc.sbuf_tensor("zeros", [P, 1, EMBD], F32))
        zeros_stored = nc.alloc_semaphore("zeros_stored")
        load_phase(nc, sems, x, x_sb, mv_all, ident, rows_dram[0], zeros, zeros_stored)
        sems.clear()
        attention_phase(nc, sems, "aa_", x_sb, mv_all, rstd, ident,
                        dict(wq=wq, wk=wk, wv=wv, wo=wo, bq=column(bq), bk=column(bk), bv=rows(bv), bo=rows(bo)),
                        rel_bias)
        sems.clear()
        ffn_phase(nc, sems, "f1_", x_sb, mv_all, rstd, ident, rows_dram, zeros_stored, gate_w, w1, b1, w2, b2, None)
        sems.held.append(zeros_stored)
        sems.clear()
        with nc.allow_non_contiguous_dma("q and k biases, one value per partition"):
            attention_phase(nc, sems, "ab_", x_sb, mv_all, rstd, ident,
                            dict(wq=by_head(wqkv, 0), wk=by_head(wqkv, 1), wv=by_head(wqkv, 2), wo=wout,
                                 bq=by_head(bqkv, 0), bk=by_head(bqkv, 1), bv=rows(by_head(bqkv, 2)), bo=rows(bout)),
                            None)
        sems.clear()
        ffn_phase(nc, sems, "f2_", x_sb, mv_all, rstd, ident, rows_dram, None, gate_w, w1, b1, w2, b2, out)
        sems.clear()


_INS = ["L0_attn_a_hidden_states", "L0_attn_a_Wq", "L0_attn_a_bq", "L0_attn_a_Wk", "L0_attn_a_bk", "L0_attn_a_Wv",
        "L0_attn_a_bv", "L0_attn_a_Wo", "L0_attn_a_bo", "L0_attn_a_rel_bias", "L0_attn_b_Wqkv", "L0_attn_b_bqkv",
        "L0_attn_b_Wout", "L0_attn_b_bout", "L0_ffn_gate_w", "L0_ffn_w1", "L0_ffn_b1", "L0_ffn_w2", "L0_ffn_b2"]


def kernel(**inputs):
    import numpy as _np
    import concourse.bacc as _bacc
    from concourse import mybir as _mybir
    from concourse.bass_utils import run_bass_kernel_spmd as _run

    nc = _bacc.Bacc("TRN2", target_bir_lowering=False, num_devices=1)
    arrays, args = {}, []
    for name in _INS:
        a = _np.ascontiguousarray(inputs[name])
        arrays[f"in_{name}"] = a
        args.append(nc.dram_tensor(f"in_{name}", a.shape, _mybir.dt.from_np(a.dtype), kind="ExternalInput").ap())
    out = nc.dram_tensor("out_0", (BATCH, SEQ, EMBD), _mybir.dt.from_np(_np.dtype("float32")),
                         kind="ExternalOutput").ap()
    hybrid(nc, *args, out)
    r = _run(nc, [arrays], core_ids=[0])
    return r.results[0]["out_0"]
```
